# Optimizing a Trainium2 kernel written in Bass

```python
import numpy as np
import jax
import jax.numpy as jnp

def _softmax(x, axis=-1):
    return jax.nn.softmax(x, axis=axis)

def _gelu(x):
    return jax.nn.gelu(x, approximate=True)

def _silu(x):
    return jax.nn.silu(x)

def _sigmoid(x):
    return jax.nn.sigmoid(x)

def _layernorm(x, axis=-1, eps=1e-05):
    m = jnp.mean(x, axis=axis, keepdims=True)
    v = jnp.var(x, axis=axis, keepdims=True)
    return (x - m) / jnp.sqrt(v + eps)

def _scatter_add(tgt, idx, src, axis=0):
    return tgt.at[idx].add(src)

def _segment_sum(src, seg, n):
    return jax.ops.segment_sum(src, seg, n)
kernel_name = 'mk_seq_postln_d1_jaxref_r8_310f0e'

def setup_inputs(seed: int=0):
    np.random.seed(seed)
    _w = jnp.asarray

    def _L0_attn_setup():
        import jax, jax.numpy as jnp
        import numpy as np
        EMBED_DIM = 128
        NUM_HEADS = 16
        HEAD_DIM = EMBED_DIM // NUM_HEADS
        BATCH = 2
        SEQ = 256
        BASE = 10000.0
        EPS = 1e-05

        def _lrpe(t, theta, offset=0):
            n = t.shape[-2]
            idx = (jnp.arange(n) + offset).reshape(1, -1, 1).astype(theta.dtype)
            ang = theta * idx
            return jnp.concatenate([t * jnp.cos(ang), t * jnp.sin(ang)], axis=-1)
        key = jax.random.key(seed)
        ks = jax.random.split(key, 8)
        d, h, hd = (EMBED_DIM, NUM_HEADS, HEAD_DIM)
        s = d ** (-0.5)
        x = jax.random.normal(ks[0], (BATCH, SEQ, d), dtype=jnp.float32)
        Wq = jax.random.normal(ks[1], (d, d), dtype=jnp.float32) * s
        Wk = jax.random.normal(ks[2], (d, d), dtype=jnp.float32) * s
        Wv = jax.random.normal(ks[3], (d, d), dtype=jnp.float32) * s
        Wo = jax.random.normal(ks[4], (d, d), dtype=jnp.float32) * s
        G1 = jax.random.normal(ks[5], (d, hd), dtype=jnp.float32) * s
        G2 = jax.random.normal(ks[6], (hd, d), dtype=jnp.float32) * hd ** (-0.5)
        gamma = jnp.ones((d,), jnp.float32)
        beta = jnp.zeros((d,), jnp.float32)
        theta = jnp.asarray((BASE ** (-2.0 / (h * hd) * np.arange(h * hd))).reshape(h, 1, hd), dtype=jnp.float32)
        return {'x': x, 'Wq': Wq, 'Wk': Wk, 'Wv': Wv, 'Wo': Wo, 'G1': G1, 'G2': G2, 'gamma': gamma, 'beta': beta, 'theta': theta}
    _L0_attn_in = _L0_attn_setup()

    def _L0_ffn_setup():
        import jax, jax.numpy as jnp
        import numpy as np
        B, S, H = (4, 256, 128)
        E, K = (8, 2)
        I_R, I_S = (4 * H, 8 * H)
        CAP_FACTOR = 1.25
        SCALE = 1.0
        key = jax.random.key(seed)
        ks = jax.random.split(key, 9)
        std = 0.02
        return {'x': jax.random.normal(ks[0], (B, S, H), jnp.float32), 'router_w': std * jax.random.normal(ks[1], (E, H), jnp.float32), 'rg': std * jax.random.normal(ks[2], (E, H, I_R), jnp.float32), 'ru': std * jax.random.normal(ks[3], (E, H, I_R), jnp.float32), 'rd': std * jax.random.normal(ks[4], (E, I_R, H), jnp.float32), 'sg': std * jax.random.normal(ks[5], (H, I_S), jnp.float32), 'su': std * jax.random.normal(ks[6], (H, I_S), jnp.float32), 'sd': std * jax.random.normal(ks[7], (I_S, H), jnp.float32)}
    _L0_ffn_in = _L0_ffn_setup()
    _d = {'L0_attn_x': _L0_attn_in['x'], 'L0_attn_Wq': _L0_attn_in['Wq'], 'L0_attn_Wk': _L0_attn_in['Wk'], 'L0_attn_Wv': _L0_attn_in['Wv'], 'L0_attn_Wo': _L0_attn_in['Wo'], 'L0_attn_G1': _L0_attn_in['G1'], 'L0_attn_G2': _L0_attn_in['G2'], 'L0_attn_gamma': _L0_attn_in['gamma'], 'L0_attn_beta': _L0_attn_in['beta'], 'L0_attn_theta': _L0_attn_in['theta'], 'L0_ffn_router_w': _L0_ffn_in['router_w'], 'L0_ffn_rg': _L0_ffn_in['rg'], 'L0_ffn_ru': _L0_ffn_in['ru'], 'L0_ffn_rd': _L0_ffn_in['rd'], 'L0_ffn_sg': _L0_ffn_in['sg'], 'L0_ffn_su': _L0_ffn_in['su'], 'L0_ffn_sd': _L0_ffn_in['sd']}
    _x0 = _d['L0_attn_x']
    _d['L0_attn_x'] = jax.random.normal(jax.random.fold_in(jax.random.key(seed), 1), (16, 512, 128), dtype=_x0.dtype)
    del _x0
    return _d

def reference(L0_attn_x, L0_attn_Wq, L0_attn_Wk, L0_attn_Wv, L0_attn_Wo, L0_attn_G1, L0_attn_G2, L0_attn_gamma, L0_attn_beta, L0_attn_theta, L0_ffn_router_w, L0_ffn_rg, L0_ffn_ru, L0_ffn_rd, L0_ffn_sg, L0_ffn_su, L0_ffn_sd):

    def _L0_attn_ref(x, Wq, Wk, Wv, Wo, G1, G2, gamma, beta, theta):
        import jax, jax.numpy as jnp
        import numpy as np
        EMBED_DIM = 128
        NUM_HEADS = 16
        HEAD_DIM = EMBED_DIM // NUM_HEADS
        BATCH = 2
        SEQ = 256
        BASE = 10000.0
        EPS = 1e-05

        def _lrpe(t, theta, offset=0):
            n = t.shape[-2]
            idx = (jnp.arange(n) + offset).reshape(1, -1, 1).astype(theta.dtype)
            ang = theta * idx
            return jnp.concatenate([t * jnp.cos(ang), t * jnp.sin(ang)], axis=-1)
        b, n, d = x.shape
        h, hd = (NUM_HEADS, HEAD_DIM)
        q = jax.nn.silu(x @ Wq)
        k = jax.nn.silu(x @ Wk)
        v = x @ Wv
        split = lambda t: t.reshape(b, n, h, hd).transpose(0, 2, 1, 3)
        q, k, v = (split(q), split(k), split(v))
        q = _lrpe(q, theta)
        k = _lrpe(k, theta)
        mask = jnp.tril(jnp.ones((n, n), dtype=x.dtype))
        energy = jnp.einsum('bhnd,bhmd->bhnm', q, k) * mask
        out = jnp.einsum('bhnm,bhmd->bhnd', energy, v)
        out = out.transpose(0, 2, 1, 3).reshape(b, n, d)
        out = out @ Wo
        gate = jax.nn.sigmoid(x @ G1 @ G2)
        out = out * gate
        mu = jnp.mean(out, axis=-1, keepdims=True)
        var = jnp.var(out, axis=-1, keepdims=True)
        out = (out - mu) / jnp.sqrt(var + EPS) * gamma + beta
        return out

    def _L0_ffn_ref(x, router_w, rg, ru, rd, sg, su, sd):
        import jax, jax.numpy as jnp
        import numpy as np
        B, S, H = (4, 256, 128)
        E, K = (8, 2)
        I_R, I_S = (4 * H, 8 * H)
        CAP_FACTOR = 1.25
        SCALE = 1.0
        b, s, h = x.shape
        T = b * s
        capacity = max(int(CAP_FACTOR * T / E), 1)
        xf = x.reshape(T, h)
        eps = jnp.finfo(x.dtype).eps
        xn = xf * jax.lax.rsqrt(jnp.mean(xf * xf, axis=-1, keepdims=True) + eps)
        logits = xn @ router_w.T
        probs = jax.nn.softmax(logits, axis=-1)
        topk_p, topk_i = jax.lax.top_k(probs, K)
        rw = topk_p / jnp.sum(topk_p, axis=-1, keepdims=True)
        one_hot = jax.nn.one_hot(topk_i, E, dtype=x.dtype)
        mask = one_hot.sum(1)
        wdense = (one_hot * rw[..., None]).sum(1)
        sel = mask.T.astype(bool)
        order = jnp.argsort(~sel, axis=1, stable=True)
        dispatch = order[:, :capacity]
        count = sel.sum(axis=1)
        valid = (jnp.arange(capacity)[None, :] < count[:, None]).astype(x.dtype)
        xg = xf[dispatch]
        gate = jax.nn.silu(jnp.einsum('ech,ehi->eci', xg, rg))
        up = jnp.einsum('ech,ehi->eci', xg, ru)
        eout = jnp.einsum('eci,eih->ech', gate * up, rd)
        w = jnp.take_along_axis(wdense.T, dispatch, axis=1)
        contrib = eout * (w * valid)[..., None]
        routed = jnp.zeros_like(xf).at[dispatch.reshape(-1)].add(contrib.reshape(-1, h))
        shared = jax.nn.silu(x @ sg) * (x @ su) @ sd
        return shared + SCALE * routed.reshape(b, s, h)
    x = L0_attn_x
    x = _layernorm(x + _L0_attn_ref(x, L0_attn_Wq, L0_attn_Wk, L0_attn_Wv, L0_attn_Wo, L0_attn_G1, L0_attn_G2, L0_attn_gamma, L0_attn_beta, L0_attn_theta), axis=-1)
    x = _layernorm(x + _L0_ffn_ref(x, L0_ffn_router_w, L0_ffn_rg, L0_ffn_ru, L0_ffn_rd, L0_ffn_sg, L0_ffn_su, L0_ffn_sd), axis=-1)
    return x

_drawn_inputs = setup_inputs


def setup_inputs(seed=0):
    import zlib

    import numpy as np

    out = dict(_drawn_inputs(seed))
    spreads = {'L0_attn_gamma': (1.0, 0.2), 'L0_attn_beta': (0.0, 0.1)}
    factors = {'L0_ffn_router_w': 8.0,
     'L0_ffn_rg': 8.0,
     'L0_ffn_ru': 8.0,
     'L0_ffn_rd': 8.0,
     'L0_ffn_sg': 3.431,
     'L0_ffn_su': 3.402,
     'L0_ffn_sd': 3.403}
    for name, (base, spread) in spreads.items():
        noise = np.random.default_rng([zlib.crc32(name.encode()), seed]).standard_normal(out[name].shape)
        drawn = base * np.exp(spread * noise) if base else spread * noise
        out[name] = jnp.asarray(drawn.astype(out[name].dtype))
    for name, factor in factors.items():
        out[name] = (out[name] * factor).astype(out[name].dtype)
    return out
```

```python
import concourse.bass as bass
from concourse import mybir
from contextlib import ExitStack

f32 = mybir.dt.float32
f32r = mybir.dt.float32r
bf16 = mybir.dt.bfloat16
i32 = mybir.dt.int32
u32 = mybir.dt.uint32
ALU = mybir.AluOpType
ACT = mybir.ActivationFunctionType
AX = mybir.AxisListType

P = 128
D = 128
B, S = 16, 512
NC = S // P
H, HD = 16, 8
E, FR, FS = 8, 512, 1024
CAP = int(1.25 * B * S / E)
SLOTS = E * CAP
CT = CAP // P
GROUPS = [(0, 4), (4, 4), (8, 2)]
EPS = 1e-5
EPS_RMS = 2.0 ** -23
FAR = 16384.0
TWO_PI = [6.28125, 0.0019350051879882812, 3.01991598e-07]
MAGIC = 12582912.0
PI_IN = 3.1415925
GP = {"KA": 0}


def build(nc, x, wqk, wvg, g1t, g2, wo, gamma, beta, theta, rwt, rg, ru, rd, sg, su, sd, out):
    x_v = x.rearrange("b (c p) d -> b p c d", p=P)
    out_v = out.rearrange("b (c p) d -> b p c d", p=P)
    ctx = ExitStack()
    with ctx:
        def sb(name, shape, dt=f32):
            return ctx.enter_context(nc.sbuf_tensor(name, shape, dt))

        def sem(name):
            return ctx.enter_context(nc.semaphore(name))

        xg_d = nc.dram_tensor("dispatched_rows", [SLOTS, D], f32, kind="Internal").ap()
        yd_d = nc.dram_tensor("expert_rows", [SLOTS + P, D], f32, kind="Internal").ap()
        x1_d = nc.dram_tensor("x1_rows", [B, P, NC * D], f32, kind="Internal").ap()
        slot_d = nc.dram_tensor("slots", [B, P, 2 * NC], i32, kind="Internal").ap()
        weight_d = nc.dram_tensor("weights", [B, P, 2 * NC], f32, kind="Internal").ap()

        ident = sb("ident", [P, P])
        causal = sb("causal", [P, P])
        before = sb("before", [P, P], bf16)
        before_f = sb("before_f", [P, P])
        ones = sb("ones", [P, P], bf16)
        headmask = sb("headmask", [P, 2, 64])
        bits = sb("bits", [P, 3, 8])
        pairmask = sb("pairmask", [P, 3])
        iota8 = sb("iota8", [P, 2 * NC, 8])
        eoff = sb("eoff", [P, NC, 8])
        minus_half = sb("minus_half", [P, 8])
        gam = sb("gam", [P, D])
        bet = sb("bet", [P, D])
        zeros = sb("zeros", [P, CT * D])
        pos_n = sb("pos_n", [P, S])
        theta_s = sb("theta_s", [P, 2])
        phase = sb("phase", [P, 2])
        table = sb("table", [P, 2, S])
        rwt_s = sb("rwt_s", [P, E])
        wo_s = sb("wo_s", [P, D])
        g1t_s = sb("g1t_s", [8, D])
        g2_s = sb("g2_s", [8, D])
        wqk_hi = sb("wqk_hi", [P, 512], f32r)
        wqk_lo = sb("wqk_lo", [P, 512], f32r)
        wvg_hi = sb("wvg_hi", [P, 256], f32r)
        wvg_lo = sb("wvg_lo", [P, 256], f32r)
        warm = sb("warm", [P, 1])

        xin = sb("xin", [P, 2, NC, D])
        xb = sb("xb", [P, 2, NC, D])
        xhi = sb("xhi", [P, 2, S], f32r)
        xlo = sb("xlo", [P, 2, S], f32r)
        sq = sb("sq", [P, 2, S])
        QT = sb("QT", [P, 2, 2, S])
        KT = sb("KT", [P, 2, 2, S])
        QM = sb("QM", [P, 2, 2, 2, S])
        Kt = sb("Kt", [P, 2, 3, 256])
        VP = sb("VP", [P, 2, NC, 512])
        EM = sb("EM", [P, 2, 4, 512])
        SM = sb("SM", [P, 2, 128])
        oT = sb("oT", [P, 2, S])
        th = sb("th", [P, 2, S])
        y2 = sb("y2", [P, NC, D])
        wv = sb("wv", [P, NC, D])
        s1 = sb("s1", [P, NC, D])
        x1 = sb("x1", [P, 2, NC, D])
        x1T = sb("x1T", [P, S])
        st = sb("st", [P, NC, 6])
        mv = sb("mv", [P, NC, 2])
        mv2 = sb("mv2", [P, NC, 2])
        ve = sb("ve", [P, NC])
        rs = sb("rs", [P, NC])
        vq = sb("vq", [P, 2, NC])
        rr = sb("rr", [P, 2, 2, NC])
        lg = sb("lg", [P, NC, 8])
        m8 = sb("m8", [P, NC, 8])
        ix8 = sb("ix8", [P, NC, 8], u32)
        ixf = sb("ixf", [P, 2, NC])
        oh = sb("oh", [P, 2 * NC, 8])
        mb = sb("mb", [P, NC, 8], bf16)
        seen = sb("seen", [P, 8], bf16)
        seen_f = sb("seen_f", [P, 8])
        over = sb("over", [P, NC, 8])
        slotv = sb("slotv", [P, NC, 8])
        pick = sb("pick", [P, 2 * NC, 8])
        slotf = sb("slotf", [P, 2 * NC])
        gap = sb("gap", [P, NC])
        gapr = sb("gapr", [P, NC])
        tw = sb("tw", [P, NC])
        slot = sb("slot", [P, 2, 2 * NC], i32)
        wts = sb("wts", [P, 2, 2 * NC])

        xgT_hi = sb("xgT_hi", [P, 2, CAP], f32r)
        xgT_lo = sb("xgT_lo", [P, 2, CAP], f32r)
        we_hi = sb("we_hi", [P, 2, 2, FR], f32r)
        we_lo = sb("we_lo", [P, 2, 2, FR], f32r)
        ws_hi = sb("ws_hi", [P, 2, FS], f32r)
        ws_lo = sb("ws_lo", [P, 2, FS], f32r)
        sd_s = sb("sd_s", [P, FS // P, D])
        flat = lambda t: t[:].rearrange({4: "p a b c -> p (a b c)", 3: "p a b -> p (a b)", 5: "p a b c d -> p (a b c d)"}[len(t.shape)])
        xg = flat(QM)[:, 0:2 * CT * D].rearrange("p (e j d) -> p e j d", e=2, j=CT)
        ye = flat(VP)[:, 0:2 * CT * D].rearrange("p (e j d) -> p e j d", e=2, j=CT)
        wraw = flat(QT).rearrange("p (e g n) -> p e g n", e=2, g=2)
        wd = flat(KT)[:, 0:2 * FR].rearrange("p (e f d) -> p e f d", e=2, f=FR // P)
        sraw = [flat(Kt)[:, 0:FS], flat(KT)[:, 2 * FR:2 * FR + FS]]
        he = EM
        hs = [flat(QM).rearrange("p (f n) -> p f n", n=S), flat(VP).rearrange("p (f n) -> p f n", n=S)]
        ge = flat(QT).rearrange("p (m k c d) -> p m k c d", m=2, k=2, c=NC)
        slot3 = sb("slot3", [P, 2, 2 * NC], i32)
        wts3 = sb("wts3", [P, 2, 2 * NC])

        banks = [ctx.enter_context(nc.psum_tensor(f"bank{i}", [P, 512], f32)) for i in range(8)]
        EB, PB, OB, SBK = banks[0:4], banks[4:6], banks[6], banks[7]

        ld_w = sem("weights_loaded"); ld_x = sem("x_loaded"); c_pool = sem("pool_constants")
        c_dve = sem("dve_constants"); c_sin = sem("table_ready"); c_g = sem("g1g2_product"); c_warm = sem("act_table_warm")
        pe_xT = sem("x_transposed")
        pe_qk = sem("qk_projected")
        pe_vg = sem("vg_projected")
        pe_kt = sem("k_by_token")
        pe_E = sem("energies")
        pe_S = sem("state_summed")
        pe_av = sem("attention_out")
        pe_wo = sem("wo_projected")
        pe_x1T = sem("x1_transposed")
        pe_lg = sem("logits")
        pe_pos = sem("positions")
        a_xhi = sem("xhi_ready"); a_silu = sem("silu_ready"); a_v = sem("v_ready"); a_th = sem("gate_ready")
        a_kt = sem("kt_ready"); a_out = sem("out_copied"); a_x1T = sem("x1T_ready"); a_tw = sem("route_tanh")
        v_xlo = sem("xlo_ready"); v_qk = sem("qk_turned"); v_mask = sem("energies_masked"); v_S = sem("state_masked")
        v_y = sem("gated"); v_bn = sem("stats"); v_ag = sem("moments"); v_ve = sem("variance_eps"); v_ln = sem("ln_steps")
        v_x1 = sem("x1_ready"); v_lg = sem("logits_copied"); v_rt = sem("route_steps"); v_M = sem("choices_ready")
        v_gap = sem("gap_ready"); v_slot = sem("slots_ready"); v_wts = sem("weights_ready"); v_woke = sem("vector_woke")
        v_M2 = sem("mean_square_steps"); v_P = sem("slot_steps")
        g_qm = sem("q_by_pair"); g_xb = sem("x_beta"); g_r1 = sem("rstd1"); g_r2 = sem("rstd2"); g_woke = sem("gpsimd_woke")
        g_sc = sem("rows_dispatched")
        sp_x1 = sem("x1_stored"); sp_rt = sem("route_stored"); x1_free = sem("x1_kept"); rt_free = sem("route_kept"); sp_woke = sem("sync_woke")
        e_ld = sem("expert_weights_loaded"); e_ldx = sem("expert_rows_loaded"); e_xT = sem("e_transposed"); e_gu = sem("e_gate_up"); e_dn = sem("e_down")
        e_hi = sem("e_xhi"); e_lo = sem("e_xlo"); e_silu = sem("e_silu"); e_h = sem("e_hidden"); e_y = sem("e_copied")
        e_w = sem("e_weights_split"); e_yst = sem("e_stored"); ye_free = sem("e_rows_kept"); s_ld = sem("shared_loaded"); s_w = sem("shared_split")
        m_ld = sem("m_loaded"); m_xT = sem("m_transposed"); m_hi = sem("m_xhi"); m_lo = sem("m_xlo"); m_gu = sem("m_gate_up")
        m_silu = sem("m_silu"); m_h = sem("m_hidden"); m_dn = sem("m_down"); m_g = sem("m_gathered"); m_z = sem("m_sums")
        m_bn = sem("m_stats"); m_ag = sem("m_moments"); m_ve = sem("m_variance_eps"); m_r = sem("m_rstd"); m_o = sem("m_normed")
        m_st = sem("m_stored"); m_woke_v = sem("m_vector_woke"); m_woke_g = sem("m_gpsimd_woke")

        def need(eng, s, value):
            if not isinstance(value, int) or value > 0:
                eng.wait_ge(s, value)

        def hold(eng, s, value, woke):
            if not isinstance(value, int) or value > 0:
                eng.wait_ge(s, value)
                eng.sem_inc(woke, 1)

        def last(n):
            return min(n, B - 1) if isinstance(n, int) else n

        def within(b, lo, hi):
            return not isinstance(b, int) or lo <= b <= hi

        def stage1(eng, step):
            for b in (-1, 0, 1):
                step(b, b % 2)
            with eng.Fori(1, 7) as i:
                for par in (0, 1):
                    step(i * 2 + par, par)
            for b in (14, 15, 16, 17):
                step(b, b % 2)

        def stage2(eng, step):
            step(0, 0)
            with eng.Fori(0, 3) as i:
                for k in (1, 2):
                    step(i * 2 + k, k % 2)
            step(E - 1, 1)

        def stage3(eng, step):
            for m in (0, 1, 2):
                step(m, m % 2)
            with eng.Fori(0, 6) as i:
                for k in (3, 4):
                    step(i * 2 + k, k % 2)
            step(B - 1, 1)
            step(B, 0)

        block = ctx.enter_context(nc.Block())

        @block.sync
        def _(sp):
            sp.dma_start(xin[:, 0], x_v[0]).then_inc(ld_x, 16)
            for dst, src in [(sq[:, 0], wqk), (sq[:, 1, 0:D], wvg), (g1t_s[:], g1t), (g2_s[:], g2), (wo_s[:], wo),
                             (theta_s[:], theta), (rwt_s[:], rwt),
                             (gam[:], gamma.rearrange("(o d) -> o d", o=1).broadcast_to([P, D])),
                             (bet[:], beta.rearrange("(o d) -> o d", o=1).broadcast_to([P, D]))]:
                sp.dma_start(dst, src).then_inc(ld_w, 16)
            sp.wait_ge(ld_x, 16)
            sp.dma_start(xin[:, 1], x_v[1]).then_inc(ld_x, 16)
            sp.dma_start(sd_s[:], sd.rearrange("(f p) d -> p f d", p=P)).then_inc(s_ld, 16)
            sp.wait_ge(c_pool, 1)
            sp.dma_start(yd_d[SLOTS:SLOTS + P], zeros[:, 0:D]).then_inc(s_ld, 16)
            sp.sem_inc(x1_free, 2)
            sp.sem_inc(rt_free, 2)
            sp.sem_inc(ye_free, 2)

            def step(b, par):
                if within(b, 0, 13):
                    hold(sp, ld_x, 16 * (b + 2), sp_woke)
                    hold(sp, pe_xT, b + 1, sp_woke)
                    hold(sp, g_xb, b + 1, sp_woke)
                    sp.dma_start(xin[:, par], x_v[b + 2]).then_inc(ld_x, 16)
                if within(b, 1, B):
                    hold(sp, v_x1, 4 * b, sp_woke)
                    sp.dma_start(x1_d[b - 1], x1[:, 1 - par].rearrange("p c d -> p (c d)")).then_inc(sp_x1, 16)
                    hold(sp, sp_x1, 16 * b, sp_woke)
                    sp.sem_inc(x1_free, 1)
                if within(b, 2, B + 1):
                    hold(sp, v_slot, b - 1, sp_woke)
                    hold(sp, v_wts, b - 1, sp_woke)
                    sp.dma_start(slot_d[b - 2], slot[:, par]).then_inc(sp_rt, 16)
                    sp.dma_start(weight_d[b - 2], wts[:, par]).then_inc(sp_rt, 16)
                    hold(sp, sp_rt, 32 * (b - 1), sp_woke)
                    sp.sem_inc(rt_free, 1)
            stage1(sp, step)

            sp.wait_ge(pe_av, 4 * B)
            for i, src in enumerate((sg, su)):
                sp.dma_start(sraw[i], src).then_inc(s_ld, 16)

            def load_weights(e, par):
                sp.dma_start(wraw[:, par, 0], rg[e]).then_inc(e_ld, 16)
                sp.dma_start(wraw[:, par, 1], ru[e]).then_inc(e_ld, 16)
                sp.dma_start(wd[:, par], rd[e].rearrange("(f p) d -> p f d", p=P)).then_inc(e_ld, 16)

            def load_rows(e, par):
                sp.dma_start(xg[:, par], xg_r[e]).then_inc(e_ldx, 16)

            xg_r = xg_d.rearrange("(e p j) d -> e p j d", e=E, p=P)
            yd_r = yd_d[0:SLOTS].rearrange("(e p j) d -> e p j d", e=E, p=P)
            load_weights(0, 0)
            sp.wait_ge(g_sc, P * (B + 1))
            load_rows(0, 0)

            def step(e, par):
                if within(e, 0, E - 2):
                    hold(sp, e_ld, 48 * (e + 1), sp_woke)
                    hold(sp, e_ldx, 16 * (e + 1), sp_woke)
                    hold(sp, e_w, 4 * e, sp_woke)
                    hold(sp, e_dn, 3 * e, sp_woke)
                    load_weights(e + 1, 1 - par)
                    hold(sp, e_xT, 3 * e, sp_woke)
                    load_rows(e + 1, 1 - par)
                hold(sp, e_y, 3 * (e + 1), sp_woke)
                sp.dma_start(yd_r[e], ye[:, par]).then_inc(e_yst, 16)
                hold(sp, e_yst, 16 * (e + 1), sp_woke)
                sp.sem_inc(ye_free, 1)
            stage2(sp, step)

            def load_batch(m, par):
                sp.dma_start(xin[:, par].rearrange("p c d -> p (c d)"), x1_d[m]).then_inc(m_ld, 16)
                sp.dma_start(slot3[:, par], slot_d[m]).then_inc(m_ld, 16)
                sp.dma_start(wts3[:, par], weight_d[m]).then_inc(m_ld, 16)
            load_batch(0, 0)

            def step(m, par):
                if within(m, 0, B - 2):
                    hold(sp, m_ld, 48 * (m + 1), sp_woke)
                    hold(sp, m_z, 9 * m - 1, sp_woke)
                    hold(sp, m_xT, m, sp_woke)
                    hold(sp, m_g, P * m, sp_woke)
                    load_batch(m + 1, 1 - par)
                if within(m, 1, B):
                    hold(sp, m_o, 4 * m, sp_woke)
                    hold(sp, m_st, 16 * (m - 1), sp_woke)
                    sp.dma_start(out_v[m - 1], x1[:, 1 - par]).then_inc(m_st, 16)
            stage3(sp, step)
            sp.wait_ge(m_st, 16 * B)

        @block.gpsimd
        def _(gp):
            g = nc.gpsimd
            g.memset(zeros[:], 0.0).then_inc(c_pool, 1)
            g.memset(ident[:], 0.0).then_inc(c_pool, 1)
            g.memset(causal[:], 1.0).then_inc(c_pool, 1)
            g.memset(before_f[:], 1.0).then_inc(c_pool, 1)
            g.memset(ones[:], 1.0).then_inc(c_pool, 1)
            g.memset(headmask[:], 1.0).then_inc(c_pool, 1)
            g.memset(bits[:], 1.0).then_inc(c_pool, 1)
            g.memset(minus_half[:], -0.5).then_inc(c_pool, 1)
            g.memset(seen[:], 0.0).then_inc(c_pool, 1)
            g.iota(iota8[:], [[0, 2 * NC], [1, 8]], base=0, channel_multiplier=0,
                   allow_small_or_imprecise_dtypes=True).then_inc(c_pool, 1)
            g.iota(eoff[:], [[0, NC], [CAP, 8]], base=0, channel_multiplier=0,
                   allow_small_or_imprecise_dtypes=True).then_inc(c_pool, 1)
            g.iota(pos_n[:], [[1, S]], base=0, channel_multiplier=0,
                   allow_small_or_imprecise_dtypes=True).then_inc(c_pool, 1)
            gp.wait_ge(c_pool, 12)
            g.affine_select(out=ident[:], in_=ident[:], compare_op=ALU.not_equal, fill=1.0, base=0,
                            pattern=[[-1, P]], channel_multiplier=1).then_inc(c_pool, 1)
            g.affine_select(out=causal[:], in_=causal[:], compare_op=ALU.is_ge, fill=0.0, base=0,
                            pattern=[[1, P]], channel_multiplier=-1).then_inc(c_pool, 1)
            g.affine_select(out=before_f[:], in_=before_f[:], compare_op=ALU.is_gt, fill=0.0, base=0,
                            pattern=[[1, P]], channel_multiplier=-1).then_inc(c_pool, 1)
            hm = headmask[:].rearrange("p t (h j) -> p t h j", h=8)
            g.affine_select(out=hm, in_=hm, compare_op=ALU.is_ge, fill=0.0, base=0,
                            pattern=[[0, 2], [-16, 8], [0, 8]], channel_multiplier=1).then_inc(c_pool, 1)
            for v in (0, 1):
                g.affine_select(out=bits[:, v, 0:4], in_=bits[:, v, 0:4], compare_op=ALU.is_ge, fill=0.0, base=-16 * v,
                                pattern=[[-32, 4]], channel_multiplier=1).then_inc(c_pool, 1)
            g.affine_select(out=bits[:, 2], in_=bits[:, 2], compare_op=ALU.is_ge, fill=0.0, base=0,
                            pattern=[[-16, 8]], channel_multiplier=1).then_inc(c_pool, 1)
            gp.wait_ge(c_pool, 19)
            g.affine_select(out=hm, in_=hm, compare_op=ALU.is_ge, fill=0.0, base=15,
                            pattern=[[0, 2], [16, 8], [0, 8]], channel_multiplier=-1).then_inc(c_pool, 1)
            for v in (0, 1):
                g.affine_select(out=bits[:, v, 0:4], in_=bits[:, v, 0:4], compare_op=ALU.is_ge, fill=0.0, base=15 + 16 * v,
                                pattern=[[32, 4]], channel_multiplier=-1).then_inc(c_pool, 1)
            g.affine_select(out=bits[:, 2], in_=bits[:, 2], compare_op=ALU.is_ge, fill=0.0, base=7,
                            pattern=[[16, 8]], channel_multiplier=-1).then_inc(c_pool, 1)
            g.memset(VP[:, 0], 0.0).then_inc(c_pool, 1)
            g.memset(VP[:, 1], 0.0).then_inc(c_pool, 1)
            xg_r = xg_d.rearrange("(e p j) d -> e p (j d)", e=E, p=P)
            for e in range(E):
                gp.dma_start(xg_r[e], zeros[:]).then_inc(g_sc, 16)
            gp.wait_ge(c_dve, 2)
            gp.wait_ge(c_pool, 25)
            gp.wait_ge(ld_w, 9 * 16)

            def step(b, par):
                f = b + 1
                if within(b, 1, B):
                    need(gp, v_ve, 2 * b - 1)
                    g.tensor_tensor(rs[:], ve[:], minus_half[:, 0:NC], ALU.pow).then_inc(g_r1, 1)

                def by_pair(t):
                    hold(gp, v_qk, 4 * f + t + 1, g_woke)
                    hold(gp, pe_E, 16 * (f - 1), g_woke)
                    for v in (0, 1):
                        g.tensor_scalar(QM[:, 1 - par, t, v], QT[:, 1 - par, t], pairmask[:, v:v + 1], None,
                                        ALU.mult).then_inc(g_qm, 1)
                if within(b, -1, 14):
                    by_pair(0)
                    by_pair(1)
                if within(b, 1, B):
                    need(gp, v_ve, 2 * b)
                    g.tensor_tensor(rr[:, 1 - par], vq[:], minus_half[:].rearrange("p (a c) -> p a c", a=2),
                                    ALU.pow).then_inc(g_r2, 1)
                if within(b, -1, 14):
                    need(gp, ld_x, 16 * (f + 1))
                    need(gp, v_ln, 8 * (f - 1))
                    g.tensor_tensor(xb[:, 1 - par], xin[:, 1 - par], bet[:].unsqueeze(1).broadcast_to([P, NC, D]),
                                    ALU.add).then_inc(g_xb, 1)
                if within(b, 2, B + 1):
                    hold(gp, g_sc, P * (b - 1), g_woke)
                    hold(gp, v_slot, b - 1, g_woke)
                    for j in range(2 * NC):
                        g.indirect_dma_start(out=xg_d, out_offset=bass.IndirectOffsetOnAxis(ap=slot[:, par, j:j + 1], axis=0),
                                             in_=x1[:, par, j % NC, :], in_offset=None, bounds_check=SLOTS - 1,
                                             oob_is_err=False).then_inc(g_sc, 16)
            stage1(gp, step)

            def split_shared(i):
                gp.wait_ge(s_ld, 64)
                g.tensor_copy(ws_hi[:, i], sraw[i]).then_inc(s_w, 1)
                gp.wait_ge(s_w, 2 * i + 1)
                g.tensor_tensor(ws_lo[:, i], sraw[i], ws_hi[:, i].bitcast(f32), ALU.subtract).then_inc(s_w, 1)

            def step(e, par):
                for i in (0, 1):
                    hold(gp, e_ld, 48 * (e + 1), m_woke_g)
                    g.tensor_copy(we_hi[:, par, i], wraw[:, par, i]).then_inc(e_w, 1)
                    need(gp, e_w, 4 * e + 2 * i + 1)
                    g.tensor_tensor(we_lo[:, par, i], wraw[:, par, i], we_hi[:, par, i].bitcast(f32),
                                    ALU.subtract).then_inc(e_w, 1)
            stage2(gp, step)
            split_shared(0)
            split_shared(1)

            gp.wait_ge(e_yst, 16 * E)

            def step(m, par):
                if within(m, 0, B - 1):
                    hold(gp, m_ld, 48 * (m + 1), m_woke_g)
                    hold(gp, m_z, 9 * (m - 1), m_woke_g)
                    hold(gp, m_g, P * m, m_woke_g)
                    for j in range(2 * NC):
                        g.indirect_dma_start(out=ge[:, par, j // NC, j % NC, :], out_offset=None, in_=yd_d[0:SLOTS + 1],
                                             in_offset=bass.IndirectOffsetOnAxis(ap=slot3[:, par, j:j + 1], axis=0)
                                             ).then_inc(m_g, 16)
                if within(m, 1, B):
                    need(gp, m_ve, m)
                    g.tensor_tensor(rs[:], ve[:], minus_half[:, 0:NC], ALU.pow).then_inc(m_r, 1)
            stage3(gp, step)

        @block.scalar
        def _(act):
            a = nc.scalar
            act.wait_ge(c_pool, 1)
            a.activation(warm[:], zeros[:, 0:1], ACT.Silu).then_inc(c_warm, 1)
            act.wait_ge(c_dve, 15)
            a.activation(table[:], table[:], ACT.Sin).then_inc(c_sin, 1)
            act.wait_ge(c_pool, 25)

            def silu(f, par, i):
                need(act, pe_qk, 4 * f + i + 1)
                need(act, v_qk, 4 * f + i - 1)
                a.activation(sq[:, i % 2], PB[(1, 1, 0, 1)[i]][:], ACT.Silu).then_inc(a_silu, 1)

            def copy_out(b, c, par):
                need(act, pe_av, 4 * b + c + 1)
                need(act, pe_wo, b - 1)
                a.activation(oT[:, par, P * c:P * (c + 1)], OB[:, P * c:P * (c + 1)], ACT.Copy).then_inc(a_out, 1)

            def values(f, par, i):
                need(act, pe_vg, 2 * f + i + 1)
                need(act, pe_av, 4 * (f - 1))
                for c in (0, 1):
                    src = PB[i][:, 256 * c:256 * c + D].rearrange("p (j i d) -> p j i d", j=4, i=4)
                    a.activation(vp_view(par, 2 * i + c), src, ACT.Copy).then_inc(a_v, 1)
                need(act, v_y, f - 1)
                src = PB[i][:].rearrange("p (c n) -> p c n", c=2)[:, :, D:2 * D]
                dst = th[:, par].rearrange("p (c n) -> p c n", c=NC)[:, 2 * i:2 * i + 2]
                a.activation(dst, src, ACT.Tanh, scale=0.5).then_inc(a_th, 1)

            def step(b, par):
                f, fp = b + 1, 1 - par
                front = within(b, -1, 14)
                if within(b, 1, B):
                    copy_out(b - 1, 3, 1 - par)
                if front:
                    need(act, pe_xT, f + 1)
                    need(act, pe_vg, 2 * f)
                    a.activation(xhi[:, 0], PB[0][:], ACT.Copy).then_inc(a_xhi, 1)
                    silu(f, fp, 0)
                if within(b, 0, B - 1):
                    copy_out(b, 0, par)
                if within(b, 2, B + 1):
                    need(act, v_gap, b - 1)
                    a.activation(tw[:], gapr[:], ACT.Tanh, scale=0.5).then_inc(a_tw, 1)
                if front:
                    silu(f, fp, 1)
                    silu(f, fp, 2)
                if within(b, 0, B - 1):
                    copy_out(b, 1, par)
                if front:
                    silu(f, fp, 3)
                    values(f, fp, 0)
                    values(f, fp, 1)
                if within(b, 0, B - 1):
                    copy_out(b, 2, par)
                if front:
                    for i, n in ((0, 2), (1, 1)):
                        need(act, pe_kt, 2 * f + i + 1)
                        need(act, pe_S, 3 * (f - 1))
                        a.activation(Kt[:, fp, 2 * i:2 * i + n], PB[i][:, 0:256 * n].rearrange("p (c n) -> p c n", c=n),
                                     ACT.Copy).then_inc(a_kt, 1)
                if within(b, 1, B):
                    need(act, pe_x1T, b)
                    need(act, pe_lg, b - 1)
                    a.activation(x1T[:], PB[0][:], ACT.Copy).then_inc(a_x1T, 1)

            def vp_view(par, c):
                v = VP[:, par, c]
                return bass.AP(tensor=v.tensor, offset=v.offset, ap=[list(v.ap[0]), [128, 4], [40, 4], [1, 8]])
            stage1(act, step)

            def step(e, par):
                def split(k, kp):
                    for i, (t0, n) in enumerate(GROUPS):
                        need(act, e_xT, 3 * k + i + 1)
                        if i == 0:
                            need(act, e_gu, 12 * (k - 1))
                        a.activation(xgT_hi[:, kp, P * t0:P * (t0 + n)], PB[(3 * kp + i) % 2][:, 0:P * n],
                                     ACT.Copy).then_inc(e_hi, 1)

                def group(n):
                    for f in range(4):
                        k = 12 * e + 4 * n + f
                        need(act, e_gu, k + 1)
                        need(act, e_h, k - 1)
                        w = P * GROUPS[n][1]
                        a.activation(sq[:, f % 2, 0:w], EB[f % 2][:, 0:w], ACT.Silu).then_inc(e_silu, 1)

                def rows(n):
                    t0, cnt = GROUPS[n]
                    need(act, e_dn, 3 * e + n + 1)
                    if n == 0:
                        need(act, ye_free, e + 1)
                    a.activation(ye[:, par, t0:t0 + cnt], (OB, SBK)[(n + par) % 2][:, 0:P * cnt].rearrange("p (t d) -> p t d", t=cnt),
                                 ACT.Copy).then_inc(e_y, 1)
                if isinstance(e, int) and e == 0:
                    split(0, 0)
                group(0)
                if within(e, 0, E - 2):
                    split(e + 1, 1 - par)
                group(1)
                rows(0)
                group(2)
                rows(1)
                rows(2)
            stage2(act, step)

            def step(m, par):
                def split(k, kp):
                    need(act, m_xT, k + 1)
                    need(act, m_gu, 8 * (k - 1))
                    a.activation(xhi[:, kp], PB[kp][:], ACT.Copy).then_inc(m_hi, 1)
                if isinstance(m, int) and m == 0:
                    split(0, 0)
                if within(m, 0, B - 1):
                    for f in range(8):
                        need(act, m_gu, 8 * m + f + 1)
                        need(act, m_h, 8 * m + f - 1)
                        a.activation(sq[:, f % 2], EB[f % 2][:], ACT.Silu).then_inc(m_silu, 1)
                        if f == 5 and within(m, 0, B - 2):
                            split(m + 1, 1 - par)
            stage3(act, step)

        @block.vector
        def _(dve):
            v = nc.vector
            n_c = [0]
            turns = QM[:, 0, 0]

            def link(ins):
                n_c[0] += 1
                ins.then_inc(c_dve, 1)
                dve.wait_ge(c_dve, n_c[0])
            dve.wait_ge(c_pool, 23)
            link(v.tensor_reduce(pairmask[:, 0:2], bits[:, 0:2, 0:4], AX.X, ALU.add))
            link(v.tensor_reduce(pairmask[:, 2:3], bits[:, 2:3], AX.X, ALU.add))
            link(v.tensor_copy(before[:], before_f[:]))
            link(v.tensor_scalar(phase[:, 0:1], pairmask[:, 2:3], 0.25, None, ALU.mult))
            link(v.tensor_scalar(phase[:, 1:2], pairmask[:, 2:3], 1.5707963267948966, None, ALU.mult))
            dve.wait_ge(ld_w, 9 * 16)
            link(v.tensor_scalar(table[:, 0], pos_n[:], theta_s[:, 0:1], None, ALU.mult))
            link(v.tensor_scalar(table[:, 1], pos_n[:], theta_s[:, 1:2], None, ALU.mult))
            link(v.tensor_scalar(turns, table[:], 0.15915494309189535, phase[:, 0:1], ALU.mult, ALU.add))
            link(v.tensor_scalar(turns, turns, MAGIC, None, ALU.add))
            link(v.tensor_scalar(turns, turns, MAGIC, None, ALU.subtract))
            for part in TWO_PI:
                link(v.scalar_tensor_tensor(table[:], turns, -part, table[:], ALU.mult, ALU.add))
            link(v.tensor_scalar(table[:], table[:], phase[:, 1:2], PI_IN, ALU.add, ALU.min))
            link(v.tensor_scalar(table[:], table[:], -PI_IN, None, ALU.max))
            link(v.tensor_copy(wqk_hi[:], sq[:, 0]))
            link(v.tensor_tensor(wqk_lo[:], sq[:, 0], wqk_hi[:].bitcast(f32), ALU.subtract))
            dve.wait_ge(c_g, 1)
            link(v.tensor_copy(sq[:, 1, D:2 * D], PB[0][:, 0:D]))
            link(v.tensor_copy(wvg_hi[:], sq[:, 1, 0:2 * D]))
            link(v.tensor_tensor(wvg_lo[:], sq[:, 1, 0:2 * D], wvg_hi[:].bitcast(f32), ALU.subtract))

            def turn(f, fp, i):
                dst = (QT, KT)[i // 2][:, fp, i % 2]
                need(dve, a_silu, 4 * f + i + 1)
                if i == 0 and isinstance(f, int) and f == 0:
                    dve.wait_ge(c_sin, 1)
                need(dve, pe_av, 4 * (f - 1))
                if i < 2:
                    need(dve, g_qm, 4 * (f - 2) + 2 * (i + 1))
                v.tensor_tensor(dst, sq[:, i % 2], table[:, i % 2], ALU.mult).then_inc(v_qk, 1)

            def mask(b, par, c):
                for q in range(4):
                    need(dve, pe_E, 16 * b + 4 * c + q + 1)
                    need(dve, pe_av, 4 * b + c - 1)
                    v.tensor_tensor(EM[:, c % 2, q].rearrange("p (h n) -> p h n", h=4),
                                    EB[q][:].rearrange("p (h n) -> p h n", h=4),
                                    causal[:].unsqueeze(1).broadcast_to([P, 4, P]), ALU.mult).then_inc(v_mask, 1)
                if c < 3:
                    need(dve, pe_S, 3 * b + c + 1)
                    need(dve, pe_av, 4 * b + c)
                    v.tensor_tensor(SM[:, c % 2], SBK[:, 0:128], headmask[:].rearrange("p t n -> p (t n)"),
                                    ALU.mult).then_inc(v_S, 1)

            def moments(src, dst, n, s_bn, s_ag, woke):
                for c in range(NC):
                    v.bn_stats(st[:, c], src[:, c]).then_inc(s_bn, 1)
                hold(dve, s_bn, 4 * n + 4, woke)
                for c in range(NC):
                    v.bn_aggr(dst[:, c], st[:, c]).then_inc(s_ag, 1)
                need(dve, s_ag, 4 * n + 4)

            def step(b, par):
                f, fp = b + 1, 1 - par
                front, core = within(b, -1, 14), within(b, 0, B - 1)
                back, route = within(b, 1, B), within(b, 2, B + 1)
                R = 9 * (b - 2)
                if core:
                    mask(b, par, 0)
                if front:
                    need(dve, a_xhi, f + 1)
                    need(dve, pe_vg, 2 * f)
                    v.tensor_tensor(xlo[:, 0], PB[0][:], xhi[:, 0].bitcast(f32), ALU.subtract).then_inc(v_xlo, 1)
                if route:
                    hold(dve, v_lg, b - 1, v_woke)
                    for c in range(NC):
                        v.max(m8[:, c], lg[:, c]).then_inc(v_rt, 1)
                    hold(dve, v_rt, R + 4, v_woke)
                    for c in range(NC):
                        v.max_index(ix8[:, c], m8[:, c], lg[:, c]).then_inc(v_rt, 1)
                    v.tensor_tensor(gap[:], m8[:, :, 0], m8[:, :, 1], ALU.subtract).then_inc(v_rt, 1)
                    need(dve, v_rt, R + 9)
                    v.tensor_tensor(gapr[:], gap[:], rr[:, par, 1], ALU.mult).then_inc(v_gap, 1)
                    v.tensor_copy(ixf[:].rearrange("p k c -> p c k"), ix8[:, :, 0:2]).then_inc(v_M, 1)
                    need(dve, v_M, 6 * (b - 2) + 1)
                    v.tensor_tensor(oh[:], iota8[:], ixf[:].rearrange("p k c -> p (k c)").unsqueeze(2).broadcast_to([P, 2 * NC, 8]),
                                    ALU.is_equal).then_inc(v_M, 1)
                    need(dve, v_M, 6 * (b - 2) + 2)
                    v.tensor_tensor(mb[:], oh[:, 0:NC], oh[:, NC:2 * NC], ALU.add).then_inc(v_M, 1)
                if core:
                    mask(b, par, 1)
                if front:
                    turn(f, fp, 0)
                if back:
                    need(dve, pe_wo, b)
                    need(dve, a_th, 2 * b)
                    v.scalar_tensor_tensor(y2[:].rearrange("p c d -> p (c d)"), th[:, 1 - par], 1.0, PB[0][:], ALU.add,
                                           ALU.mult).then_inc(v_y, 1)
                    need(dve, v_y, b)
                    moments(y2, mv, 2 * (b - 1), v_bn, v_ag, v_woke)
                    v.tensor_scalar(ve[:], mv[:, :, 1], 4 * EPS, None, ALU.add).then_inc(v_ve, 1)
                if core:
                    mask(b, par, 2)
                if front:
                    turn(f, fp, 1)
                    turn(f, fp, 2)
                    turn(f, fp, 3)
                if back:
                    for c in range(NC):
                        v.scalar_tensor_tensor(wv[:, c], y2[:, c], mv[:, c, 0:1], gam[:], ALU.subtract,
                                               ALU.mult).then_inc(v_ln, 1)
                    need(dve, v_ln, 8 * (b - 1) + 4)
                    need(dve, g_xb, b)
                    need(dve, g_r1, b)
                    for c in range(NC):
                        v.scalar_tensor_tensor(s1[:, c], wv[:, c], rs[:, c:c + 1], xb[:, 1 - par, c], ALU.mult,
                                               ALU.add).then_inc(v_ln, 1)
                    need(dve, v_ln, 8 * b)
                    moments(s1, mv2, 2 * (b - 1) + 1, v_bn, v_ag, v_woke)
                    v.tensor_scalar(vq[:, 0], mv2[:, :, 1], EPS, None, ALU.add).then_inc(v_M2, 1)
                    need(dve, v_M2, 3 * (b - 1) + 1)
                    v.reciprocal(vq[:, 1], vq[:, 0]).then_inc(v_M2, 1)
                    need(dve, v_M2, 3 * (b - 1) + 2)
                    v.tensor_tensor(vq[:, 1], vq[:, 1], mv2[:, :, 1], ALU.mult).then_inc(v_M2, 1)
                    need(dve, v_M2, 3 * (b - 1) + 3)
                    v.tensor_scalar(vq[:, 1], vq[:, 1], EPS_RMS, None, ALU.add).then_inc(v_ve, 1)
                if core:
                    mask(b, par, 3)
                if route:
                    need(dve, pe_pos, b - 1)
                    posb = PB[1][:, 64:64 + 8 * NC].rearrange("p (c e) -> p c e", c=NC)
                    v.tensor_scalar(over[:], posb, float(CAP), FAR, ALU.is_ge, ALU.mult).then_inc(v_P, 1)
                    v.tensor_tensor(slotv[:], posb, eoff[:], ALU.add).then_inc(v_P, 1)
                    v.tensor_reduce(seen_f[:], mb[:].rearrange("p c e -> p e c"), AX.X, ALU.add).then_inc(v_P, 1)
                    need(dve, v_P, 6 * (b - 2) + 3)
                    v.tensor_tensor(slotv[:], slotv[:], over[:], ALU.add).then_inc(v_P, 1)
                    v.tensor_tensor(seen[:], seen[:], seen_f[:], ALU.add).then_inc(v_M, 1)
                    need(dve, v_P, 6 * (b - 2) + 4)
                    for k in (0, 1):
                        v.tensor_tensor(pick[:, NC * k:NC * (k + 1)], oh[:, NC * k:NC * (k + 1)], slotv[:],
                                        ALU.mult).then_inc(v_M, 1)
                    need(dve, v_M, 6 * (b - 2) + 6)
                    v.tensor_reduce(slotf[:], pick[:], AX.X, ALU.add).then_inc(v_P, 1)
                    need(dve, v_P, 6 * (b - 2) + 5)
                    need(dve, rt_free, b - 1)
                    v.tensor_scalar(slot[:, par], slotf[:], float(SLOTS), None, ALU.min).then_inc(v_slot, 1)
                    need(dve, a_tw, b - 1)
                    v.tensor_scalar(wts[:, par, 0:NC], tw[:], 0.5, 0.5, ALU.mult, ALU.add).then_inc(v_P, 1)
                    v.tensor_scalar(wts[:, par, NC:2 * NC], tw[:], -0.5, 0.5, ALU.mult, ALU.add).then_inc(v_wts, 1)
                if back:
                    need(dve, g_r2, b)
                    need(dve, x1_free, b)
                    need(dve, g_sc, P * (b - 1))
                    for c in range(NC):
                        v.tensor_scalar(x1[:, 1 - par, c], s1[:, c], mv2[:, c, 0:1], rr[:, 1 - par, 0, c:c + 1],
                                        ALU.subtract, ALU.mult).then_inc(v_x1, 1)
                    need(dve, pe_lg, b)
                    v.tensor_copy(lg[:].rearrange("p c e -> p (c e)"), PB[1][:, 0:8 * NC]).then_inc(v_lg, 1)
            stage1(dve, step)

            def step(e, par):
                def split(k, kp):
                    for i, (t0, n) in enumerate(GROUPS):
                        need(dve, e_hi, 3 * k + i + 1)
                        if i == 0:
                            need(dve, e_gu, 12 * (k - 1))
                        cols = slice(P * t0, P * (t0 + n))
                        v.tensor_tensor(xgT_lo[:, kp, cols], PB[(3 * kp + i) % 2][:, 0:P * n],
                                        xgT_hi[:, kp, cols].bitcast(f32), ALU.subtract).then_inc(e_lo, 1)

                def group(n):
                    hp = (n + par) % 2
                    for f in range(4):
                        k = 12 * e + 4 * n + f
                        w = P * GROUPS[n][1]
                        need(dve, e_silu, k + 1)
                        if f == 0:
                            need(dve, e_dn, 3 * e + n - 1)
                        v.tensor_tensor(he[:, hp, f, 0:w], sq[:, f % 2, 0:w], EB[2 + f % 2][:, 0:w],
                                        ALU.mult).then_inc(e_h, 1)
                if isinstance(e, int) and e == 0:
                    split(0, 0)
                group(0)
                if within(e, 0, E - 2):
                    split(e + 1, 1 - par)
                group(1)
                group(2)
            stage2(dve, step)

            def step(m, par):
                def split(k, kp):
                    need(dve, m_hi, k + 1)
                    need(dve, m_gu, 8 * (k - 1))
                    v.tensor_tensor(xlo[:, kp], PB[kp][:], xhi[:, kp].bitcast(f32), ALU.subtract).then_inc(m_lo, 1)

                def hidden(f):
                    need(dve, m_silu, 8 * m + f + 1)
                    if f == 0:
                        need(dve, m_dn, m - 1)
                    v.tensor_tensor(hs[par][:, f], sq[:, f % 2], EB[2 + f % 2][:], ALU.mult).then_inc(m_h, 1)
                work, comb = within(m, 0, B - 1), within(m, 1, B)
                q = 1 - par
                if isinstance(m, int) and m == 0:
                    split(0, 0)
                if work:
                    hidden(0)
                if comb:
                    need(dve, m_g, P * m)
                    for c in range(NC):
                        v.scalar_tensor_tensor(wv[:, c], ge[:, q, 0, c], wts3[:, q, c:c + 1], xin[:, q, c], ALU.mult,
                                               ALU.add).then_inc(m_z, 1)
                    need(dve, m_z, 9 * (m - 1) + 4)
                if work:
                    hidden(1)
                if comb:
                    for c in range(NC):
                        v.scalar_tensor_tensor(s1[:, c], ge[:, q, 1, c], wts3[:, q, NC + c:NC + c + 1], wv[:, c],
                                               ALU.mult, ALU.add).then_inc(m_z, 1)
                if work:
                    hidden(2)
                    hidden(3)
                if comb:
                    need(dve, m_z, 9 * (m - 1) + 8)
                    need(dve, m_dn, m)
                    v.tensor_tensor(y2[:].rearrange("p c d -> p (c d)"), s1[:].rearrange("p c d -> p (c d)"),
                                    (OB, SBK)[q][:], ALU.add).then_inc(m_z, 1)
                    need(dve, m_z, 9 * m)
                    moments(y2, mv, m - 1, m_bn, m_ag, m_woke_v)
                    v.tensor_scalar(ve[:], mv[:, :, 1], EPS, None, ALU.add).then_inc(m_ve, 1)
                if work:
                    hidden(4)
                    hidden(5)
                    if within(m, 0, B - 2):
                        split(m + 1, 1 - par)
                    hidden(6)
                if comb:
                    need(dve, m_r, m)
                    need(dve, m_st, 16 * (m - 2))
                    for c in range(NC):
                        v.tensor_scalar(x1[:, q, c], y2[:, c], mv[:, c, 0:1], rs[:, c:c + 1], ALU.subtract,
                                        ALU.mult).then_inc(m_o, 1)
                if work:
                    hidden(7)
            stage3(dve, step)

        @block.tensor
        def _(pe):
            t = nc.tensor
            pe.wait_ge(ld_w, 9 * 16)
            t.matmul(PB[0][:, 0:D], g1t_s[:], g2_s[:], start=True, stop=True).then_inc(c_g, 1)
            pe.wait_ge(c_pool, 13)

            def three(dst, w_hi, w_lo, x_hi, x_lo):
                t.matmul(dst, w_hi, x_hi, start=True, stop=False)
                t.matmul(dst, w_hi, x_lo, start=False, stop=False)
                return t.matmul(dst, w_lo, x_hi, start=False, stop=True)

            def project(f, i):
                bank = (1, 1, 0, 1)[i]
                if i == 0:
                    need(pe, a_xhi, f + 1)
                    need(pe, v_xlo, f + 1)
                    need(pe, v_lg, f - 2)
                    need(pe, a_kt, 2 * f)
                elif i == 1:
                    need(pe, a_silu, 4 * f + 1)
                elif i == 2:
                    need(pe, v_y, f - 1)
                else:
                    need(pe, a_silu, 4 * f + 2)
                cols = slice(P * i, P * (i + 1))
                three(PB[bank][:], wqk_hi[:, cols], wqk_lo[:, cols], xhi[:, 0], xlo[:, 0]).then_inc(pe_qk, 1)

            def step(b, par):
                f, fp = b + 1, 1 - par
                front, core = within(b, -1, 14), within(b, 0, B - 1)
                back, route = within(b, 1, B), within(b, 2, B + 1)
                if isinstance(b, int) and b == -1:
                    pe.wait_ge(c_dve, 20)

                def energies(c):
                    tok = slice(P * c, P * (c + 1))
                    if c == 0:
                        need(pe, v_qk, 4 * b + 4)
                        need(pe, g_qm, 4 * b + 4)
                    for q in range(4):
                        need(pe, v_mask, 16 * b + 4 * c + q - 3)
                        rows = slice(32 * q, 32 * q + 32)
                        for half in (0, 1):
                            ins = t.matmul(EB[q][:, 256 * half:256 * half + 256], KT[rows, par, half, tok],
                                           QM[rows, par, half, :, tok], start=True, stop=True)
                        ins.then_inc(pe_E, 1)

                def state(c):
                    if c == 0:
                        need(pe, a_kt, 2 * b + 2)
                        need(pe, a_v, 4 * b + 4)
                        need(pe, v_S, 3 * b)
                    else:
                        need(pe, v_S, 3 * b + c)
                    for half in (0, 1):
                        ins = t.matmul(SBK[:, 64 * half:64 * half + 64], Kt[:, par, c, P * half:P * half + P],
                                       v_rows(par, c, half), start=(c == 0 and half == 0), stop=True,
                                       skip_group_check=True)
                    ins.then_inc(pe_S, 1)

                def attend(b, par, c):
                    tok = slice(P * c, P * (c + 1))
                    need(pe, a_out, 4 * b + c)
                    need(pe, a_v, 4 * b + 4)
                    if c > 0:
                        need(pe, v_S, 3 * b + c)
                        for half in (0, 1):
                            t.matmul(OB[64 * half:64 * half + 64, tok], SM[:, (c - 1) % 2, 64 * half:64 * half + 64],
                                     QT[:, par, half, tok], start=True, stop=False)
                    need(pe, v_mask, 16 * b + 4 * c + 4)
                    for i in range(4):
                        for j in range(4):
                            h = 4 * j + i
                            half, q, pair = h // 8, (h % 8) // 2, h % 2
                            e0 = 256 * half + P * pair
                            ins = t.matmul(OB[32 * j:32 * j + 32, tok], VP[:, par, c, 32 * h:32 * h + 32],
                                           EM[:, c % 2, q, e0:e0 + P], start=(c == 0 and i == 0), stop=(i == 3))
                    ins.then_inc(pe_av, 1)

                if core:
                    energies(0)
                    state(0)
                if within(b, 1, B):
                    attend(b - 1, 1 - par, 3)
                if front:
                    need(pe, ld_x, 16 * (f + 1))
                    need(pe, a_x1T, f - 2)
                    need(pe, a_kt, 2 * f)
                    for c in range(NC):
                        ins = t.transpose(PB[0][:, P * c:P * (c + 1)], xin[:, fp, c], ident[:])
                    ins.then_inc(pe_xT, 1)
                    project(f, 0)
                if core:
                    energies(1)
                    state(1)
                    attend(b, par, 0)
                if back:
                    need(pe, a_out, 4 * b)
                    need(pe, a_xhi, last(b + 1) + 1)
                    need(pe, v_xlo, last(b + 1) + 1)
                    for c in range(NC):
                        ins = t.matmul(PB[0][:, P * c:P * (c + 1)], oT[:, 1 - par, P * c:P * (c + 1)], wo_s[:],
                                       start=True, stop=True)
                    ins.then_inc(pe_wo, 1)
                if front:
                    project(f, 1)
                    project(f, 2)
                if core:
                    energies(2)
                    state(2)
                    attend(b, par, 1)
                if front:
                    project(f, 3)
                    for i in (0, 1):
                        need(pe, a_silu, 4 * f + 3 + i)
                        for c in (0, 1):
                            tok = slice(P * (2 * i + c), P * (2 * i + c + 1))
                            ins = three_r(PB[i][:, 256 * c:256 * c + 256], tok)
                        ins.then_inc(pe_vg, 1)
                if core:
                    energies(3)
                    attend(b, par, 2)
                if front:
                    need(pe, v_qk, 4 * f + 4)
                    for i, n in ((0, 2), (1, 1)):
                        need(pe, a_v, 4 * f + 2 * i + 2)
                        need(pe, a_th, 2 * f + i + 1)
                        for c in range(n):
                            for half in (0, 1):
                                ins = t.transpose(PB[i][:, 256 * c + P * half:256 * c + P * half + P],
                                                  KT[:, fp, half, P * (2 * i + c):P * (2 * i + c + 1)], ident[:])
                        ins.then_inc(pe_kt, 1)
                if route:
                    need(pe, v_M, 6 * (b - 2) + 3)
                    need(pe, a_kt, 2 * last(b + 1) + 2)
                    o = PB[1][:, 64:64 + 8 * NC]
                    t.matmul(o.rearrange("p (c e) -> p c e", c=NC), ones[:], seen[:].unsqueeze(1).broadcast_to([P, NC, 8]),
                             start=True, stop=False)
                    mf = mb[:].rearrange("p c e -> p (c e)")
                    for k in (1, 2, 3):
                        t.matmul(o[:, 8 * k:8 * NC], ones[:], mf[:, 0:8 * (NC - k)], start=False, stop=False,
                                 skip_group_check=True)
                    t.matmul(o, before[:], mf, start=False, stop=True).then_inc(pe_pos, 1)
                if back:
                    need(pe, v_x1, 4 * b)
                    need(pe, a_kt, 2 * last(b + 1) + 1)
                    for c in range(NC):
                        ins = t.transpose(PB[0][:, P * c:P * (c + 1)], x1[:, 1 - par, c], ident[:])
                    ins.then_inc(pe_x1T, 1)
                    need(pe, a_x1T, b)
                    need(pe, a_kt, 2 * last(b + 1) + 2)
                    need(pe, v_P, 6 * (b - 2) + 2)
                    for c in range(NC):
                        ins = t.matmul(PB[1][:, 8 * c:8 * c + 8], x1T[:, P * c:P * (c + 1)], rwt_s[:], start=True, stop=True)
                    ins.then_inc(pe_lg, 1)

            def three_r(dst, tok):
                t.matmul(dst, xhi[:, 0, tok], wvg_hi[:], start=True, stop=False)
                t.matmul(dst, xhi[:, 0, tok], wvg_lo[:], start=False, stop=False)
                return t.matmul(dst, xlo[:, 0, tok], wvg_hi[:], start=False, stop=True)

            def v_rows(par, c, half):
                v = VP[:, par, c]
                return bass.AP(tensor=v.tensor, offset=v.offset + 256 * half, ap=[list(v.ap[0]), [128, 2], [40, 4], [1, 8]])
            stage1(pe, step)

            def step(e, par):
                def turn_rows(k, kp):
                    need(pe, e_ldx, 16 * (k + 1))
                    for i, (t0, n) in enumerate(GROUPS):
                        bank = (3 * kp + i) % 2
                        need(pe, e_lo, 3 * k + i - 1)
                        for c in range(n):
                            ins = t.transpose(PB[bank][:, P * c:P * (c + 1)], xg[:, kp, t0 + c], ident[:])
                        ins.then_inc(e_xT, 1)

                def gate_up(n):
                    cols = slice(P * GROUPS[n][0], P * (GROUPS[n][0] + GROUPS[n][1]))
                    w = P * GROUPS[n][1]
                    need(pe, e_lo, 3 * e + n + 1)
                    need(pe, e_hi, 3 * e + n + 1)
                    need(pe, e_w, 4 * e + 4)
                    for f in range(4):
                        need(pe, e_h, 12 * e + 4 * n + f - 1)
                        ff = slice(P * f, P * (f + 1))
                        for gu in (0, 1):
                            ins = three(EB[2 * gu + f % 2][:, 0:w], we_hi[:, par, gu, ff], we_lo[:, par, gu, ff],
                                        xgT_hi[:, par, cols], xgT_lo[:, par, cols])
                        ins.then_inc(e_gu, 1)

                def down(n):
                    hp = (n + par) % 2
                    need(pe, e_h, 12 * e + 4 * n + 4)
                    need(pe, e_y, 3 * e + n - 1)
                    for c in range(GROUPS[n][1]):
                        for f in range(4):
                            ins = t.matmul((OB, SBK)[hp][:, P * c:P * (c + 1)], he[:, hp, f, P * c:P * (c + 1)],
                                           wd[:, par, f], start=(f == 0), stop=(f == 3))
                    ins.then_inc(e_dn, 1)
                if isinstance(e, int) and e == 0:
                    turn_rows(0, 0)
                gate_up(0)
                if within(e, 0, E - 2):
                    turn_rows(e + 1, 1 - par)
                gate_up(1)
                down(0)
                gate_up(2)
                down(1)
                down(2)
            stage2(pe, step)

            pe.wait_ge(s_w, 4)

            def step(m, par):
                def turn_rows(k, kp):
                    need(pe, m_ld, 48 * (k + 1))
                    need(pe, m_lo, k - 1)
                    for c in range(NC):
                        ins = t.transpose(PB[kp][:, P * c:P * (c + 1)], xin[:, kp, c], ident[:])
                    ins.then_inc(m_xT, 1)

                def down(k, kp):
                    need(pe, m_h, 8 * (k + 1))
                    need(pe, m_z, 9 * (k - 1))
                    for c in range(NC):
                        for f in range(8):
                            ins = t.matmul((OB, SBK)[kp][:, P * c:P * (c + 1)], hs[kp][:, f, P * c:P * (c + 1)],
                                           sd_s[:, f], start=(f == 0), stop=(f == 7))
                    ins.then_inc(m_dn, 1)
                if isinstance(m, int) and m == 0:
                    turn_rows(0, 0)
                if within(m, 0, B - 1):
                    need(pe, m_lo, m + 1)
                    need(pe, m_hi, m + 1)
                    for f in range(8):
                        need(pe, m_h, 8 * m + f - 1)
                        ff = slice(P * f, P * (f + 1))
                        for gu in (0, 1):
                            ins = three(EB[2 * gu + f % 2][:], ws_hi[:, gu, ff], ws_lo[:, gu, ff], xhi[:, par], xlo[:, par])
                        ins.then_inc(m_gu, 1)
                        if f == 1 and within(m, 1, B):
                            down(m - 1, 1 - par)
                        if f == 5 and within(m, 0, B - 2):
                            turn_rows(m + 1, 1 - par)
                else:
                    down(m - 1, 1 - par)
            stage3(pe, step)


def kernel(**inputs):
    import numpy as _np
    import concourse.bacc as _bacc
    from concourse import mybir as _mybir
    from concourse.bass_utils import run_bass_kernel_spmd as _run

    d = {k.split("_", 2)[2]: _np.ascontiguousarray(_np.asarray(v)) for k, v in inputs.items() if k != "L0_attn_x"}
    x = _np.ascontiguousarray(_np.asarray(inputs["L0_attn_x"]))
    def doubled(w):
        w = w.reshape(D, 2, H // 2, 1, HD)
        return _np.broadcast_to(w, (D, 2, H // 2, 2, HD)).reshape(D, 2 * P)
    theta = _np.broadcast_to(d["theta"].reshape(2, H // 2, 1, HD), (2, H // 2, 2, HD)).reshape(2, P).T
    arrays = {
        "x": x, "wqk": _np.concatenate([doubled(d["Wq"]), doubled(d["Wk"])], axis=1), "wv": d["Wv"],
        "g1t": d["G1"].T, "g2": d["G2"], "wo": d["Wo"], "gamma": d["gamma"], "beta": d["beta"], "theta": theta,
        "rwt": d["router_w"].T, "rg": d["rg"], "ru": d["ru"], "rd": d["rd"], "sg": d["sg"], "su": d["su"], "sd": d["sd"],
    }
    arrays = {f"in_{k}": _np.ascontiguousarray(v) for k, v in arrays.items()}
    nc = _bacc.Bacc("TRN2", target_bir_lowering=False, num_devices=1)
    args = [nc.dram_tensor(k, v.shape, _mybir.dt.from_np(v.dtype), kind="ExternalInput").ap() for k, v in arrays.items()]
    args.append(nc.dram_tensor("out_x", (B, S, D), _mybir.dt.float32, kind="ExternalOutput").ap())
    build(nc, *args)
    r = _run(nc, [arrays], core_ids=[0])
    return r.results[0]["out_x"]
```

```python
import concourse.bass as bass
from concourse import mybir
from contextlib import ExitStack

f32 = mybir.dt.float32
f32r = mybir.dt.float32r
bf16 = mybir.dt.bfloat16
i32 = mybir.dt.int32
u32 = mybir.dt.uint32
ALU = mybir.AluOpType
ACT = mybir.ActivationFunctionType
AX = mybir.AxisListType

P = 128
D = 128
B, S = 16, 512
NC = S // P
T = 64
NS = S // T - 1
H, HD = 16, 8
E, FR, FS = 8, 512, 1024
CAP = int(1.25 * B * S / E)
SLOTS = E * CAP
CT = CAP // P
GROUPS = [(0, 4), (4, 4), (8, 2)]
EPS = 1e-5
EPS_RMS = 2.0 ** -23
FAR = 16384.0
TWO_PI = [6.28125, 0.0019350051879882812, 3.01991598e-07]
MAGIC = 12582912.0
PI_IN = 3.1415925


def build(nc, x, wqk, wvg, g1t, g2, wo, gamma, beta, theta, rwt, rg, ru, rd, sg, su, sd, out):
    x_v = x.rearrange("b (c p) d -> b p c d", p=P)
    out_v = out.rearrange("b (c p) d -> b p c d", p=P)
    ctx = ExitStack()
    with ctx:
        def sb(name, shape, dt=f32):
            return ctx.enter_context(nc.sbuf_tensor(name, shape, dt))

        def sem(name):
            return ctx.enter_context(nc.semaphore(name))

        xg_d = nc.dram_tensor("dispatched_rows", [SLOTS, D], f32, kind="Internal").ap()
        yd_d = nc.dram_tensor("expert_rows", [SLOTS + P, D], f32, kind="Internal").ap()
        x1_d = nc.dram_tensor("x1_rows", [B, P, NC * D], f32, kind="Internal").ap()
        slot_d = nc.dram_tensor("slots", [B, P, 2 * NC], i32, kind="Internal").ap()
        weight_d = nc.dram_tensor("weights", [B, P, 2 * NC], f32, kind="Internal").ap()

        ident = sb("ident", [P, P])
        causal = sb("causal", [P, T])
        before = sb("before", [P, P], bf16)
        before_f = sb("before_f", [P, P])
        ones = sb("ones", [P, P], bf16)
        headmask = sb("headmask", [P, 2, 64])
        bits = sb("bits", [P, 3, 8])
        pairmask = sb("pairmask", [P, 3])
        iota8 = sb("iota8", [P, 2 * NC, 8])
        eoff = sb("eoff", [P, NC, 8])
        minus_half = sb("minus_half", [P, 8])
        gam = sb("gam", [P, D])
        bet = sb("bet", [P, D])
        zeros = sb("zeros", [P, CT * D])
        theta_s = sb("theta_s", [P, 2])
        phase = sb("phase", [P, 2])
        table = sb("table", [P, 2, S])
        rwt_s = sb("rwt_s", [P, E])
        wo_s = sb("wo_s", [P, D])
        g1t_s = sb("g1t_s", [8, D])
        g2_s = sb("g2_s", [8, D])
        wqk_hi = sb("wqk_hi", [P, 512], f32r)
        wqk_lo = sb("wqk_lo", [P, 512], f32r)
        wvg_hi = sb("wvg_hi", [P, 256], f32r)
        wvg_lo = sb("wvg_lo", [P, 256], f32r)
        warm = sb("warm", [P, 1])

        xin = sb("xin", [P, 2, NC, D])
        xb = sb("xb", [P, 2, NC, D])
        xhi = sb("xhi", [P, 2, S], f32r)
        xlo = sb("xlo", [P, 2, S], f32r)
        sq = sb("sq", [P, 2, S])
        QT = sb("QT", [P, 2, 2, S])
        KT = sb("KT", [P, 2, 2, S])
        QM = sb("QM", [P, 2, 2, 2, S])
        Kt = sb("Kt", [P, 2, NC, 256])
        VP = sb("VP", [P, 2, NC, 512])
        EM = sb("EM", [P, 2, 4, 256])
        SM = sb("SM", [P, 8, 128])
        oT = sb("oT", [P, 2, S])
        th = sb("th", [P, 2, S])
        y2 = sb("y2", [P, NC, D])
        pos_n = y2[:].rearrange("p c d -> p (c d)")
        wv = sb("wv", [P, NC, D])
        s1 = sb("s1", [P, NC, D])
        x1 = sb("x1", [P, 2, NC, D])
        x1T = sb("x1T", [P, S])
        st = sb("st", [P, NC, 6])
        mv = sb("mv", [P, NC, 2])
        mv2 = sb("mv2", [P, NC, 2])
        ve = sb("ve", [P, NC])
        rs = sb("rs", [P, NC])
        vq = sb("vq", [P, 2, NC])
        rr = sb("rr", [P, 2, 2, NC])
        lg = sb("lg", [P, NC, 8])
        m8 = sb("m8", [P, NC, 8])
        ix8 = sb("ix8", [P, NC, 8], u32)
        ixf = sb("ixf", [P, 2, NC])
        oh = sb("oh", [P, 2 * NC, 8])
        mb = sb("mb", [P, NC, 8], bf16)
        seen = sb("seen", [P, 8], bf16)
        seen_f = sb("seen_f", [P, 8])
        over = sb("over", [P, NC, 8])
        slotv = sb("slotv", [P, NC, 8])
        pick = sb("pick", [P, 2 * NC, 8])
        slotf = sb("slotf", [P, 2 * NC])
        gap = sb("gap", [P, NC])
        gapr = sb("gapr", [P, NC])
        tw = sb("tw", [P, NC])
        slot = sb("slot", [P, 2, 2 * NC], i32)
        wts = sb("wts", [P, 2, 2 * NC])

        xgT_hi = sb("xgT_hi", [P, 2, CAP], f32r)
        xgT_lo = sb("xgT_lo", [P, 2, CAP], f32r)
        we_hi = sb("we_hi", [P, 2, 2, FR], f32r)
        we_lo = sb("we_lo", [P, 2, 2, FR], f32r)
        ws_hi = sb("ws_hi", [P, 2, FS], f32r)
        ws_lo = sb("ws_lo", [P, 2, FS], f32r)
        sd_s = sb("sd_s", [P, FS // P, D])
        sf = sb("sf", [P, 2, S])
        xs = zeros[:, 0:2 * S].rearrange("p (i c d) -> p i c d", i=2, c=NC)
        flat = lambda t: t[:].rearrange({4: "p a b c -> p (a b c)", 3: "p a b -> p (a b)", 5: "p a b c d -> p (a b c d)"}[len(t.shape)])
        xg = flat(QM)[:, 0:2 * CT * D].rearrange("p (e j d) -> p e j d", e=2, j=CT)
        ye = flat(VP)[:, 0:2 * CT * D].rearrange("p (e j d) -> p e j d", e=2, j=CT)
        wraw = flat(QT).rearrange("p (e g n) -> p e g n", e=2, g=2)
        wd = flat(KT)[:, 0:2 * FR].rearrange("p (e f d) -> p e f d", e=2, f=FR // P)
        he = sb("he", [P, 2, FR // P, S])
        sraw = [flat(he)[:, 0:FS], flat(he)[:, FS:2 * FS]]
        hs = flat(he).rearrange("p (f n) -> p f n", n=S)
        ge = flat(QT).rearrange("p (m k c d) -> p m k c d", m=2, k=2, c=NC)
        slot3 = sb("slot3", [P, 2, 2 * NC], i32)
        wts3 = sb("wts3", [P, 2, 2 * NC])

        EB2 = ctx.enter_context(nc.psum_tensor("energy_banks", [P, 2, 512], f32))
        banks = [ctx.enter_context(nc.psum_tensor(f"bank{i}", [P, 512], f32)) for i in range(6)]
        PB, OB, SBK, GB, UB = banks[0:2], banks[2], banks[3], banks[4], banks[5]
        EB = [EB2[:, 0], EB2[:, 1], GB, UB]

        ld_w = sem("weights_loaded"); ld_x = sem("x_loaded"); c_pool = sem("pool_constants")
        c_dve = sem("dve_constants"); c_sin = sem("table_ready"); c_g = sem("g1g2_product"); c_warm = sem("act_table_warm")
        pe_xT = sem("x_transposed")
        pe_qk = sem("qk_projected")
        pe_vg = sem("vg_projected")
        pe_kt = sem("k_by_token")
        pe_E = sem("energies")
        pe_S = sem("state_summed")
        pe_av0 = sem("first_block_out")
        pe_av = sem("attention_out")
        pe_wo = sem("wo_projected")
        pe_x1T = sem("x1_transposed")
        pe_lg = sem("logits")
        pe_gt = sem("shared_gate")
        pe_up = sem("shared_up")
        pe_dn = sem("shared_down")
        a_x1h = sem("x1hi_ready"); v_x1l = sem("x1lo_ready"); a_sf = sem("shared_silu"); v_h = sem("shared_hidden"); v_xs = sem("shared_added")
        pe_woke = sem("tensor_woke"); pe_pos = sem("positions")
        a_xhi = sem("xhi_ready"); a_silu = sem("silu_ready"); a_v = sem("v_ready"); a_th = sem("gate_ready")
        a_kt = sem("kt_ready"); a_out = sem("out_copied"); a_x1T = sem("x1T_ready"); a_tw = sem("route_tanh")
        v_xlo = sem("xlo_ready"); v_qk = sem("qk_turned"); v_mask = sem("energies_masked"); v_S = sem("state_masked")
        v_y = sem("gated"); v_bn = sem("stats"); v_ag = sem("moments"); v_ve = sem("variance_eps"); v_ln = sem("ln_steps")
        v_x1 = sem("x1_ready"); v_lg = sem("logits_copied"); v_rt = sem("route_steps"); v_M = sem("choices_ready")
        v_gap = sem("gap_ready"); v_slot = sem("slots_ready"); v_pos = sem("positions_read"); v_wts = sem("weights_ready"); v_woke = sem("vector_woke")
        v_M2 = sem("mean_square_steps"); v_P = sem("slot_steps")
        g_qm = sem("q_by_pair"); g_xb = sem("x_beta"); g_r1 = sem("rstd1"); g_r2 = sem("rstd2"); g_woke = sem("gpsimd_woke")
        g_sc = sem("rows_dispatched")
        sp_x1 = sem("sums_stored"); sp_rt = sem("route_stored"); xs_free = sem("sums_kept"); rt_free = sem("route_kept"); sp_woke = sem("sync_woke")
        e_ld = sem("expert_weights_loaded"); e_ldx = sem("expert_rows_loaded"); e_xT = sem("e_transposed"); e_gt = sem("e_gate"); e_gu = sem("e_up"); e_dn = sem("e_down")
        e_hi = sem("e_xhi"); e_lo = sem("e_xlo"); e_silu = sem("e_silu"); e_h = sem("e_hidden"); e_y = sem("e_copied")
        e_w = sem("e_weights_split"); e_yst = sem("e_stored"); ye_free = sem("e_rows_kept"); s_ld = sem("shared_loaded"); s_w = sem("shared_split")
        m_ld = sem("m_loaded"); m_xT = sem("m_transposed"); m_hi = sem("m_xhi"); m_lo = sem("m_xlo"); m_gu = sem("m_gate_up")
        m_silu = sem("m_silu"); m_h = sem("m_hidden"); m_dn = sem("m_down"); m_g = (sem("m_gathered_even"), sem("m_gathered_odd")); m_z = sem("m_sums")
        m_bn = sem("m_stats"); m_ag = sem("m_moments"); m_ve = sem("m_variance_eps"); m_r = sem("m_rstd"); m_o = sem("m_normed")
        m_st = sem("m_stored"); m_woke_v = sem("m_vector_woke"); m_woke_g = sem("m_gpsimd_woke")

        def need(eng, s, value):
            if not isinstance(value, int) or value > 0:
                eng.wait_ge(s, value)

        def hold(eng, s, value, woke):
            if not isinstance(value, int) or value > 0:
                eng.wait_ge(s, value)
                eng.sem_inc(woke, 1)

        def last(n):
            return min(n, B - 1) if isinstance(n, int) else n

        def within(b, lo, hi):
            return not isinstance(b, int) or lo <= b <= hi

        def stage1(eng, step):
            for b in (-1, 0, 1, 2):
                step(b, b % 2)
            with eng.Fori(1, 6) as i:
                for k in (1, 2):
                    step(i * 2 + k, k % 2)
            for b in (13, 14, 15, 16, 17, 18):
                step(b, b % 2)

        def stage2(eng, step):
            step(0, 0)
            with eng.Fori(0, 2) as i:
                for k in (1, 2):
                    step(i * 2 + k, k % 2)
            for e in (5, 6, 7):
                step(e, e % 2)

        def stage3(eng, step):
            for m in (0, 1, 2):
                step(m, m % 2)
            with eng.Fori(0, 6) as i:
                for k in (3, 4):
                    step(i * 2 + k, k % 2)
            step(B - 1, 1)
            step(B, 0)

        block = ctx.enter_context(nc.Block())

        @block.sync
        def _(sp):
            sp.dma_start(xin[:, 0], x_v[0]).then_inc(ld_x, 16)
            for dst, src in [(sq[:, 0], wqk), (sq[:, 1, 0:D], wvg), (g1t_s[:], g1t), (g2_s[:], g2), (wo_s[:], wo),
                             (theta_s[:], theta), (rwt_s[:], rwt),
                             (gam[:], gamma.rearrange("(o d) -> o d", o=1).broadcast_to([P, D])),
                             (bet[:], beta.rearrange("(o d) -> o d", o=1).broadcast_to([P, D]))]:
                sp.dma_start(dst, src).then_inc(ld_w, 16)
            sp.wait_ge(ld_x, 16)
            sp.dma_start(xin[:, 1], x_v[1]).then_inc(ld_x, 16)
            sp.dma_start(sraw[0], sg).then_inc(s_ld, 16)
            sp.dma_start(sraw[1], su).then_inc(s_ld, 16)
            sp.dma_start(sd_s[:], sd.rearrange("(f p) d -> p f d", p=P)).then_inc(s_ld, 16)
            sp.wait_ge(c_pool, 1)
            sp.dma_start(yd_d[SLOTS:SLOTS + P], zeros[:, 0:D]).then_inc(s_ld, 16)
            sp.sem_inc(xs_free, 2)
            sp.sem_inc(rt_free, 2)
            sp.sem_inc(ye_free, 2)

            def step(b, par):
                if within(b, 0, 13):
                    hold(sp, ld_x, 16 * (b + 2), sp_woke)
                    hold(sp, pe_xT, b + 1, sp_woke)
                    hold(sp, g_xb, b + 1, sp_woke)
                    sp.dma_start(xin[:, par], x_v[b + 2]).then_inc(ld_x, 16)
                if within(b, 3, B + 2):
                    hold(sp, v_xs, b - 2, sp_woke)
                    sp.dma_start(x1_d[b - 3], xs[:, 1 - par].rearrange("p c d -> p (c d)")).then_inc(sp_x1, 16)
                    hold(sp, sp_x1, 16 * (b - 2), sp_woke)
                    sp.sem_inc(xs_free, 1)
                if within(b, 2, B + 1):
                    hold(sp, v_slot, b - 1, sp_woke)
                    hold(sp, v_wts, b - 1, sp_woke)
                    sp.dma_start(slot_d[b - 2], slot[:, par]).then_inc(sp_rt, 16)
                    sp.dma_start(weight_d[b - 2], wts[:, par]).then_inc(sp_rt, 16)
                    hold(sp, sp_rt, 32 * (b - 1), sp_woke)
                    sp.sem_inc(rt_free, 1)
            stage1(sp, step)

            sp.wait_ge(pe_av, 4 * B)

            def load_weights(e, par):
                sp.dma_start(wraw[:, par, 0], rg[e]).then_inc(e_ld, 16)
                sp.dma_start(wraw[:, par, 1], ru[e]).then_inc(e_ld, 16)
                sp.dma_start(wd[:, par], rd[e].rearrange("(f p) d -> p f d", p=P)).then_inc(e_ld, 16)

            def load_rows(e, par):
                sp.dma_start(xg[:, par], xg_r[e]).then_inc(e_ldx, 16)

            xg_r = xg_d.rearrange("(e p j) d -> e p j d", e=E, p=P)
            yd_r = yd_d[0:SLOTS].rearrange("(e p j) d -> e p j d", e=E, p=P)
            load_weights(0, 0)
            sp.wait_ge(g_sc, P * (B + 1))
            load_rows(0, 0)
            sp.wait_ge(e_ldx, 16)
            load_rows(1, 1)

            def step(e, par):
                if within(e, 0, E - 2):
                    hold(sp, e_ld, 48 * (e + 1), sp_woke)
                    hold(sp, e_w, 4 * e, sp_woke)
                    hold(sp, e_dn, 3 * e, sp_woke)
                    load_weights(e + 1, 1 - par)
                if within(e, 1, E):
                    hold(sp, e_y, 3 * e, sp_woke)
                    hold(sp, e_yst, 16 * (e - 1), sp_woke)
                    sp.dma_start(yd_r[e - 1], ye[:, 1 - par]).then_inc(e_yst, 16)
                if within(e, 0, E - 3):
                    hold(sp, e_ldx, 16 * (e + 2), sp_woke)
                    hold(sp, e_xT, 3 * (e + 1), sp_woke)
                    load_rows(e + 2, par)
                if within(e, 1, E):
                    hold(sp, e_yst, 16 * e, sp_woke)
                    sp.sem_inc(ye_free, 1)
            stage2(sp, step)
            step(E, 0)

            def load_batch(m, par):
                sp.dma_start(xin[:, par].rearrange("p c d -> p (c d)"), x1_d[m]).then_inc(m_ld, 16)
                sp.dma_start(slot3[:, par], slot_d[m]).then_inc(m_ld, 16)
                sp.dma_start(wts3[:, par], weight_d[m]).then_inc(m_ld, 16)
            load_batch(0, 0)

            def step(m, par):
                if within(m, 0, B - 2):
                    hold(sp, m_ld, 48 * (m + 1), sp_woke)
                    hold(sp, m_z, 8 * m, sp_woke)
                    load_batch(m + 1, 1 - par)
                if within(m, 1, B):
                    hold(sp, m_o, 4 * m, sp_woke)
                    hold(sp, m_st, 16 * (m - 1), sp_woke)
                    sp.dma_start(out_v[m - 1], x1[:, 1 - par]).then_inc(m_st, 16)
            stage3(sp, step)
            sp.wait_ge(m_st, 16 * B)

        @block.gpsimd
        def _(gp):
            g = nc.gpsimd
            g.memset(zeros[:], 0.0).then_inc(c_pool, 1)
            g.memset(ident[:], 0.0).then_inc(c_pool, 1)
            g.memset(causal[:], 1.0).then_inc(c_pool, 1)
            g.memset(before_f[:], 1.0).then_inc(c_pool, 1)
            g.memset(ones[:], 1.0).then_inc(c_pool, 1)
            g.memset(headmask[:], 1.0).then_inc(c_pool, 1)
            g.memset(bits[:], 1.0).then_inc(c_pool, 1)
            g.memset(minus_half[:], -0.5).then_inc(c_pool, 1)
            g.memset(seen[:], 0.0).then_inc(c_pool, 1)
            g.iota(iota8[:], [[0, 2 * NC], [1, 8]], base=0, channel_multiplier=0,
                   allow_small_or_imprecise_dtypes=True).then_inc(c_pool, 1)
            g.iota(eoff[:], [[0, NC], [CAP, 8]], base=0, channel_multiplier=0,
                   allow_small_or_imprecise_dtypes=True).then_inc(c_pool, 1)
            g.iota(pos_n, [[1, S]], base=0, channel_multiplier=0,
                   allow_small_or_imprecise_dtypes=True).then_inc(c_pool, 1)
            gp.wait_ge(c_pool, 12)
            g.affine_select(out=ident[:], in_=ident[:], compare_op=ALU.not_equal, fill=1.0, base=0,
                            pattern=[[-1, P]], channel_multiplier=1).then_inc(c_pool, 1)
            for n, rows in ((13, slice(0, T)), (14, slice(T, P))):
                gp.wait_ge(c_pool, n)
                g.affine_select(out=causal[rows], in_=causal[rows], compare_op=ALU.is_ge, fill=0.0, base=0,
                                pattern=[[1, T]], channel_multiplier=-1).then_inc(c_pool, 1)
            gp.wait_ge(c_pool, 15)
            g.affine_select(out=before_f[:], in_=before_f[:], compare_op=ALU.is_gt, fill=0.0, base=0,
                            pattern=[[1, P]], channel_multiplier=-1).then_inc(c_pool, 1)
            hm = headmask[:].rearrange("p t (h j) -> p t h j", h=8)
            g.affine_select(out=hm, in_=hm, compare_op=ALU.is_ge, fill=0.0, base=0,
                            pattern=[[0, 2], [-16, 8], [0, 8]], channel_multiplier=1).then_inc(c_pool, 1)
            for v in (0, 1):
                g.affine_select(out=bits[:, v, 0:4], in_=bits[:, v, 0:4], compare_op=ALU.is_ge, fill=0.0, base=-16 * v,
                                pattern=[[-32, 4]], channel_multiplier=1).then_inc(c_pool, 1)
            g.affine_select(out=bits[:, 2], in_=bits[:, 2], compare_op=ALU.is_ge, fill=0.0, base=0,
                            pattern=[[-16, 8]], channel_multiplier=1).then_inc(c_pool, 1)
            gp.wait_ge(c_pool, 20)
            g.affine_select(out=hm, in_=hm, compare_op=ALU.is_ge, fill=0.0, base=15,
                            pattern=[[0, 2], [16, 8], [0, 8]], channel_multiplier=-1).then_inc(c_pool, 1)
            for v in (0, 1):
                g.affine_select(out=bits[:, v, 0:4], in_=bits[:, v, 0:4], compare_op=ALU.is_ge, fill=0.0, base=15 + 16 * v,
                                pattern=[[32, 4]], channel_multiplier=-1).then_inc(c_pool, 1)
            g.affine_select(out=bits[:, 2], in_=bits[:, 2], compare_op=ALU.is_ge, fill=0.0, base=7,
                            pattern=[[16, 8]], channel_multiplier=-1).then_inc(c_pool, 1)
            g.memset(VP[:, 0], 0.0).then_inc(c_pool, 1)
            g.memset(VP[:, 1], 0.0).then_inc(c_pool, 1)
            xg_r = xg_d.rearrange("(e p j) d -> e p (j d)", e=E, p=P)
            for e in range(E):
                gp.dma_start(xg_r[e], zeros[:]).then_inc(g_sc, 16)
            gp.wait_ge(c_dve, 2)
            gp.wait_ge(c_pool, 26)
            gp.wait_ge(ld_w, 9 * 16)

            def step(b, par):
                f = b + 1
                if within(b, 1, B):
                    need(gp, v_ve, 2 * b - 1)
                    g.tensor_tensor(rs[:], ve[:], minus_half[:, 0:NC], ALU.pow).then_inc(g_r1, 1)

                def by_pair(t):
                    hold(gp, v_qk, 4 * f + t + 1, g_woke)
                    hold(gp, pe_E, 8 * (f - 1), g_woke)
                    for v in (0, 1):
                        g.tensor_scalar(QM[:, 1 - par, t, v], QT[:, 1 - par, t], pairmask[:, v:v + 1], None,
                                        ALU.mult).then_inc(g_qm, 1)
                if within(b, -1, 14):
                    by_pair(0)
                    by_pair(1)
                if within(b, 1, B):
                    need(gp, v_ve, 2 * b)
                    g.tensor_tensor(rr[:, 1 - par], vq[:], minus_half[:].rearrange("p (a c) -> p a c", a=2),
                                    ALU.pow).then_inc(g_r2, 1)
                if within(b, -1, 14):
                    need(gp, ld_x, 16 * (f + 1))
                    need(gp, v_ln, 8 * (f - 1))
                    g.tensor_tensor(xb[:, 1 - par], xin[:, 1 - par], bet[:].unsqueeze(1).broadcast_to([P, NC, D]),
                                    ALU.add).then_inc(g_xb, 1)
                if isinstance(b, int) and b == 0:
                    gp.wait_ge(s_ld, 64)
                    for i in (0, 1):
                        g.tensor_copy(ws_hi[:, i], sraw[i]).then_inc(s_w, 1)
                        gp.wait_ge(s_w, 2 * i + 1)
                        g.tensor_tensor(ws_lo[:, i], sraw[i], ws_hi[:, i].bitcast(f32), ALU.subtract).then_inc(s_w, 1)
                if within(b, 2, B + 1):
                    hold(gp, g_sc, P * (b - 1), g_woke)
                    hold(gp, v_slot, b - 1, g_woke)
                    for j in range(2 * NC):
                        g.indirect_dma_start(out=xg_d, out_offset=bass.IndirectOffsetOnAxis(ap=slot[:, par, j:j + 1], axis=0),
                                             in_=x1[:, par, j % NC, :], in_offset=None, bounds_check=SLOTS - 1,
                                             oob_is_err=False).then_inc(g_sc, 16)
            stage1(gp, step)

            def step(e, par):
                for i in (0, 1):
                    hold(gp, e_ld, 48 * (e + 1), m_woke_g)
                    g.tensor_copy(we_hi[:, par, i], wraw[:, par, i]).then_inc(e_w, 1)
                    need(gp, e_w, 4 * e + 2 * i + 1)
                    g.tensor_tensor(we_lo[:, par, i], wraw[:, par, i], we_hi[:, par, i].bitcast(f32),
                                    ALU.subtract).then_inc(e_w, 1)
            stage2(gp, step)

            gp.wait_ge(e_yst, 16 * E)

            def step(m, par):
                if within(m, 0, B - 1):
                    hold(gp, m_ld, 48 * (m + 1), m_woke_g)
                    hold(gp, m_z, 8 * (m - 1), m_woke_g)
                    for j in range(2 * NC):
                        g.indirect_dma_start(out=ge[:, par, j // NC, j % NC, :], out_offset=None, in_=yd_d[0:SLOTS + 1],
                                             in_offset=bass.IndirectOffsetOnAxis(ap=slot3[:, par, j:j + 1], axis=0)
                                             ).then_inc(m_g[par], 16)
                if within(m, 1, B):
                    need(gp, m_ve, m)
                    g.tensor_tensor(rs[:], ve[:], minus_half[:, 0:NC], ALU.pow).then_inc(m_r, 1)
            stage3(gp, step)

        @block.scalar
        def _(act):
            a = nc.scalar
            act.wait_ge(c_pool, 1)
            a.activation(warm[:], zeros[:, 0:1], ACT.Silu).then_inc(c_warm, 1)
            act.wait_ge(c_dve, 15)
            a.activation(table[:], table[:], ACT.Sin).then_inc(c_sin, 1)
            act.wait_ge(c_pool, 26)

            def silu(f, par, i):
                need(act, pe_qk, 4 * f + i + 1)
                need(act, v_qk, 4 * f + i - 1)
                a.activation(sq[:, i % 2], PB[i % 2][:], ACT.Silu).then_inc(a_silu, 1)

            def copy_out(b, c, par):
                need(act, pe_av, 4 * b + c + 1)
                need(act, pe_wo, b - 1)
                a.activation(oT[:, par, P * c:P * (c + 1)], OB[:, P * c:P * (c + 1)], ACT.Copy).then_inc(a_out, 1)

            def values(f, par, i):
                need(act, pe_vg, 2 * f + i + 1)
                need(act, pe_av, 4 * (f - 1))
                for c in (0, 1):
                    src = PB[i][:, 256 * c:256 * c + D].rearrange("p (j i d) -> p j i d", j=4, i=4)
                    a.activation(vp_view(par, 2 * i + c), src, ACT.Copy).then_inc(a_v, 1)
                need(act, v_y, f - 1)
                src = PB[i][:].rearrange("p (c n) -> p c n", c=2)[:, :, D:2 * D]
                dst = th[:, par].rearrange("p (c n) -> p c n", c=NC)[:, 2 * i:2 * i + 2]
                a.activation(dst, src, ACT.Tanh, scale=0.5).then_inc(a_th, 1)

            def shared_silu(b, f):
                if within(b, 2, B + 1):
                    n = 8 * (b - 2) + f
                    need(act, pe_gt, n + 1)
                    need(act, v_h, n - 1)
                    a.activation(sf[:, f % 2], GB[:], ACT.Silu).then_inc(a_sf, 1)

            def step(b, par):
                f, fp = b + 1, 1 - par
                front, core = within(b, -1, 14), within(b, 0, B - 1)
                if within(b, 1, B):
                    copy_out(b - 1, 3, 1 - par)
                if front:
                    need(act, pe_xT, f + 1)
                    need(act, pe_vg, 2 * f)
                    a.activation(xhi[:, 0], PB[0][:], ACT.Copy).then_inc(a_xhi, 1)
                if within(b, 2, B + 1):
                    need(act, pe_x1T, b - 1)
                    a.activation(x1T[:], PB[1][:], ACT.Copy).then_inc(a_x1T, 1)
                    need(act, a_x1T, b - 1)
                    a.activation(xhi[:, 1], x1T[:], ACT.Copy).then_inc(a_x1h, 1)
                if front:
                    silu(f, fp, 0)
                shared_silu(b, 0)
                if core:
                    copy_out(b, 0, par)
                shared_silu(b, 1)
                if front:
                    silu(f, fp, 1)
                shared_silu(b, 2)
                if core:
                    copy_out(b, 1, par)
                shared_silu(b, 3)
                if front:
                    silu(f, fp, 2)
                    silu(f, fp, 3)
                shared_silu(b, 4)
                if front:
                    values(f, fp, 0)
                    values(f, fp, 1)
                shared_silu(b, 5)
                if core:
                    copy_out(b, 2, par)
                shared_silu(b, 6)
                if front:
                    for i in (0, 1):
                        need(act, pe_kt, 2 * f + i + 1)
                        need(act, pe_S, NS * (f - 1))
                        a.activation(Kt[:, fp, 2 * i:2 * i + 2], PB[i][:].rearrange("p (c n) -> p c n", c=2),
                                     ACT.Copy).then_inc(a_kt, 1)
                if within(b, 2, B + 1):
                    need(act, v_gap, b - 1)
                    a.activation(tw[:], gapr[:], ACT.Tanh, scale=0.5).then_inc(a_tw, 1)
                shared_silu(b, 7)

            def vp_view(par, c):
                v = VP[:, par, c]
                return bass.AP(tensor=v.tensor, offset=v.offset, ap=[list(v.ap[0]), [128, 4], [40, 4], [1, 8]])
            stage1(act, step)

            def step(e, par):
                def split(k, kp):
                    for i, (t0, n) in enumerate(GROUPS):
                        need(act, e_xT, 3 * k + i + 1)
                        if i == 0:
                            need(act, e_gu, 12 * (k - 1))
                        a.activation(xgT_hi[:, kp, P * t0:P * (t0 + n)], PB[(3 * kp + i) % 2][:, 0:P * n],
                                     ACT.Copy).then_inc(e_hi, 1)

                def group(n):
                    for f in range(4):
                        k = 12 * e + 4 * n + f
                        need(act, e_gt, k + 1)
                        need(act, e_h, k - 1)
                        w = P * GROUPS[n][1]
                        a.activation(sq[:, f % 2, 0:w], EB[f % 2][:, 0:w], ACT.Silu).then_inc(e_silu, 1)

                def rows(n):
                    t0, cnt = GROUPS[n]
                    need(act, e_dn, 3 * e + n + 1)
                    if n == 0:
                        need(act, ye_free, e + 1)
                    a.activation(ye[:, par, t0:t0 + cnt], (OB, SBK)[(n + par) % 2][:, 0:P * cnt].rearrange("p (t d) -> p t d", t=cnt),
                                 ACT.Copy).then_inc(e_y, 1)
                if isinstance(e, int) and e == 0:
                    split(0, 0)
                group(0)
                if within(e, 0, E - 2):
                    split(e + 1, 1 - par)
                group(1)
                rows(0)
                group(2)
                rows(1)
                rows(2)
            stage2(act, step)

        @block.vector
        def _(dve):
            v = nc.vector
            n_c = [0]
            dve.sem_inc(v_pos, 2)
            turns = QM[:, 0, 0]

            def link(ins):
                n_c[0] += 1
                ins.then_inc(c_dve, 1)
                dve.wait_ge(c_dve, n_c[0])
            dve.wait_ge(c_pool, 24)
            link(v.tensor_reduce(pairmask[:, 0:2], bits[:, 0:2, 0:4], AX.X, ALU.add))
            link(v.tensor_reduce(pairmask[:, 2:3], bits[:, 2:3], AX.X, ALU.add))
            link(v.tensor_copy(before[:], before_f[:]))
            link(v.tensor_scalar(phase[:, 0:1], pairmask[:, 2:3], 0.25, None, ALU.mult))
            link(v.tensor_scalar(phase[:, 1:2], pairmask[:, 2:3], 1.5707963267948966, None, ALU.mult))
            dve.wait_ge(ld_w, 9 * 16)
            link(v.tensor_scalar(table[:, 0], pos_n, theta_s[:, 0:1], None, ALU.mult))
            link(v.tensor_scalar(table[:, 1], pos_n, theta_s[:, 1:2], None, ALU.mult))
            link(v.tensor_scalar(turns, table[:], 0.15915494309189535, phase[:, 0:1], ALU.mult, ALU.add))
            link(v.tensor_scalar(turns, turns, MAGIC, None, ALU.add))
            link(v.tensor_scalar(turns, turns, MAGIC, None, ALU.subtract))
            for part in TWO_PI:
                link(v.scalar_tensor_tensor(table[:], turns, -part, table[:], ALU.mult, ALU.add))
            link(v.tensor_scalar(table[:], table[:], phase[:, 1:2], PI_IN, ALU.add, ALU.min))
            link(v.tensor_scalar(table[:], table[:], -PI_IN, None, ALU.max))
            link(v.tensor_copy(wqk_hi[:], sq[:, 0]))
            link(v.tensor_tensor(wqk_lo[:], sq[:, 0], wqk_hi[:].bitcast(f32), ALU.subtract))
            dve.wait_ge(c_g, 1)
            link(v.tensor_copy(sq[:, 1, D:2 * D], PB[0][:, 0:D]))
            link(v.tensor_copy(wvg_hi[:], sq[:, 1, 0:2 * D]))
            link(v.tensor_tensor(wvg_lo[:], sq[:, 1, 0:2 * D], wvg_hi[:].bitcast(f32), ALU.subtract))

            def turn(f, fp, i):
                dst = (QT, KT)[i // 2][:, fp, i % 2]
                need(dve, a_silu, 4 * f + i + 1)
                if i == 0 and isinstance(f, int) and f == 0:
                    dve.wait_ge(c_sin, 1)
                need(dve, pe_av, 4 * (f - 1))
                if i < 2:
                    need(dve, g_qm, 4 * (f - 2) + 2 * (i + 1))
                v.tensor_tensor(dst, sq[:, i % 2], table[:, i % 2], ALU.mult).then_inc(v_qk, 1)

            def mask(b, par, c, i):
                if within(b, 0, B - 1):
                    need(dve, pe_E, 8 * b + 2 * c + i + 1)
                    need(dve, pe_av, 4 * b + c - 1)
                    v.tensor_tensor(EM[:, c % 2, 2 * i:2 * i + 2].rearrange("p q (h n) -> p q h n", h=4),
                                    EB2[:, :, 0:4 * T].rearrange("p q (h n) -> p q h n", h=4),
                                    causal[:].unsqueeze(1).unsqueeze(1).broadcast_to([P, 2, 4, T]), ALU.mult).then_inc(v_mask, 1)
                    k = 2 * c + i
                    if k < NS:
                        need(dve, pe_S, NS * b + k + 1)
                        need(dve, pe_av, 4 * (b - 1) + (k + 1) // 2 + 1)
                        v.tensor_tensor(SM[:, k], SBK[:, 0:128], headmask[:].rearrange("p t n -> p (t n)"),
                                        ALU.mult).then_inc(v_S, 1)

            def shared_hidden(b, f):
                if within(b, 2, B + 1):
                    n = 8 * (b - 2) + f
                    need(dve, a_sf, n + 1)
                    need(dve, pe_up, n + 1)
                    if f == 0:
                        need(dve, pe_dn, b - 2)
                    v.tensor_tensor(hs[:, f], sf[:, f % 2], UB[:], ALU.mult).then_inc(v_h, 1)

            def moments(src, dst, n, s_bn, s_ag, woke):
                for c in range(NC):
                    v.bn_stats(st[:, c], src[:, c]).then_inc(s_bn, 1)
                hold(dve, s_bn, 4 * n + 4, woke)
                for c in range(NC):
                    v.bn_aggr(dst[:, c], st[:, c]).then_inc(s_ag, 1)
                need(dve, s_ag, 4 * n + 4)

            def step(b, par):
                f, fp = b + 1, 1 - par
                front = within(b, -1, 14)
                back, route = within(b, 1, B), within(b, 2, B + 1)
                R = 9 * (b - 2)
                mask(b, par, 0, 0)
                mask(b, par, 0, 1)
                if front:
                    need(dve, a_xhi, f + 1)
                    need(dve, pe_vg, 2 * f)
                    v.tensor_tensor(xlo[:, 0], PB[0][:], xhi[:, 0].bitcast(f32), ALU.subtract).then_inc(v_xlo, 1)
                if route:
                    need(dve, a_x1h, b - 1)
                    v.tensor_tensor(xlo[:, 1], x1T[:], xhi[:, 1].bitcast(f32), ALU.subtract).then_inc(v_x1l, 1)
                if within(b, 3, B + 2):
                    need(dve, pe_dn, b - 2)
                    need(dve, xs_free, b - 2)
                    v.tensor_tensor(xs[:, 1 - par].rearrange("p c d -> p (c d)"), x1[:, 1 - par].rearrange("p c d -> p (c d)"),
                                    UB[:], ALU.add).then_inc(v_xs, 1)
                mask(b, par, 1, 0)
                shared_hidden(b, 0)
                mask(b, par, 1, 1)
                shared_hidden(b, 1)
                if front:
                    turn(f, fp, 0)
                if back:
                    need(dve, pe_wo, b)
                    need(dve, a_th, 2 * b)
                    v.scalar_tensor_tensor(y2[:].rearrange("p c d -> p (c d)"), th[:, 1 - par], 1.0, PB[0][:], ALU.add,
                                           ALU.mult).then_inc(v_y, 1)
                    need(dve, v_y, b)
                    moments(y2, mv, 2 * (b - 1), v_bn, v_ag, v_woke)
                    v.tensor_scalar(ve[:], mv[:, :, 1], 4 * EPS, None, ALU.add).then_inc(v_ve, 1)
                mask(b, par, 2, 0)
                shared_hidden(b, 2)
                mask(b, par, 2, 1)
                shared_hidden(b, 3)
                if route:
                    need(dve, pe_lg, b - 1)
                    v.tensor_copy(lg[:].rearrange("p c e -> p (c e)"), PB[1][:, 0:8 * NC]).then_inc(v_lg, 1)
                if front:
                    turn(f, fp, 1)
                    turn(f, fp, 2)
                    turn(f, fp, 3)
                shared_hidden(b, 4)
                if route:
                    hold(dve, v_lg, b - 1, v_woke)
                    for c in range(NC):
                        v.max(m8[:, c], lg[:, c]).then_inc(v_rt, 1)
                    hold(dve, v_rt, R + 4, v_woke)
                    for c in range(NC):
                        v.max_index(ix8[:, c], m8[:, c], lg[:, c]).then_inc(v_rt, 1)
                    v.tensor_tensor(gap[:], m8[:, :, 0], m8[:, :, 1], ALU.subtract).then_inc(v_rt, 1)
                    need(dve, v_rt, R + 9)
                    v.tensor_tensor(gapr[:], gap[:], rr[:, par, 1], ALU.mult).then_inc(v_gap, 1)
                    v.tensor_copy(ixf[:].rearrange("p k c -> p c k"), ix8[:, :, 0:2]).then_inc(v_M, 1)
                    need(dve, v_M, 6 * (b - 2) + 1)
                    v.tensor_tensor(oh[:], iota8[:], ixf[:].rearrange("p k c -> p (k c)").unsqueeze(2).broadcast_to([P, 2 * NC, 8]),
                                    ALU.is_equal).then_inc(v_M, 1)
                    need(dve, v_M, 6 * (b - 2) + 2)
                    v.tensor_tensor(mb[:], oh[:, 0:NC], oh[:, NC:2 * NC], ALU.add).then_inc(v_M, 1)
                if back:
                    for c in range(NC):
                        v.scalar_tensor_tensor(wv[:, c], y2[:, c], mv[:, c, 0:1], gam[:], ALU.subtract,
                                               ALU.mult).then_inc(v_ln, 1)
                    need(dve, v_ln, 8 * (b - 1) + 4)
                    need(dve, g_xb, b)
                    need(dve, g_r1, b)
                    for c in range(NC):
                        v.scalar_tensor_tensor(s1[:, c], wv[:, c], rs[:, c:c + 1], xb[:, 1 - par, c], ALU.mult,
                                               ALU.add).then_inc(v_ln, 1)
                mask(b, par, 3, 0)
                shared_hidden(b, 5)
                if back:
                    need(dve, v_ln, 8 * b)
                    moments(s1, mv2, 2 * (b - 1) + 1, v_bn, v_ag, v_woke)
                    v.tensor_scalar(vq[:, 0], mv2[:, :, 1], EPS, None, ALU.add).then_inc(v_M2, 1)
                    need(dve, v_M2, 3 * (b - 1) + 1)
                    v.reciprocal(vq[:, 1], vq[:, 0]).then_inc(v_M2, 1)
                    need(dve, v_M2, 3 * (b - 1) + 2)
                    v.tensor_tensor(vq[:, 1], vq[:, 1], mv2[:, :, 1], ALU.mult).then_inc(v_M2, 1)
                    need(dve, v_M2, 3 * (b - 1) + 3)
                    v.tensor_scalar(vq[:, 1], vq[:, 1], EPS_RMS, None, ALU.add).then_inc(v_ve, 1)
                mask(b, par, 3, 1)
                shared_hidden(b, 6)
                if route:
                    need(dve, pe_pos, b - 1)
                    posb = SBK[:, P:P + 8 * NC].rearrange("p (c e) -> p c e", c=NC)
                    v.tensor_scalar(over[:], posb, float(CAP), FAR, ALU.is_ge, ALU.mult).then_inc(v_P, 1)
                    v.tensor_tensor(slotv[:], posb, eoff[:], ALU.add).then_inc(v_pos, 1)
                    v.tensor_reduce(seen_f[:], mb[:].rearrange("p c e -> p e c"), AX.X, ALU.add).then_inc(v_P, 1)
                    need(dve, v_P, 5 * (b - 2) + 2)
                    need(dve, v_pos, b + 1)
                    v.tensor_tensor(slotv[:], slotv[:], over[:], ALU.add).then_inc(v_P, 1)
                    v.tensor_tensor(seen[:], seen[:], seen_f[:], ALU.add).then_inc(v_M, 1)
                    need(dve, v_P, 5 * (b - 2) + 3)
                    for k in (0, 1):
                        v.tensor_tensor(pick[:, NC * k:NC * (k + 1)], oh[:, NC * k:NC * (k + 1)], slotv[:],
                                        ALU.mult).then_inc(v_M, 1)
                    need(dve, v_M, 6 * (b - 2) + 6)
                    v.tensor_reduce(slotf[:], pick[:], AX.X, ALU.add).then_inc(v_P, 1)
                    need(dve, v_P, 5 * (b - 2) + 4)
                    need(dve, rt_free, b - 1)
                    v.tensor_scalar(slot[:, par], slotf[:], float(SLOTS), None, ALU.min).then_inc(v_slot, 1)
                    need(dve, a_tw, b - 1)
                    v.tensor_scalar(wts[:, par, 0:NC], tw[:], 0.5, 0.5, ALU.mult, ALU.add).then_inc(v_P, 1)
                    v.tensor_scalar(wts[:, par, NC:2 * NC], tw[:], -0.5, 0.5, ALU.mult, ALU.add).then_inc(v_wts, 1)
                if back:
                    need(dve, g_r2, b)
                    need(dve, g_sc, P * (b - 1))
                    for c in range(NC):
                        v.tensor_scalar(x1[:, 1 - par, c], s1[:, c], mv2[:, c, 0:1], rr[:, 1 - par, 0, c:c + 1],
                                        ALU.subtract, ALU.mult).then_inc(v_x1, 1)
                shared_hidden(b, 7)
            stage1(dve, step)

            def step(e, par):
                def split(k, kp):
                    for i, (t0, n) in enumerate(GROUPS):
                        need(dve, e_hi, 3 * k + i + 1)
                        if i == 0:
                            need(dve, e_gu, 12 * (k - 1))
                        cols = slice(P * t0, P * (t0 + n))
                        v.tensor_tensor(xgT_lo[:, kp, cols], PB[(3 * kp + i) % 2][:, 0:P * n],
                                        xgT_hi[:, kp, cols].bitcast(f32), ALU.subtract).then_inc(e_lo, 1)

                def group(n):
                    hp = (n + par) % 2
                    for f in range(4):
                        k = 12 * e + 4 * n + f
                        w = P * GROUPS[n][1]
                        need(dve, e_silu, k + 1)
                        need(dve, e_gu, k + 1)
                        if f == 0:
                            need(dve, e_dn, 3 * e + n - 1)
                        v.tensor_tensor(he[:, hp, f, 0:w], sq[:, f % 2, 0:w], EB[2 + f % 2][:, 0:w],
                                        ALU.mult).then_inc(e_h, 1)
                if isinstance(e, int) and e == 0:
                    split(0, 0)
                group(0)
                if within(e, 0, E - 2):
                    split(e + 1, 1 - par)
                group(1)
                group(2)
            stage2(dve, step)

            def step(m, par):
                q = 1 - par
                if within(m, 1, B):
                    need(dve, m_g[q], P // 2 * (m + par))
                    need(dve, m_ld, 48 * m)
                    for c in range(NC):
                        v.scalar_tensor_tensor(wv[:, c], ge[:, q, 0, c], wts3[:, q, c:c + 1], xin[:, q, c], ALU.mult,
                                               ALU.add).then_inc(m_z, 1)
                    need(dve, m_z, 8 * (m - 1) + 4)
                    for c in range(NC):
                        v.scalar_tensor_tensor(y2[:, c], ge[:, q, 1, c], wts3[:, q, NC + c:NC + c + 1], wv[:, c],
                                               ALU.mult, ALU.add).then_inc(m_z, 1)
                    need(dve, m_z, 8 * m)
                    moments(y2, mv, m - 1, m_bn, m_ag, m_woke_v)
                    v.tensor_scalar(ve[:], mv[:, :, 1], EPS, None, ALU.add).then_inc(m_ve, 1)
                    need(dve, m_r, m)
                    need(dve, m_st, 16 * (m - 2))
                    for c in range(NC):
                        v.tensor_scalar(x1[:, q, c], y2[:, c], mv[:, c, 0:1], rs[:, c:c + 1], ALU.subtract,
                                        ALU.mult).then_inc(m_o, 1)
            stage3(dve, step)

        @block.tensor
        def _(pe):
            t = nc.tensor
            pe.wait_ge(ld_w, 9 * 16)
            t.matmul(PB[0][:, 0:D], g1t_s[:], g2_s[:], start=True, stop=True).then_inc(c_g, 1)
            pe.wait_ge(c_pool, 13)

            def three(dst, w_hi, w_lo, x_hi, x_lo):
                t.matmul(dst, w_hi, x_hi, start=True, stop=False)
                t.matmul(dst, w_hi, x_lo, start=False, stop=False)
                return t.matmul(dst, w_lo, x_hi, start=False, stop=True)

            def project(f, i):
                bank = i % 2
                if i == 0:
                    need(pe, a_xhi, f + 1)
                    need(pe, v_xlo, f + 1)
                elif i == 1:
                    need(pe, a_x1T, f - 2)
                elif i == 2:
                    need(pe, a_silu, 4 * f + 1)
                    need(pe, v_y, f - 1)
                else:
                    need(pe, a_silu, 4 * f + 2)
                    need(pe, v_lg, f - 2)
                cols = slice(P * i, P * (i + 1))
                three(PB[bank][:], wqk_hi[:, cols], wqk_lo[:, cols], xhi[:, 0], xlo[:, 0]).then_inc(pe_qk, 1)

            def step(b, par):
                f, fp = b + 1, 1 - par
                front, core = within(b, -1, 14), within(b, 0, B - 1)
                back, route = within(b, 1, B), within(b, 2, B + 1)
                if isinstance(b, int) and b == -1:
                    pe.wait_ge(c_dve, 20)

                def energies(c, i):
                    if c == 0 and i == 0:
                        need(pe, v_qk, 4 * b + 4)
                        need(pe, g_qm, 4 * b + 4)
                    need(pe, v_mask, 8 * b + 2 * c + i)
                    for q in (2 * i, 2 * i + 1):
                        rows = slice(32 * q, 32 * q + 32)
                        for half in (0, 1):
                            for s in (0, 1):
                                tok = slice(P * c + T * s, P * c + T * (s + 1))
                                ins = t.matmul(EB2[T * s:T * (s + 1), q % 2, 2 * T * half:2 * T * (half + 1)],
                                               KT[rows, par, half, tok], QM[rows, par, half, :, tok], start=True, stop=True)
                    ins.then_inc(pe_E, 1)
                    k = 2 * c + i
                    if k == NS:
                        return
                    if k == 0:
                        need(pe, a_kt, 2 * b + 2)
                        need(pe, a_v, 4 * b + 4)
                        need(pe, v_pos, b)
                    need(pe, v_S, NS * b + k)
                    tok = slice(T * i, T * (i + 1))
                    for half in (0, 1):
                        ins = t.matmul(SBK[:, T * half:T * half + T], Kt[tok, par, c, P * half:P * half + P],
                                       v_rows(par, c, half, tok), start=(k == 0 and half == 0), stop=True,
                                       skip_group_check=True)
                    ins.then_inc(pe_S, 1)

                def attend(b, par, c, s):
                    if s == 0:
                        need(pe, a_out, 4 * b + c)
                        need(pe, v_S, NS * b + 2 * c)
                        hold(pe, v_mask, 8 * b + 2 * c + 2, pe_woke)
                    else:
                        need(pe, v_S, NS * b + 2 * c + 1)
                        hold(pe, pe_av0, 4 * b + c + 1, pe_woke)
                    tok = slice(P * c + T * s, P * c + T * (s + 1))
                    keys = slice(T * s, T * (s + 1))
                    k = 2 * c + s
                    for half in (0, 1):
                        if k > 0:
                            t.matmul(OB[T * half:T * half + T, tok], SM[:, k - 1, T * half:T * half + T],
                                     QT[:, par, half, tok], start=True, stop=False)
                    for i in range(4):
                        for j in range(4):
                            h = 4 * j + i
                            half, q, pair = h // 8, (h % 8) // 2, h % 2
                            e0 = 2 * T * half + T * pair
                            ins = t.matmul(OB[32 * j:32 * j + 32, tok], VP[keys, par, c, 32 * h:32 * h + 32],
                                           EM[keys, c % 2, q, e0:e0 + T], start=(k == 0 and i == 0), stop=(i == 3))
                    ins.then_inc((pe_av0, pe_av)[s], 1)

                def shared_pair(f):
                    if not route:
                        return
                    n = 8 * (b - 2) + f
                    ff = slice(P * f, P * (f + 1))
                    if f == 0:
                        need(pe, a_x1h, b - 1)
                        need(pe, v_x1l, b - 1)
                        if isinstance(b, int):
                            need(pe, s_w, 4)
                    need(pe, a_sf, n)
                    three(GB[:], ws_hi[:, 0, ff], ws_lo[:, 0, ff], xhi[:, 1], xlo[:, 1]).then_inc(pe_gt, 1)
                    need(pe, v_h, n)
                    if f == 0:
                        need(pe, v_xs, b - 2)
                    three(UB[:], ws_hi[:, 1, ff], ws_lo[:, 1, ff], xhi[:, 1], xlo[:, 1]).then_inc(pe_up, 1)

                def shared_down(cs):
                    if not within(b, 3, B + 2):
                        return
                    need(pe, v_h, 8 * (b - 2))
                    for c in cs:
                        for f in range(8):
                            ins = t.matmul(UB[:, P * c:P * (c + 1)], hs[:, f, P * c:P * (c + 1)], sd_s[:, f],
                                           start=(f == 0), stop=(f == 7))
                    if NC - 1 in cs:
                        ins.then_inc(pe_dn, 1)

                def part(c, s):
                    if core:
                        energies(c, s)
                    if c > 0 and core:
                        attend(b, par, c - 1, s)
                    elif c == 0 and back:
                        attend(b - 1, 1 - par, 3, s)

                part(0, 0)
                shared_down((0, 1))
                part(0, 1)
                if front:
                    need(pe, ld_x, 16 * (f + 1))
                    need(pe, a_kt, 2 * f)
                    for c in range(NC):
                        ins = t.transpose(PB[0][:, P * c:P * (c + 1)], xin[:, fp, c], ident[:])
                    ins.then_inc(pe_xT, 1)
                if route:
                    need(pe, v_x1, 4 * (b - 1))
                    need(pe, a_kt, 2 * last(b) + 2)
                    if isinstance(b, int):
                        need(pe, v_lg, b - 2)
                    for c in range(NC):
                        ins = t.transpose(PB[1][:, P * c:P * (c + 1)], x1[:, par, c], ident[:])
                    ins.then_inc(pe_x1T, 1)
                shared_down((2, 3))
                if front:
                    project(f, 0)
                part(1, 0)
                shared_pair(0)
                part(1, 1)
                shared_pair(1)
                if front:
                    project(f, 1)
                if back:
                    need(pe, a_out, 4 * b)
                    need(pe, a_silu, 4 * last(b + 1) + 1)
                    if isinstance(b, int):
                        need(pe, v_y, b - 1)
                    for c in range(NC):
                        ins = t.matmul(PB[0][:, P * c:P * (c + 1)], oT[:, 1 - par, P * c:P * (c + 1)], wo_s[:],
                                       start=True, stop=True)
                    ins.then_inc(pe_wo, 1)
                if route:
                    need(pe, a_x1T, b - 1)
                    need(pe, a_silu, 4 * last(b + 1) + 2)
                    for c in range(NC):
                        ins = t.matmul(PB[1][:, 8 * c:8 * c + 8], x1T[:, P * c:P * (c + 1)], rwt_s[:], start=True, stop=True)
                    ins.then_inc(pe_lg, 1)
                part(2, 0)
                shared_pair(2)
                part(2, 1)
                shared_pair(3)
                if front:
                    project(f, 2)
                    project(f, 3)
                shared_pair(4)
                if front:
                    for i in (0, 1):
                        need(pe, a_silu, 4 * f + 3 + i)
                        for c in (0, 1):
                            tok = slice(P * (2 * i + c), P * (2 * i + c + 1))
                            ins = three_r(PB[i][:, 256 * c:256 * c + 256], tok)
                        ins.then_inc(pe_vg, 1)
                part(3, 0)
                shared_pair(5)
                part(3, 1)
                shared_pair(6)
                if front:
                    need(pe, v_qk, 4 * f + 4)
                    for i in (0, 1):
                        need(pe, a_v, 4 * f + 2 * i + 2)
                        need(pe, a_th, 2 * f + i + 1)
                        for c in (0, 1):
                            for half in (0, 1):
                                ins = t.transpose(PB[i][:, 256 * c + P * half:256 * c + P * half + P],
                                                  KT[:, fp, half, P * (2 * i + c):P * (2 * i + c + 1)], ident[:])
                        ins.then_inc(pe_kt, 1)
                if route:
                    need(pe, v_M, 6 * (b - 2) + 3)
                    need(pe, v_S, NS * (last(b) + 1))
                    o = SBK[:, P:P + 8 * NC]
                    t.matmul(o.rearrange("p (c e) -> p c e", c=NC), ones[:], seen[:].unsqueeze(1).broadcast_to([P, NC, 8]),
                             start=True, stop=False)
                    mf = mb[:].rearrange("p c e -> p (c e)")
                    for k in (1, 2, 3):
                        t.matmul(o[:, 8 * k:8 * NC], ones[:], mf[:, 0:8 * (NC - k)], start=False, stop=False,
                                 skip_group_check=True)
                    t.matmul(o, before[:], mf, start=False, stop=True).then_inc(pe_pos, 1)
                shared_pair(7)

            def three_r(dst, tok):
                t.matmul(dst, xhi[:, 0, tok], wvg_hi[:], start=True, stop=False)
                t.matmul(dst, xhi[:, 0, tok], wvg_lo[:], start=False, stop=False)
                return t.matmul(dst, xlo[:, 0, tok], wvg_hi[:], start=False, stop=True)

            def v_rows(par, c, half, tok):
                v = VP[tok, par, c]
                return bass.AP(tensor=v.tensor, offset=v.offset + 256 * half, ap=[list(v.ap[0]), [128, 2], [40, 4], [1, 8]])
            stage1(pe, step)
            pe.wait_ge(v_xs, B)

            def step(e, par):
                def turn_rows(k, kp):
                    need(pe, e_ldx, 16 * (k + 1))
                    for i, (t0, n) in enumerate(GROUPS):
                        bank = (3 * kp + i) % 2
                        need(pe, e_lo, 3 * k + i - 1)
                        for c in range(n):
                            ins = t.transpose(PB[bank][:, P * c:P * (c + 1)], xg[:, kp, t0 + c], ident[:])
                        ins.then_inc(e_xT, 1)

                def gate_up(n):
                    cols = slice(P * GROUPS[n][0], P * (GROUPS[n][0] + GROUPS[n][1]))
                    w = P * GROUPS[n][1]
                    need(pe, e_lo, 3 * e + n + 1)
                    need(pe, e_hi, 3 * e + n + 1)
                    need(pe, e_w, 4 * e + 4)
                    for f in range(4):
                        need(pe, e_h, 12 * e + 4 * n + f - 1)
                        ff = slice(P * f, P * (f + 1))
                        for gu in (0, 1):
                            three(EB[2 * gu + f % 2][:, 0:w], we_hi[:, par, gu, ff], we_lo[:, par, gu, ff],
                                  xgT_hi[:, par, cols], xgT_lo[:, par, cols]).then_inc((e_gt, e_gu)[gu], 1)

                def down(n):
                    hp = (n + par) % 2
                    need(pe, e_h, 12 * e + 4 * n + 4)
                    need(pe, e_y, 3 * e + n - 1)
                    for c in range(GROUPS[n][1]):
                        for f in range(4):
                            ins = t.matmul((OB, SBK)[hp][:, P * c:P * (c + 1)], he[:, hp, f, P * c:P * (c + 1)],
                                           wd[:, par, f], start=(f == 0), stop=(f == 3))
                    ins.then_inc(e_dn, 1)
                if isinstance(e, int) and e == 0:
                    turn_rows(0, 0)
                gate_up(0)
                if within(e, 0, E - 2):
                    turn_rows(e + 1, 1 - par)
                gate_up(1)
                down(0)
                gate_up(2)
                down(1)
                down(2)
            stage2(pe, step)


def kernel(**inputs):
    import numpy as _np
    import concourse.bacc as _bacc
    from concourse import mybir as _mybir
    from concourse.bass_utils import run_bass_kernel_spmd as _run

    d = {k.split("_", 2)[2]: _np.ascontiguousarray(_np.asarray(v)) for k, v in inputs.items() if k != "L0_attn_x"}
    x = _np.ascontiguousarray(_np.asarray(inputs["L0_attn_x"]))
    def doubled(w):
        w = w.reshape(D, 2, H // 2, 1, HD)
        return _np.broadcast_to(w, (D, 2, H // 2, 2, HD)).reshape(D, 2 * P)
    theta = _np.broadcast_to(d["theta"].reshape(2, H // 2, 1, HD), (2, H // 2, 2, HD)).reshape(2, P).T
    arrays = {
        "x": x, "wqk": _np.concatenate([doubled(d["Wq"]), doubled(d["Wk"])], axis=1), "wv": d["Wv"],
        "g1t": d["G1"].T, "g2": d["G2"], "wo": d["Wo"], "gamma": d["gamma"], "beta": d["beta"], "theta": theta,
        "rwt": d["router_w"].T, "rg": d["rg"], "ru": d["ru"], "rd": d["rd"], "sg": d["sg"], "su": d["su"], "sd": d["sd"],
    }
    arrays = {f"in_{k}": _np.ascontiguousarray(v) for k, v in arrays.items()}
    nc = _bacc.Bacc("TRN2", target_bir_lowering=False, num_devices=1)
    args = [nc.dram_tensor(k, v.shape, _mybir.dt.from_np(v.dtype), kind="ExternalInput").ap() for k, v in arrays.items()]
    args.append(nc.dram_tensor("out_x", (B, S, D), _mybir.dt.float32, kind="ExternalOutput").ap())
    build(nc, *args)
    r = _run(nc, [arrays], core_ids=[0])
    return r.results[0]["out_x"]
```

```python
import concourse.bass as bass
from concourse import mybir
from contextlib import ExitStack

f32 = mybir.dt.float32
f32r = mybir.dt.float32r
bf16 = mybir.dt.bfloat16
i32 = mybir.dt.int32
u32 = mybir.dt.uint32
ALU = mybir.AluOpType
ACT = mybir.ActivationFunctionType
AX = mybir.AxisListType

P = 128
D = 128
B, S = 16, 512
NC = S // P
T = 64
NS = S // T - 1
H, HD = 16, 8
E, FR, FS = 8, 512, 1024
CAP = int(1.25 * B * S / E)
SLOTS = E * CAP
RW = D + 2
NT = B * S
NOWHERE = 4.0 * NT
CT = CAP // P
LATE = 5
FIRST_LATE = B - 1 - LATE
EARLY = B - LATE
GROUPS = [(0, 4), (4, 4), (8, 2)]
EPS = 1e-5
EPS_RMS = 2.0 ** -23
FAR = 16384.0
TWO_PI = [6.28125, 0.0019350051879882812, 3.01991598e-07]
MAGIC = 12582912.0
PI_IN = 3.1415925


def build(nc, x, wqk, wvg, g1t, g2, wo, gamma, beta, theta, rwt, rg, ru, rd, sg, su, sd, out):
    x_v = x.rearrange("b (c p) d -> b p c d", p=P)
    out_v = out.rearrange("b (c p) d -> b p c d", p=P)
    ctx = ExitStack()
    with ctx:
        def sb(name, shape, dt=f32):
            return ctx.enter_context(nc.sbuf_tensor(name, shape, dt))

        def sem(name):
            return ctx.enter_context(nc.semaphore(name))

        xg_d = nc.dram_tensor("dispatched_rows", [SLOTS, RW], f32, kind="Internal").ap()
        yd_d = nc.dram_tensor("expert_rows", [2 * NT, D], f32, kind="Internal").ap()
        x1_d = nc.dram_tensor("x1_rows", [B, P, NC * D], f32, kind="Internal").ap()
        weight_d = nc.dram_tensor("weights", [B, P, 2 * NC], f32, kind="Internal").ap()

        ident = sb("ident", [P, P])
        causal = sb("causal", [P, T])
        before = sb("before", [P, P], bf16)
        ones = sb("ones", [P, P], bf16)
        headmask = sb("headmask", [P, 2, 64])
        bits = sb("bits", [P, 8])
        cosine = sb("cosine", [P, 1])
        iota8 = sb("iota8", [P, 2 * NC, 8])
        eoff = sb("eoff", [P, NC, 8])
        minus_half = sb("minus_half", [P, 8])
        gam = sb("gam", [P, D])
        bet = sb("bet", [P, D])
        empty = sb("empty", [P, CT * RW])
        zeros = sb("zeros", [P, D])
        theta_s = sb("theta_s", [P, 2])
        phase = sb("phase", [P, 2])
        table = sb("table", [P, 2, S])
        rwt_s = sb("rwt_s", [P, E])
        wo_s = sb("wo_s", [P, D])
        xgT_hi = sb("xgT_hi", [P, 2, CAP], f32r)
        xgT_lo = sb("xgT_lo", [P, 2, CAP], f32r)
        we_hi = sb("we_hi", [P, 2, 2, FR], f32r)
        we_lo = sb("we_lo", [P, 2, 2, FR], f32r)
        wqk_hi, wqk_lo = we_hi[:, 1, 0], we_lo[:, 1, 0]
        wvg_hi, wvg_lo = we_hi[:, 1, 1, 0:2 * D], we_lo[:, 1, 1, 0:2 * D]
        warm = sb("warm", [P, 1])

        xin = sb("xin", [P, 2, NC, D])
        xb = sb("xb", [P, 2, NC, D])
        xhi = xgT_hi[:, 1, 0:2 * S].rearrange("p (i n) -> p i n", i=2)
        xlo = xgT_lo[:, 1, 0:2 * S].rearrange("p (i n) -> p i n", i=2)
        sq = sb("sq", [P, 2, S])
        QT = sb("QT", [P, 2, 2, 2, 2 * P])
        KT = sb("KT", [P, 2, 2, S])
        QM = sb("QM", [P, 2, 2, 2, 8, P])
        Kt = sb("Kt", [P, 2, NC, 256])
        VP = sb("VP", [P, 2, NC, 512])
        EM = sb("EM", [P, 2, 2, 8, T])
        SM = sb("SM", [P, NS, 128])
        oT = sb("oT", [P, 2, S])
        th = sb("th", [P, 2, S])
        y2 = sb("y2", [P, NC, D])
        pos_n = y2[:].rearrange("p c d -> p (c d)")
        wv = sb("wv", [P, NC, D])
        s1 = sb("s1", [P, NC, D])
        before_f, g1t_s, g2_s = wv[:, 0], s1[0:8, 0], s1[0:8, 1]
        x1 = sb("x1", [P, 2, NC, RW])
        x1T = sb("x1T", [P, S])
        st = sb("st", [P, NC, 6])
        mv = sb("mv", [P, NC, 2])
        mv2 = sb("mv2", [P, NC, 2])
        ve = sb("ve", [P, NC])
        rs = sb("rs", [P, NC])
        vq = sb("vq", [P, 2, NC])
        rr = sb("rr", [P, 2, 2, NC])
        lg = sb("lg", [P, NC, 8])
        m8 = sb("m8", [P, NC, 8])
        ix8 = sb("ix8", [P, NC, 8], u32)
        ixf = sb("ixf", [P, 2, NC])
        oh = sb("oh", [P, 2 * NC, 8])
        mb = sb("mb", [P, NC, 8], bf16)
        seen = sb("seen", [P, 8], bf16)
        seen_f = sb("seen_f", [P, 8])
        over = sb("over", [P, NC, 8])
        slotv = sb("slotv", [P, NC, 8])
        pick = sb("pick", [P, 2 * NC, 8])
        slotf = sb("slotf", [P, 2 * NC])
        gap = sb("gap", [P, NC])
        gapr = sb("gapr", [P, NC])
        tw = sb("tw", [P, NC])
        slot = sb("slot", [P, 2, 2 * NC], i32)
        wts = sb("wts", [P, 2, 2 * NC])

        ws_hi = sb("ws_hi", [P, 2, FS], f32r)
        ws_lo = sb("ws_lo", [P, 2, FS], f32r)
        sd_s = sb("sd_s", [P, FS // P, D])
        sf = sb("sf", [P, 2, S])
        xs = empty[:, 0:2 * S].rearrange("p (i c d) -> p i c d", i=2, c=NC)

        def flat(t):
            axes = "abcde"[:len(t.shape) - 1]
            return t[:].rearrange(f"p {' '.join(axes)} -> p ({' '.join(axes)})")
        xg = flat(QM)[:, 0:2 * CT * RW].rearrange("p (e j d) -> p e j d", e=2, j=CT)
        ye = flat(VP)[:, 0:2 * CT * D].rearrange("p (e j d) -> p e j d", e=2, j=CT)
        wraw = flat(QT).rearrange("p (e g n) -> p e g n", e=2, g=2)
        wd = flat(KT)[:, 0:2 * FR].rearrange("p (e f d) -> p e f d", e=2, f=FR // P)
        he = sb("he", [P, 2, FR // P, S])
        sraw = [flat(he)[:, 0:FS], flat(he)[:, FS:2 * FS]]
        hs = flat(he).rearrange("p (f n) -> p f n", n=S)
        ge = flat(QM)[:, 0:24 * P].rearrange("p (m k c d) -> p m k c d", m=3, k=2, c=NC)
        xc = flat(QM)[:, 24 * P:36 * P].rearrange("p (m c d) -> p m c d", m=3, c=NC)
        xo = flat(QM)[:, 36 * P:48 * P].rearrange("p (m c d) -> p m c d", m=3, c=NC)
        x1t = flat(QM)[:, 48 * P:52 * P].rearrange("p (c d) -> p c d", c=NC)
        y3 = [y2] + [flat(QM)[:, P * i:P * (i + 4)].rearrange("p (c d) -> p c d", c=NC) for i in (56, 60)]
        x1a = flat(QM)[:, 52 * P:56 * P].rearrange("p (c d) -> p c d", c=NC)
        expert = sb("expert", [P, 1])
        second = sb("second", [P, CT])
        goal = sb("goal", [P, CT])
        goal_i = sb("goal_i", [P, 2, CT], i32)
        w3 = [wv[:], s1[:], th[:, 0].rearrange("p (c d) -> p c d", c=NC)]
        mv3 = sb("mv3", [P, 3, NC, 2])
        minus_mean = sb("minus_mean", [P, 3, NC])
        rs3 = sb("rs3", [P, 3, NC])
        shift = sb("shift", [P, 3, NC])
        wts3 = sb("wts3", [P, 3, 2 * NC])

        EB2 = ctx.enter_context(nc.psum_tensor("energy_banks", [P, 2, 512], f32))
        banks = [ctx.enter_context(nc.psum_tensor(f"bank{i}", [P, 512], f32)) for i in range(6)]
        PB, OB, SBK, GB, UB = banks[0:2], banks[2], banks[3], banks[4], banks[5]
        EB = [EB2[:, 0], EB2[:, 1], GB, UB]

        ld_w = sem("weights_loaded"); ld_x = sem("x_loaded"); c_pool = sem("pool_constants"); c_id = sem("identity")
        c_dve = sem("dve_constants"); c_sin = sem("table_ready"); c_g = sem("g1g2_product"); c_warm = sem("act_table_warm")
        pe_xT = sem("x_transposed")
        pe_qk = sem("qk_projected")
        pe_vg = sem("vg_projected")
        pe_kt = sem("k_by_token")
        pe_E = sem("energies")
        pe_S = sem("state_summed")
        pe_av0 = sem("first_block_out")
        pe_av = sem("attention_out")
        pe_wo = sem("wo_projected")
        pe_x1T = sem("x1_transposed")
        pe_lg = sem("logits")
        pe_gt = sem("shared_gate")
        pe_up = sem("shared_up")
        pe_dn = sem("shared_down")
        a_x1h = sem("x1hi_ready"); v_x1l = sem("x1lo_ready"); a_sf = sem("shared_silu"); v_h = sem("shared_hidden"); v_xs = sem("shared_added")
        pe_woke = sem("tensor_woke"); pe_pos = sem("positions")
        a_xhi = sem("xhi_ready"); a_silu = sem("silu_ready"); a_v = sem("v_ready"); a_th = sem("gate_ready")
        a_kt = sem("kt_ready"); a_out = sem("out_copied"); a_x1T = sem("x1T_ready"); a_tw = sem("route_tanh")
        v_xlo = sem("xlo_ready"); v_qk = sem("qk_turned"); v_mask = sem("energies_masked"); v_S = sem("state_masked")
        v_y = sem("gated"); v_bn = sem("stats"); v_ag = sem("moments"); v_ve = sem("variance_eps"); v_ln = sem("ln_steps")
        v_x1 = sem("x1_ready"); v_lg = sem("logits_copied"); v_rt = sem("route_steps"); v_M = sem("choices_ready")
        v_gap = sem("gap_ready"); v_slot = sem("slots_ready"); v_pos = sem("positions_read"); v_wts = sem("weights_ready"); v_woke = sem("vector_woke")
        v_e0 = sem("first_expert_noted"); v_tok = sem("tokens_noted")
        v_M2 = sem("mean_square_steps"); v_P = sem("slot_steps")
        g_xb = sem("x_beta"); g_r1 = sem("rstd1"); g_r2 = sem("rstd2"); g_woke = sem("gpsimd_woke")
        g_sc = sem("rows_dispatched")
        g_qm = (sem("q_by_head_first"), sem("q_by_head_second"))
        sp_x1 = sem("sums_stored"); sp_rt = sem("route_stored"); xs_free = sem("sums_kept"); rt_free = sem("route_kept"); sp_woke = sem("sync_woke")
        e_ld = sem("expert_weights_loaded"); e_ldx = sem("expert_rows_loaded"); e_xT = sem("e_transposed"); e_gt = sem("e_gate"); e_gu = sem("e_up"); e_dn = sem("e_down")
        e_hi = sem("e_xhi"); e_lo = sem("e_xlo"); e_silu = sem("e_silu"); e_h = sem("e_hidden"); e_y = sem("e_copied")
        e_w = sem("e_weights_split"); s_ld = sem("shared_loaded"); s_w = sem("shared_split")
        y_fill = sem("expert_rows_cleared"); e_ix = sem("e_goal_steps"); e_goal = sem("e_goals")
        e_sc = (sem("e_scattered_even"), sem("e_scattered_odd"))
        m_ld = [sem(f"m_loaded{i}") for i in range(3)]; m_st = [sem(f"m_stored{i}") for i in range(3)]
        m_x1 = sem("m_x1_loaded"); m_x1a = sem("m_x1_to_add_loaded"); m_x1T = sem("m_x1_transposed"); m_a = sem("m_x1T_ready")
        m_z = sem("m_sums"); m_s = sem("m_shift"); m_w1 = sem("m_weighted"); m_w = sem("m_first_sums"); sp_x1b = sem("x1_stored")
        m_bn = sem("m_stats"); m_ag = sem("m_moments"); m_ve = sem("m_variance_eps"); m_r = sem("m_rstd"); m_o = sem("m_normed")
        m_woke_v = sem("m_vector_woke"); m_woke_g = sem("m_gpsimd_woke")

        def need(eng, s, value):
            if not isinstance(value, int) or value > 0:
                eng.wait_ge(s, value)

        def hold(eng, s, value, woke):
            if not isinstance(value, int) or value > 0:
                eng.wait_ge(s, value)
                eng.sem_inc(woke, 1)

        def last(n):
            return min(n, B - 1) if isinstance(n, int) else n

        def within(b, lo, hi):
            return not isinstance(b, int) or lo <= b <= hi

        def stage1(eng, step):
            for b in (-1, 0, 1, 2):
                step(b, b % 2)
            with eng.Fori(1, 5) as i:
                for k in (1, 2):
                    step(i * 2 + k, k % 2)
            for b in range(11, B + 2):
                step(b, b % 2)

        def shared_turn(b):
            if not isinstance(b, int) or 2 <= b < FIRST_LATE + 2:
                return b - 2
            return None

        TILES_B, TILES_B1, TILES_END = (0, 1), (2, 3), (4, 5, 6, 7)

        def no_ffn(b):
            return isinstance(b, int) and FIRST_LATE + 2 <= b < B

        def position_bank(b):
            if no_ffn(b):
                return GB[:, 0:8 * NC]
            return SBK[:, P:P + 8 * NC]

        def stage2(eng, step):
            for e in (0, 1):
                step(e, e)
            with eng.Fori(1, 3) as i:
                for k in (0, 1):
                    step(i * 2 + k, k)
            for e in (6, 7):
                step(e, e % 2)

        def stage3(eng, group):
            group(0)
            with eng.Fori(1, 3) as g:
                group(g)
            for g in (3, 4, 5):
                group(g)

        def sums_of(g):
            return {0: (0, 1), 5: (-1, 0)}.get(g, (-1, 0, 1)) if isinstance(g, int) else (-1, 0, 1)

        block = ctx.enter_context(nc.Block())

        @block.sync
        def _(sp):
            sp.dma_start(xin[:, 0], x_v[0]).then_inc(ld_x, 16)
            for dst, src in [(sq[:, 0], wqk), (sq[:, 1, 0:D], wvg), (g1t_s, g1t), (g2_s, g2), (wo_s[:], wo),
                             (theta_s[:], theta), (rwt_s[:], rwt),
                             (gam[:], gamma.rearrange("(o d) -> o d", o=1).broadcast_to([P, D])),
                             (bet[:], beta.rearrange("(o d) -> o d", o=1).broadcast_to([P, D]))]:
                sp.dma_start(dst, src).then_inc(ld_w, 16)
            sp.wait_ge(ld_x, 16)
            sp.dma_start(xin[:, 1], x_v[1]).then_inc(ld_x, 16)
            sp.dma_start(sraw[0], sg).then_inc(s_ld, 16)
            sp.dma_start(sraw[1], su).then_inc(s_ld, 16)
            sp.dma_start(sd_s[:], sd.rearrange("(f p) d -> p f d", p=P)).then_inc(s_ld, 16)
            sp.wait_ge(c_pool, 1)
            sp.sem_inc(xs_free, 2)
            sp.sem_inc(rt_free, 2)

            def load_weights(e, par):
                sp.dma_start(wraw[:, par, 0], rg[e]).then_inc(e_ld, 16)
                sp.dma_start(wraw[:, par, 1], ru[e]).then_inc(e_ld, 16)
                sp.dma_start(wd[:, par], rd[e].rearrange("(f p) d -> p f d", p=P)).then_inc(e_ld, 16)

            def load_rows(e, par):
                sp.dma_start(xg[:, par], xg_r[e]).then_inc(e_ldx, 16)

            xg_r = xg_d.rearrange("(e p j) d -> e p j d", e=E, p=P)
            fill_r = yd_d.rearrange("(b p j) d -> b p j d", b=B, p=P)

            def step(b, par):
                if within(b, 0, B - 1):
                    sp.dma_start(fill_r[b], zeros[:].unsqueeze(1).broadcast_to([P, 2 * NT // (B * P), D])).then_inc(y_fill, 16)
                if within(b, 0, 13):
                    hold(sp, ld_x, 16 * (b + 2), sp_woke)
                    hold(sp, pe_xT, b + 1, sp_woke)
                    hold(sp, g_xb, b + 1, sp_woke)
                    sp.dma_start(xin[:, par], x_v[b + 2]).then_inc(ld_x, 16)
                if isinstance(b, int) and (FIRST_LATE + 2 <= b < B or b == B + 1):
                    hold(sp, v_x1, 4 * (b - 1), sp_woke)
                    sp.dma_start(x1_d[b - 2].rearrange("p (c d) -> p c d", c=NC), x1[:, par, :, 0:D]).then_inc(sp_x1b, 16)
                    hold(sp, sp_x1b, 16 * min(b - 2 - FIRST_LATE + 1, LATE), sp_woke)
                def keep_sum(q):
                    hold(sp, v_xs, q + 1, sp_woke)
                    sp.dma_start(x1_d[b - 3], xs[:, 1 - par].rearrange("p c d -> p (c d)")).then_inc(sp_x1, 16)
                    hold(sp, sp_x1, 16 * (q + 1), sp_woke)
                    sp.sem_inc(xs_free, 1)
                if shared_turn(b - 1) is not None:
                    keep_sum(shared_turn(b - 1))
                if within(b, -1, 14):
                    if isinstance(b, int) and b == -1:
                        sp.wait_ge(c_pool, 22)
                    hold(sp, v_qk, 4 * b + 6, sp_woke)
                    for g2 in (0, 1):
                        hold(sp, pe_E, 8 * b + 4 * g2 + 4, sp_woke)
                        for h in range(8):
                            rows = slice(16 * h, 16 * h + 16)
                            sp.dma_start(QM[rows, g2, :, :, h].rearrange("p t c n -> p (t c) n"),
                                         QT[rows, 1 - par, g2].rearrange("p t (c n) -> p (t c) n", c=2)).then_inc(g_qm[g2], 16)
                if isinstance(b, int) and b == B:
                    sp.wait_ge(pe_av, 4 * B)
                    load_weights(0, 0)
                if isinstance(b, int) and b == B + 1:
                    sp.wait_ge(g_sc, P * (B + 1))
                    load_rows(0, 0)
                if within(b, 2, B + 1):
                    hold(sp, v_wts, b - 1, sp_woke)
                    sp.dma_start(weight_d[b - 2], wts[:, par]).then_inc(sp_rt, 16)
                    hold(sp, sp_rt, 16 * (b - 1), sp_woke)
                    sp.sem_inc(rt_free, 1)
                if isinstance(b, int) and b == B + 1:
                    keep_sum(EARLY - 1)
            stage1(sp, step)

            sp.wait_ge(e_ldx, 16)
            load_rows(1, 1)

            def step(e, par):
                if within(e, 0, E - 2):
                    hold(sp, e_ld, 48 * (e + 1), sp_woke)
                    hold(sp, e_w, 4 * e, sp_woke)
                    hold(sp, e_dn, 3 * e, sp_woke)
                    load_weights(e + 1, 1 - par)
                if within(e, 0, E - 3):
                    hold(sp, e_ldx, 16 * (e + 2), sp_woke)
                    hold(sp, e_xT, 3 * (e + 1), sp_woke)
                    hold(sp, e_goal, e + 1, sp_woke)
                    load_rows(e + 2, par)
            stage2(sp, step)

            ge_r = yd_d.rearrange("(m p c) d -> m p (c d)", p=P, c=NC)

            def load_batch(m, i):
                if not isinstance(m, int) or m != B - 1:
                    sp.dma_start(xc[:, i].rearrange("p c d -> p (c d)"), x1_d[m]).then_inc(m_ld[i], 16)
                for k in (0, 1):
                    sp.dma_start(ge[:, i, k].rearrange("p c d -> p (c d)"), ge_r[m + k * B]).then_inc(m_ld[i], 16)
                sp.dma_start(wts3[:, i], weight_d[m]).then_inc(m_ld[i], 16)

            def load_x1(dst, r, s):
                sp.dma_start(dst.rearrange("p c d -> p (c d)"), x1_d[r]).then_inc(s, 16)
            sp.wait_ge(e_goal, E)
            sp.wait_ge(e_xT, 3 * E)
            load_x1(x1t, FIRST_LATE, m_x1)
            load_x1(x1a, FIRST_LATE, m_x1a)
            sp.wait_ge(m_x1T, 1)
            load_x1(x1t, FIRST_LATE + 1, m_x1)
            sp.wait_ge(e_sc[0], 16 * CT * E // 2)
            sp.wait_ge(e_sc[1], 16 * CT * E // 2)
            for i in range(3):
                sp.sem_inc(m_st[i], 16)
            load_batch(B - 2, 0)
            load_batch(0, 1)

            def group(g):
                q = EARLY + g

                def late(i):
                    return B - 1 if isinstance(i, int) and i == LATE - 1 else FIRST_LATE + i
                if within(g, 1, LATE - 2):
                    hold(sp, m_x1T, g + 1, sp_woke)
                    load_x1(x1t, late(g + 1), m_x1)
                for j in range(3 if within(g, 0, 4) else 2):
                    n = 3 * g + j
                    def load_next():
                        if within(n, 0, B - 3):
                            hold(sp, m_z, 4 * n, sp_woke)
                            load_batch(n + 1 if not isinstance(n, int) or n < B - 3 else B - 1, (j + 2) % 3)
                    if not isinstance(g, int) or g < 4 or j > 0:
                        load_next()
                    if j == 0 and within(g, 1, 4):
                        hold(sp, v_xs, q, sp_woke)
                        sp.dma_start(x1_d[late(g - 1)], xs[:, 0].rearrange("p c d -> p (c d)")).then_inc(sp_x1, 16)
                        load_x1(x1a, late(g), m_x1a)
                        hold(sp, sp_x1, 16 * q, sp_woke)
                    if isinstance(g, int) and g == 4 and j == 0:
                        load_next()
                    if within(n, 1, B):
                        hold(sp, m_o, 4 * n + 4, sp_woke)
                        m = n - 2 if not isinstance(n, int) or 1 < n < B else {1: B - 2, B: B - 1}[n]
                        sp.dma_start(out_v[m], xo[:, (j + 2) % 3]).then_inc(m_st[(j + 2) % 3], 16)
            stage3(sp, group)
            for i, n in enumerate((6, 5, 5)):
                sp.wait_ge(m_st[i], 16 * (n + 1))

        @block.gpsimd
        def _(gp):
            g = nc.gpsimd
            g.memset(ident[:], 0.0).then_inc(c_id, 1)
            gp.wait_ge(c_id, 1)
            g.affine_select(out=ident[:], in_=ident[:], compare_op=ALU.not_equal, fill=1.0, base=0,
                            pattern=[[-1, P]], channel_multiplier=1).then_inc(c_id, 1)
            g.memset(zeros[:], 0.0).then_inc(c_pool, 1)
            g.memset(causal[:], 1.0).then_inc(c_pool, 1)
            g.memset(before_f, 1.0).then_inc(c_pool, 1)
            g.memset(ones[:], 1.0).then_inc(c_pool, 1)
            g.memset(headmask[:], 1.0).then_inc(c_pool, 1)
            g.memset(bits[:], 1.0).then_inc(c_pool, 1)
            g.memset(minus_half[:], -0.5).then_inc(c_pool, 1)
            g.memset(seen[:], 0.0).then_inc(c_pool, 1)
            g.iota(iota8[:], [[0, 2 * NC], [1, 8]], base=0, channel_multiplier=0,
                   allow_small_or_imprecise_dtypes=True).then_inc(c_pool, 1)
            g.iota(eoff[:], [[0, NC], [CAP, 8]], base=0, channel_multiplier=0,
                   allow_small_or_imprecise_dtypes=True).then_inc(c_pool, 1)
            g.iota(pos_n, [[1, S]], base=0, channel_multiplier=0,
                   allow_small_or_imprecise_dtypes=True).then_inc(c_pool, 1)
            gp.wait_ge(c_pool, 11)
            for n, rows in ((11, slice(0, T)), (12, slice(T, P))):
                gp.wait_ge(c_pool, n)
                g.affine_select(out=causal[rows], in_=causal[rows], compare_op=ALU.is_ge, fill=0.0, base=0,
                                pattern=[[1, T]], channel_multiplier=-1).then_inc(c_pool, 1)
            gp.wait_ge(c_pool, 13)
            g.affine_select(out=before_f, in_=before_f, compare_op=ALU.is_gt, fill=0.0, base=0,
                            pattern=[[1, P]], channel_multiplier=-1).then_inc(c_pool, 1)
            hm = headmask[:].rearrange("p t (h j) -> p t h j", h=8)
            g.affine_select(out=hm, in_=hm, compare_op=ALU.is_ge, fill=0.0, base=0,
                            pattern=[[0, 2], [-16, 8], [0, 8]], channel_multiplier=1).then_inc(c_pool, 1)
            g.affine_select(out=bits[:], in_=bits[:], compare_op=ALU.is_ge, fill=0.0, base=0,
                            pattern=[[-16, 8]], channel_multiplier=1).then_inc(c_pool, 1)
            gp.wait_ge(c_pool, 16)
            g.affine_select(out=hm, in_=hm, compare_op=ALU.is_ge, fill=0.0, base=15,
                            pattern=[[0, 2], [16, 8], [0, 8]], channel_multiplier=-1).then_inc(c_pool, 1)
            g.affine_select(out=bits[:], in_=bits[:], compare_op=ALU.is_ge, fill=0.0, base=7,
                            pattern=[[16, 8]], channel_multiplier=-1).then_inc(c_pool, 1)
            g.memset(VP[:, 0], 0.0).then_inc(c_pool, 1)
            g.memset(VP[:, 1], 0.0).then_inc(c_pool, 1)
            g.memset(QM[:, 0], 0.0).then_inc(c_pool, 1)
            g.memset(QM[:, 1], 0.0).then_inc(c_pool, 1)
            g.memset(empty[:], 0.0).then_inc(c_pool, 1)
            gp.wait_ge(c_pool, 23)
            g.memset(empty[:].rearrange("p (j w) -> p j w", w=RW)[:, :, D:D + 1], NOWHERE).then_inc(c_pool, 1)
            g.iota(x1[:, 0, :, D], [[1, NC]], base=-2 * S, channel_multiplier=NC,
                   allow_small_or_imprecise_dtypes=True).then_inc(c_pool, 1)
            g.iota(x1[:, 1, :, D], [[1, NC]], base=-S, channel_multiplier=NC,
                   allow_small_or_imprecise_dtypes=True).then_inc(c_pool, 1)
            g.memset(expert[:], 0.0).then_inc(c_pool, 1)
            xg_r = xg_d.rearrange("(e p j) d -> e p (j d)", e=E, p=P)
            gp.wait_ge(ld_w, 9 * 16)

            def step(b, par):
                f = b + 1
                if within(b, 1, B):
                    need(gp, v_ve, 2 * b - 1)
                    g.tensor_tensor(rs[:], ve[:], minus_half[:, 0:NC], ALU.pow).then_inc(g_r1, 1)

                if within(b, 1, B):
                    need(gp, v_ve, 2 * b)
                    g.tensor_tensor(rr[:, 1 - par], vq[:], minus_half[:].rearrange("p (a c) -> p a c", a=2),
                                    ALU.pow).then_inc(g_r2, 1)
                if within(b, -1, 14):
                    need(gp, ld_x, 16 * (f + 1))
                    need(gp, v_ln, 8 * (f - 1))
                    g.tensor_tensor(xb[:, 1 - par], xin[:, 1 - par], bet[:].unsqueeze(1).broadcast_to([P, NC, D]),
                                    ALU.add).then_inc(g_xb, 1)
                if isinstance(b, int) and b == 0:
                    gp.wait_ge(s_ld, 48)
                    for i in (0, 1):
                        g.tensor_copy(ws_hi[:, i], sraw[i]).then_inc(s_w, 1)
                        gp.wait_ge(s_w, 2 * i + 1)
                        g.tensor_tensor(ws_lo[:, i], sraw[i], ws_hi[:, i].bitcast(f32), ALU.subtract).then_inc(s_w, 1)
                if isinstance(b, int) and b in (0, 1):
                    gp.wait_ge(c_pool, 27)
                    gp.wait_ge(g_qm[1], P * (b + 1))
                    for e in range(b * E // 2, (b + 1) * E // 2):
                        gp.dma_start(xg_r[e], empty[:]).then_inc(g_sc, 16)
                if within(b, 2, B + 1):
                    hold(gp, g_sc, P * (b - 1), g_woke)
                    hold(gp, v_slot, b - 1, g_woke)
                    hold(gp, v_e0, b - 1, g_woke)
                    hold(gp, v_tok, b - 1, g_woke)
                    for j in range(2 * NC):
                        g.indirect_dma_start(out=xg_d, out_offset=bass.IndirectOffsetOnAxis(ap=slot[:, par, j:j + 1], axis=0),
                                             in_=x1[:, par, j % NC, :], in_offset=None, bounds_check=SLOTS - 1,
                                             oob_is_err=False).then_inc(g_sc, 16)
            stage1(gp, step)

            gp.wait_ge(pe_vg, 2 * B)
            def split(k, kp):
                for i in (0, 1):
                    hold(gp, e_ld, 48 * (k + 1), m_woke_g)
                    g.tensor_copy(we_hi[:, kp, i], wraw[:, kp, i]).then_inc(e_w, 1)
                    need(gp, e_w, 4 * k + 2 * i + 1)
                    g.tensor_tensor(we_lo[:, kp, i], wraw[:, kp, i], we_hi[:, kp, i].bitcast(f32),
                                    ALU.subtract).then_inc(e_w, 1)
            split(0, 0)
            gp.wait_ge(y_fill, 16 * B)

            def step(e, par):
                if within(e, 0, E - 2):
                    split(e + 1, 1 - par)
                hold(gp, e_goal, e + 1, m_woke_g)
                for n, (t0, cnt) in enumerate(GROUPS):
                    hold(gp, e_y, 3 * e + n + 1, m_woke_g)
                    for t in range(t0, t0 + cnt):
                        g.indirect_dma_start(out=yd_d, out_offset=bass.IndirectOffsetOnAxis(ap=goal_i[:, par, t:t + 1], axis=0),
                                             in_=ye[:, par, t, :], in_offset=None, bounds_check=2 * NT - 1,
                                             oob_is_err=False).then_inc(e_sc[par], 16)
            stage2(gp, step)

            def group(g):
                def first_sum(j):
                    m, i = 3 * g + j, j % 3
                    final = isinstance(m, int) and m == B - 1
                    hold(gp, m_ld[i], 64 * (g + (0 if j < 0 else 1 if j < 3 else 2)) - (16 if final else 0), g_woke)
                    hold(gp, m_z, 4 * (m - 1), g_woke)
                    x_in = xs[:, 0] if final else xc[:, i]
                    nc.gpsimd.tensor_tensor(w3[i], ge[:, i, 0], wts3[:, i, 0:NC].unsqueeze(2).broadcast_to([P, NC, D]),
                                            ALU.mult).then_inc(m_w1, 1)
                    need(gp, m_w1, m + 1)
                    if final:
                        need(gp, v_xs, B)
                    nc.gpsimd.tensor_tensor(w3[i], w3[i], x_in, ALU.add).then_inc(m_w, 1)
                if isinstance(g, int) and g == 0:
                    first_sum(0)
                for j in sums_of(g):
                    m, i = 3 * g + j, j % 3
                    if within(m, 0, B - 2):
                        first_sum(j + 1)
                    need(gp, m_ve, 2 * (m + 1))
                    need(gp, m_o, 4 * (m - 1))
                    nc.gpsimd.tensor_tensor(rs3[:, i], ve[:], minus_half[:, 0:NC], ALU.pow).then_inc(m_r, 1)
                    need(gp, m_r, m + 1)
                    nc.gpsimd.tensor_tensor(shift[:, i], minus_mean[:, i], rs3[:, i], ALU.mult).then_inc(m_s, 1)
            stage3(gp, group)

        @block.scalar
        def _(act):
            a = nc.scalar
            act.wait_ge(c_pool, 1)
            a.activation(warm[:], zeros[:, 0:1], ACT.Silu).then_inc(c_warm, 1)

            def silu(f, par, i):
                need(act, pe_qk, 4 * f + i + 1)
                need(act, v_qk, 4 * f + i - 1)
                a.activation(sq[:, i % 2], PB[i % 2][:], ACT.Silu).then_inc(a_silu, 1)

            def copy_out(b, c, par):
                need(act, pe_av, 4 * b + c + 1)
                need(act, pe_wo, b - 1)
                a.activation(oT[:, par, P * c:P * (c + 1)], OB[:, P * c:P * (c + 1)], ACT.Copy).then_inc(a_out, 1)

            def values(f, par, i):
                need(act, pe_vg, 2 * f + i + 1)
                need(act, pe_av, 4 * (f - 1))
                for c in (0, 1):
                    src = PB[i][:, 256 * c:256 * c + D].rearrange("p (j i d) -> p j i d", j=4, i=4)
                    a.activation(vp_view(par, 2 * i + c), src, ACT.Copy).then_inc(a_v, 1)
                need(act, v_y, f - 1)
                src = PB[i][:].rearrange("p (c n) -> p c n", c=2)[:, :, D:2 * D]
                dst = th[:, par].rearrange("p (c n) -> p c n", c=NC)[:, 2 * i:2 * i + 2]
                a.activation(dst, src, ACT.Tanh, scale=0.5).then_inc(a_th, 1)

            def shared_silu(b, f, q=None):
                q = shared_turn(b) if q is None else q
                if q is not None:
                    need(act, pe_gt, 8 * q + f + 1)
                    need(act, v_h, 8 * q + f - 1)
                    a.activation(sf[:, f % 2], GB[:], ACT.Silu).then_inc(a_sf, 1)

            def step(b, par):
                f, fp = b + 1, 1 - par
                front, core = within(b, -1, 14), within(b, 0, B - 1)
                if front:
                    need(act, pe_xT, f + 1)
                    need(act, pe_vg, 2 * f)
                    a.activation(xhi[:, 0], PB[0][:], ACT.Copy).then_inc(a_xhi, 1)
                out_first = isinstance(b, int) and b == B
                if out_first:
                    copy_out(b - 1, 3, 1 - par)
                if within(b, 2, B + 1):
                    need(act, pe_x1T, b - 1)
                    a.activation(x1T[:], PB[1][:], ACT.Copy).then_inc(a_x1T, 1)
                if shared_turn(b) is not None or isinstance(b, int) and b == B:
                    need(act, a_x1T, b - 1)
                    a.activation(xhi[:, 1], x1T[:], ACT.Copy).then_inc(a_x1h, 1)
                if within(b, 1, B) and not out_first:
                    copy_out(b - 1, 3, 1 - par)
                if front:
                    silu(f, fp, 0)
                shared_silu(b, 0)
                if core:
                    copy_out(b, 0, par)
                shared_silu(b, 1)
                if front:
                    silu(f, fp, 1)
                if isinstance(b, int) and b == -1:
                    act.wait_ge(c_dve, 19)
                    a.activation(table[:], table[:], ACT.Sin).then_inc(c_sin, 1)
                    act.wait_ge(c_pool, 20)
                shared_silu(b, 2)
                if core:
                    copy_out(b, 1, par)
                shared_silu(b, 3)
                if front:
                    silu(f, fp, 2)
                    silu(f, fp, 3)
                shared_silu(b, 4)
                if front:
                    values(f, fp, 0)
                    values(f, fp, 1)
                shared_silu(b, 5)
                if front:
                    for i in (0, 1):
                        need(act, pe_kt, 2 * f + i + 1)
                        need(act, pe_S, NS * (f - 1))
                        a.activation(Kt[:, fp, 2 * i:2 * i + 2], PB[i][:].rearrange("p (c n) -> p c n", c=2),
                                     ACT.Copy).then_inc(a_kt, 1)
                if core:
                    copy_out(b, 2, par)
                shared_silu(b, 6)
                if isinstance(b, int) and b == B + 1:
                    for f in TILES_B1:
                        shared_silu(b, f, EARLY - 1)
                if within(b, 2, B + 1):
                    need(act, v_gap, b - 1)
                    a.activation(tw[:], gapr[:], ACT.Tanh, scale=0.5).then_inc(a_tw, 1)
                shared_silu(b, 7)
                if isinstance(b, int) and b >= B:
                    for f in (TILES_B, TILES_END)[b - B]:
                        shared_silu(b, f, EARLY - 1)

            def vp_view(par, c):
                v = VP[:, par, c]
                return bass.AP(tensor=v.tensor, offset=v.offset, ap=[list(v.ap[0]), [128, 4], [40, 4], [1, 8]])
            stage1(act, step)

            def split_late(r, n):
                need(act, m_x1T, n)
                a.activation(x1T[:], PB[1][:], ACT.Copy).then_inc(m_a, 1)
                need(act, m_a, n)
                need(act, pe_up, 8 * r)
                a.activation(xhi[:, 1], x1T[:], ACT.Copy).then_inc(a_x1h, 1)

            def step(e, par):
                def split(k, kp, groups):
                    for i in groups:
                        t0, n = GROUPS[i]
                        need(act, e_xT, 3 * k + i + 1)
                        if i == 0:
                            need(act, e_gu, 12 * (k - 1))
                        a.activation(xgT_hi[:, kp, P * t0:P * (t0 + n)], PB[(3 * kp + i) % 2][:, 0:P * n],
                                     ACT.Copy).then_inc(e_hi, 1)

                def group(n):
                    for f in range(4):
                        k = 12 * e + 4 * n + f
                        need(act, e_gt, k + 1)
                        need(act, e_h, k - 1)
                        w = P * GROUPS[n][1]
                        a.activation(sq[:, f % 2, 0:w], EB[f % 2][:, 0:w], ACT.Silu).then_inc(e_silu, 1)

                def rows(n):
                    t0, cnt = GROUPS[n]
                    need(act, e_dn, 3 * e + n + 1)
                    if n == 0:
                        need(act, e_sc[par], 8 * CT * (e - par))
                    a.activation(ye[:, par, t0:t0 + cnt], (OB, SBK)[(n + par) % 2][:, 0:P * cnt].rearrange("p (t d) -> p t d", t=cnt),
                                 ACT.Copy).then_inc(e_y, 1)
                last_one = isinstance(e, int) and e == E - 1
                if isinstance(e, int) and e == 0:
                    split(0, 0, (0, 1, 2))
                group(0)
                if within(e, 0, E - 2):
                    split(e + 1, 1 - par, (0, 1))
                group(1)
                if within(e, 0, E - 2):
                    split(e + 1, 1 - par, (2,))
                if last_one:
                    rows(0)
                group(2)
                if last_one:
                    need(act, e_gu, 12 * E)
                    split_late(EARLY, 1)
                else:
                    rows(0)
                rows(1)
                rows(2)
            stage2(act, step)

            act.sem_inc(m_o, 4)

            def group(g):
                r = EARLY + g

                def normed(j, cs=range(NC)):
                    m = 3 * g + j
                    need(act, m_s, m + 1)
                    need(act, m_st[j % 3], 16 * (g + (j == 0)))
                    for c in cs:
                        a.activation(xo[:, j % 3, c], y3[j % 3][:, c], ACT.Identity, scale=rs3[:, j % 3, c:c + 1],
                                     bias=shift[:, j % 3, c:c + 1]).then_inc(m_o, 1)

                def shared_silu(f):
                    need(act, pe_gt, 8 * r + f + 1)
                    need(act, v_h, 8 * r + f - 1)
                    a.activation(sf[:, f % 2], (GB[:], EB2[:, 0])[f % 2], ACT.Silu).then_inc(a_sf, 1)
                if isinstance(g, int) and g == 5:
                    normed(-2)
                    normed(-1)
                    normed(0)
                    return
                if isinstance(g, int) and g == 0:
                    for f in range(8):
                        shared_silu(f)
                    split_late(r + 1, 2)
                    normed(0)
                    return
                for f in range(8):
                    shared_silu(f)
                    if f in (1, 2):
                        normed(-2, ((0, 1), (2, 3))[f - 1])
                    if f in (4, 5):
                        normed(-1, ((0, 1), (2, 3))[f - 4])
                if within(g, 0, 3):
                    split_late(r + 1, g + 2)
                normed(0)
            stage3(act, group)

        @block.vector
        def _(dve):
            v = nc.vector
            n_c = [0]
            dve.sem_inc(v_pos, 2)
            turns = KT[:, 0]

            def link(ins):
                n_c[0] += 1
                ins.then_inc(c_dve, 1)
                dve.wait_ge(c_dve, n_c[0])
            dve.wait_ge(c_pool, 18)
            link(v.tensor_reduce(cosine[:], bits[:], AX.X, ALU.add))
            link(v.tensor_copy(before[:], before_f))
            link(v.tensor_scalar(phase[:, 0:1], cosine[:], 0.25, None, ALU.mult))
            link(v.tensor_scalar(phase[:, 1:2], cosine[:], 1.5707963267948966, None, ALU.mult))
            dve.wait_ge(ld_w, 9 * 16)
            link(v.tensor_copy(wqk_hi, sq[:, 0]))
            link(v.tensor_tensor(wqk_lo, sq[:, 0], wqk_hi.bitcast(f32), ALU.subtract))
            dve.wait_ge(c_g, 1)
            link(v.tensor_copy(sq[:, 1, D:2 * D], PB[0][:, 0:D]))
            link(v.tensor_copy(wvg_hi, sq[:, 1, 0:2 * D]))
            link(v.tensor_tensor(wvg_lo, sq[:, 1, 0:2 * D], wvg_hi.bitcast(f32), ALU.subtract))
            link(v.tensor_scalar(table[:, 0], pos_n, theta_s[:, 0:1], None, ALU.mult))
            link(v.tensor_scalar(table[:, 1], pos_n, theta_s[:, 1:2], None, ALU.mult))
            link(v.tensor_scalar(turns, table[:], 0.15915494309189535, phase[:, 0:1], ALU.mult, ALU.add))
            dve.wait_ge(a_xhi, 1)
            v.tensor_tensor(xlo[:, 0], PB[0][:], xhi[:, 0].bitcast(f32), ALU.subtract).then_inc(v_xlo, 1)
            link(v.tensor_scalar(turns, turns, MAGIC, None, ALU.add))
            link(v.tensor_scalar(turns, turns, MAGIC, None, ALU.subtract))
            for part in TWO_PI:
                link(v.scalar_tensor_tensor(table[:], turns, -part, table[:], ALU.mult, ALU.add))
            link(v.tensor_scalar(table[:], table[:], phase[:, 1:2], PI_IN, ALU.add, ALU.min))
            link(v.tensor_scalar(table[:], table[:], -PI_IN, None, ALU.max))

            def turn(f, fp, i):
                dst = QT[:, fp, :, i] if i < 2 else KT[:, fp, i % 2]
                need(dve, a_silu, 4 * f + i + 1)
                if i == 0 and isinstance(f, int) and f == 0:
                    dve.wait_ge(c_sin, 1)
                need(dve, pe_av, 4 * (f - 1))
                if i < 2:
                    need(dve, g_qm[1], P * (f - 1))
                activated, angles = sq[:, i % 2], table[:, i % 2]
                if i < 2:
                    activated, angles = (z.rearrange("p (g n) -> p g n", g=2) for z in (activated, angles))
                v.tensor_tensor(dst, activated, angles, ALU.mult).then_inc(v_qk, 1)

            def mask(b, par, c, i):
                if within(b, 0, B - 1):
                    need(dve, pe_E, 8 * b + 2 * c + i + 1)
                    need(dve, pe_av, 4 * b + c - 1)
                    v.tensor_tensor(EM[:, c % 2, i], EB2[:, i].rearrange("p (h n) -> p h n", h=8),
                                    causal[:].unsqueeze(1).broadcast_to([P, 8, T]), ALU.mult).then_inc(v_mask, 1)
                    k = 2 * c + i
                    if k < NS:
                        need(dve, pe_S, NS * b + k + 1)
                        need(dve, pe_av, 4 * (b - 1) + (k + 1) // 2 + 1)
                        v.tensor_tensor(SM[:, k], SBK[:, 0:128], headmask[:].rearrange("p t n -> p (t n)"),
                                        ALU.mult).then_inc(v_S, 1)

            def shared_add(par, q):
                if q is not None:
                    need(dve, pe_dn, q + 1)
                    need(dve, xs_free, q + 1)
                    v.tensor_tensor(xs[:, 1 - par], x1[:, 1 - par, :, 0:D],
                                    UB[:].rearrange("p (c d) -> p c d", c=NC), ALU.add).then_inc(v_xs, 1)

            def shared_hidden(b, f, q=None):
                q = shared_turn(b) if q is None else q
                if q is not None:
                    n = 8 * q + f
                    need(dve, a_sf, n + 1)
                    need(dve, pe_up, n + 1)
                    if f == 0:
                        need(dve, pe_dn, q)
                    v.tensor_tensor(hs[:, f], sf[:, f % 2], UB[:], ALU.mult).then_inc(v_h, 1)

            def moments(src, dst, n, s_bn, s_ag, woke):
                for c in range(NC):
                    v.bn_stats(st[:, c], src[:, c]).then_inc(s_bn, 1)
                hold(dve, s_bn, 4 * n + 4, woke)
                for c in range(NC):
                    v.bn_aggr(dst[:, c], st[:, c]).then_inc(s_ag, 1)
                need(dve, s_ag, 4 * n + 4)

            def scale_x1(b, buf):
                need(dve, g_r2, b)
                need(dve, g_sc, P * (b - 1))
                if isinstance(b, int):
                    need(dve, sp_x1b, 16 * min(b - 2 - FIRST_LATE, LATE - 1))
                for c in range(NC):
                    v.tensor_scalar(x1[:, buf, c, 0:D], s1[:, c], mv2[:, c, 0:1], rr[:, buf, 0, c:c + 1],
                                    ALU.subtract, ALU.mult).then_inc(v_x1, 1)
                v.tensor_scalar(x1[:, buf, :, D], x1[:, buf, :, D], 2.0 * S, None, ALU.add).then_inc(v_tok, 1)

            def step(b, par):
                f, fp = b + 1, 1 - par
                front = within(b, -1, 14)
                back, route = within(b, 1, B), within(b, 2, B + 1)
                R = 9 * (b - 2)
                mask(b, par, 0, 0)
                if within(b, 0, 14):
                    need(dve, a_xhi, f + 1)
                    need(dve, pe_vg, 2 * f)
                    v.tensor_tensor(xlo[:, 0], PB[0][:], xhi[:, 0].bitcast(f32), ALU.subtract).then_inc(v_xlo, 1)
                mask(b, par, 0, 1)
                if no_ffn(b - 1):
                    scale_x1(b - 1, par)
                q = shared_turn(b) if not isinstance(b, int) or b != B else EARLY - 1
                if q is not None:
                    need(dve, a_x1h, q + 1)
                    v.tensor_tensor(xlo[:, 1], x1T[:], xhi[:, 1].bitcast(f32), ALU.subtract).then_inc(v_x1l, 1)
                shared_add(par, shared_turn(b - 1))
                mask(b, par, 1, 0)
                shared_hidden(b, 0)
                mask(b, par, 1, 1)
                shared_hidden(b, 1)
                if front:
                    turn(f, fp, 0)
                if back:
                    need(dve, pe_wo, b)
                    need(dve, a_th, 2 * b)
                    v.scalar_tensor_tensor(y2[:].rearrange("p c d -> p (c d)"), th[:, 1 - par], 1.0, PB[0][:], ALU.add,
                                           ALU.mult).then_inc(v_y, 1)
                    need(dve, v_y, b)
                    moments(y2, mv, 2 * (b - 1), v_bn, v_ag, v_woke)
                    v.tensor_scalar(ve[:], mv[:, :, 1], 4 * EPS, None, ALU.add).then_inc(v_ve, 1)
                mask(b, par, 2, 0)
                shared_hidden(b, 2)
                if route:
                    need(dve, pe_lg, b - 1)
                    v.tensor_copy(lg[:].rearrange("p c e -> p (c e)"), PB[1][:, 0:8 * NC]).then_inc(v_lg, 1)
                mask(b, par, 2, 1)
                shared_hidden(b, 3)
                if front:
                    turn(f, fp, 1)
                    turn(f, fp, 2)
                    turn(f, fp, 3)
                shared_hidden(b, 4)
                if route:
                    hold(dve, v_lg, b - 1, v_woke)
                    for c in range(NC):
                        v.max(m8[:, c], lg[:, c]).then_inc(v_rt, 1)
                    hold(dve, v_rt, R + 4, v_woke)
                    for c in range(NC):
                        v.max_index(ix8[:, c], m8[:, c], lg[:, c]).then_inc(v_rt, 1)
                    v.tensor_tensor(gap[:], m8[:, :, 0], m8[:, :, 1], ALU.subtract).then_inc(v_rt, 1)
                    need(dve, v_rt, R + 9)
                    v.tensor_tensor(gapr[:], gap[:], rr[:, par, 1], ALU.mult).then_inc(v_gap, 1)
                    v.tensor_copy(ixf[:].rearrange("p k c -> p c k"), ix8[:, :, 0:2]).then_inc(v_M, 1)
                    need(dve, v_M, 6 * (b - 2) + 1)
                    v.tensor_tensor(oh[:], iota8[:], ixf[:].rearrange("p k c -> p (k c)").unsqueeze(2).broadcast_to([P, 2 * NC, 8]),
                                    ALU.is_equal).then_inc(v_M, 1)
                    need(dve, v_M, 6 * (b - 2) + 2)
                    v.tensor_tensor(mb[:], oh[:, 0:NC], oh[:, NC:2 * NC], ALU.add).then_inc(v_M, 1)
                if back:
                    for c in range(NC):
                        v.scalar_tensor_tensor(wv[:, c], y2[:, c], mv[:, c, 0:1], gam[:], ALU.subtract,
                                               ALU.mult).then_inc(v_ln, 1)
                    need(dve, v_ln, 8 * (b - 1) + 4)
                    need(dve, g_xb, b)
                    need(dve, g_r1, b)
                    for c in range(NC):
                        v.scalar_tensor_tensor(s1[:, c], wv[:, c], rs[:, c:c + 1], xb[:, 1 - par, c], ALU.mult,
                                               ALU.add).then_inc(v_ln, 1)
                if isinstance(b, int) and b == B + 1:
                    for f in TILES_B1:
                        shared_hidden(b, f, EARLY - 1)
                mask(b, par, 3, 0)
                if isinstance(b, int) and b == B - 1:
                    mask(b, par, 3, 1)
                shared_hidden(b, 5)
                if back:
                    need(dve, v_ln, 8 * b)
                    moments(s1, mv2, 2 * (b - 1) + 1, v_bn, v_ag, v_woke)
                    v.tensor_scalar(vq[:, 0], mv2[:, :, 1], EPS, None, ALU.add).then_inc(v_M2, 1)
                    if no_ffn(b) and b < B - 1:
                        mask(b, par, 3, 1)
                    need(dve, v_M2, 3 * (b - 1) + 1)
                    v.reciprocal(vq[:, 1], vq[:, 0]).then_inc(v_M2, 1)
                    need(dve, v_M2, 3 * (b - 1) + 2)
                    v.tensor_tensor(vq[:, 1], vq[:, 1], mv2[:, :, 1], ALU.mult).then_inc(v_M2, 1)
                    need(dve, v_M2, 3 * (b - 1) + 3)
                    v.tensor_scalar(vq[:, 1], vq[:, 1], EPS_RMS, None, ALU.add).then_inc(v_ve, 1)
                if route:
                    need(dve, pe_pos, b - 1)
                    posb = position_bank(b).rearrange("p (c e) -> p c e", c=NC)
                    v.tensor_scalar(over[:], posb, float(CAP), FAR, ALU.is_ge, ALU.mult).then_inc(v_P, 1)
                    v.tensor_tensor(slotv[:], posb, eoff[:], ALU.add).then_inc(v_pos, 1)
                if not no_ffn(b):
                    mask(b, par, 3, 1)
                shared_hidden(b, 6)
                if route:
                    v.tensor_reduce(seen_f[:], mb[:].rearrange("p c e -> p e c"), AX.X, ALU.add).then_inc(v_P, 1)
                    need(dve, v_P, 5 * (b - 2) + 2)
                    need(dve, v_pos, b + 1)
                    v.tensor_tensor(slotv[:], slotv[:], over[:], ALU.add).then_inc(v_P, 1)
                    v.tensor_tensor(seen[:], seen[:], seen_f[:], ALU.add).then_inc(v_M, 1)
                    need(dve, v_P, 5 * (b - 2) + 3)
                    v.tensor_copy(x1[:, par, :, D + 1], ixf[:, 0]).then_inc(v_e0, 1)
                    for k in (0, 1):
                        v.tensor_tensor(pick[:, NC * k:NC * (k + 1)], oh[:, NC * k:NC * (k + 1)], slotv[:],
                                        ALU.mult).then_inc(v_M, 1)
                    need(dve, v_M, 6 * (b - 2) + 6)
                    v.tensor_reduce(slotf[:], pick[:], AX.X, ALU.add).then_inc(v_P, 1)
                    need(dve, v_P, 5 * (b - 2) + 4)
                    need(dve, rt_free, b - 1)
                    v.tensor_scalar(slot[:, par], slotf[:], float(SLOTS), None, ALU.min).then_inc(v_slot, 1)
                    need(dve, a_tw, b - 1)
                    v.tensor_scalar(wts[:, par, 0:NC], tw[:], 0.5, 0.5, ALU.mult, ALU.add).then_inc(v_P, 1)
                    v.tensor_scalar(wts[:, par, NC:2 * NC], tw[:], -0.5, 0.5, ALU.mult, ALU.add).then_inc(v_wts, 1)
                if isinstance(b, int) and b == B:
                    shared_hidden(b, TILES_B[0], EARLY - 1)
                if back and not no_ffn(b):
                    scale_x1(b, 1 - par)
                shared_hidden(b, 7)
                if isinstance(b, int) and b >= B:
                    for f in (TILES_B[1:], TILES_END)[b - B]:
                        shared_hidden(b, f, EARLY - 1)
                    if b == B + 1:
                        shared_add(par, EARLY - 1)
            stage1(dve, step)

            def step(e, par):
                def goals(k, kp):
                    need(dve, e_ldx, 16 * (k + 1))
                    v.tensor_scalar(second[:], xg[:, kp, :, D + 1], expert[:, 0:1], float(NT), ALU.not_equal,
                                    ALU.mult).then_inc(e_ix, 1)
                    need(dve, e_ix, 3 * k + 1)
                    v.tensor_tensor(goal[:], second[:], xg[:, kp, :, D], ALU.add).then_inc(e_ix, 1)
                    v.tensor_scalar(expert[:], expert[:], 1.0, None, ALU.add).then_inc(e_ix, 1)
                    need(dve, e_ix, 3 * k + 3)
                    need(dve, e_sc[kp], 8 * CT * (k - kp))
                    v.tensor_scalar(goal_i[:, kp], goal[:], NOWHERE, None, ALU.min).then_inc(e_goal, 1)
                goals(e, par)

                def split(k, kp, groups):
                    for i in groups:
                        t0, n = GROUPS[i]
                        need(dve, e_hi, 3 * k + i + 1)
                        if i == 0:
                            need(dve, e_gu, 12 * (k - 1))
                        cols = slice(P * t0, P * (t0 + n))
                        v.tensor_tensor(xgT_lo[:, kp, cols], PB[(3 * kp + i) % 2][:, 0:P * n],
                                        xgT_hi[:, kp, cols].bitcast(f32), ALU.subtract).then_inc(e_lo, 1)

                def group(n):
                    hp = (n + par) % 2
                    for f in range(4):
                        k = 12 * e + 4 * n + f
                        w = P * GROUPS[n][1]
                        need(dve, e_silu, k + 1)
                        need(dve, e_gu, k + 1)
                        if f == 0:
                            need(dve, e_dn, 3 * e + n - 1)
                        v.tensor_tensor(he[:, hp, f, 0:w], sq[:, f % 2, 0:w], EB[2 + f % 2][:, 0:w],
                                        ALU.mult).then_inc(e_h, 1)
                if isinstance(e, int) and e == 0:
                    split(0, 0, (0, 1, 2))
                group(0)
                if within(e, 0, E - 2):
                    split(e + 1, 1 - par, (0, 1))
                group(1)
                if within(e, 0, E - 2):
                    split(e + 1, 1 - par, (2,))
                group(2)
            stage2(dve, step)

            def group(g):
                r = EARLY + g

                def weighted(j):
                    m, i = 3 * g + j, j % 3
                    need(dve, m_w, m + 1)
                    need(dve, m_o, 4 * (m - 1))
                    for c in range(NC):
                        v.scalar_tensor_tensor(y3[i][:, c], ge[:, i, 1, c], wts3[:, i, NC + c:NC + c + 1], w3[i][:, c],
                                               ALU.mult, ALU.add).then_inc(m_z, 1)

                def stats(j):
                    m = 3 * g + j
                    need(dve, m_z, 4 * m + 4)
                    need(dve, m_ag, 4 * m)
                    for c in range(NC):
                        v.bn_stats(st[:, c], y3[j % 3][:, c]).then_inc(m_bn, 1)

                def spread(j):
                    m = 3 * g + j
                    i = j % 3
                    hold(dve, m_bn, 4 * m + 4, m_woke_v)
                    for c in range(NC):
                        v.bn_aggr(mv3[:, i, c], st[:, c]).then_inc(m_ag, 1)
                    need(dve, m_ag, 4 * m + 4)
                    need(dve, m_r, m)
                    v.tensor_scalar(minus_mean[:, i], mv3[:, i, :, 0], -1.0, None, ALU.mult).then_inc(m_ve, 1)
                    v.tensor_scalar(ve[:], mv3[:, i, :, 1], EPS, None, ALU.add).then_inc(m_ve, 1)

                def hidden(f):
                    n = 8 * r + f
                    need(dve, a_sf, n + 1)
                    need(dve, pe_up, n + 1)
                    if f == 0:
                        need(dve, pe_dn, r)
                    v.tensor_tensor(hs[:, f], sf[:, f % 2], (UB[:], EB2[:, 1])[f % 2], ALU.mult).then_inc(v_h, 1)

                def split(n, r):
                    need(dve, a_x1h, r + 1)
                    v.tensor_tensor(xlo[:, 1], x1T[:], xhi[:, 1].bitcast(f32), ALU.subtract).then_inc(v_x1l, 1)

                def added(r, n):
                    need(dve, pe_dn, r + 1)
                    need(dve, m_x1a, 16 * n)
                    need(dve, sp_x1, 16 * r)
                    v.tensor_tensor(xs[:, 0], x1a, UB[:].rearrange("p (c d) -> p c d", c=NC), ALU.add).then_inc(v_xs, 1)
                if isinstance(g, int) and g == 0:
                    split(0, r)
                    for f in range(8):
                        hidden(f)
                    weighted(0)
                    split(1, r + 1)
                    stats(0)
                    spread(0)
                    added(r, 1)
                    weighted(1)
                    stats(1)
                    spread(1)
                    return
                if isinstance(g, int) and g == 5:
                    weighted(-1)
                    stats(-1)
                    spread(-1)
                    added(r - 1, g)
                    weighted(0)
                    stats(0)
                    spread(0)
                    return
                hidden(0)
                weighted(-1)
                hidden(1)
                stats(-1)
                hidden(2)
                spread(-1)
                hidden(3)
                weighted(0)
                hidden(4)
                stats(0)
                hidden(5)
                spread(0)
                hidden(6)
                hidden(7)
                weighted(1)
                if within(g, 0, 3):
                    split(g + 1, r + 1)
                stats(1)
                spread(1)
                if within(g, 0, 3):
                    added(r, g + 1)
            stage3(dve, group)

        @block.tensor
        def _(pe):
            t = nc.tensor
            pe.wait_ge(ld_w, 9 * 16)
            t.matmul(PB[0][:, 0:D], g1t_s, g2_s, start=True, stop=True).then_inc(c_g, 1)
            pe.wait_ge(c_id, 2)

            def three(dst, w_hi, w_lo, x_hi, x_lo):
                t.matmul(dst, w_hi, x_hi, start=True, stop=False)
                t.matmul(dst, w_hi, x_lo, start=False, stop=False)
                return t.matmul(dst, w_lo, x_hi, start=False, stop=True)

            def project(f, i):
                bank = i % 2
                if i == 0:
                    need(pe, a_xhi, f + 1)
                    need(pe, v_xlo, f + 1)
                elif i == 1:
                    need(pe, a_x1T, f - 2)
                elif i == 2:
                    need(pe, a_silu, 4 * f + 1)
                    need(pe, v_y, f - 1)
                else:
                    need(pe, a_silu, 4 * f + 2)
                    need(pe, v_lg, f - 2)
                cols = slice(P * i, P * (i + 1))
                three(PB[bank][:], wqk_hi[:, cols], wqk_lo[:, cols], xhi[:, 0], xlo[:, 0]).then_inc(pe_qk, 1)

            def step(b, par):
                f, fp = b + 1, 1 - par
                front, core = within(b, -1, 14), within(b, 0, B - 1)
                back, route = within(b, 1, B), within(b, 2, B + 1)
                if isinstance(b, int) and b == -1:
                    pe.wait_ge(c_dve, 7)

                def energies(c, i):
                    if c == 0 and i == 0:
                        need(pe, v_qk, 4 * b + 4)
                    if c % 2 == 0 and i == 0:
                        need(pe, g_qm[c // 2], P * (b + 1))
                    need(pe, v_mask, 8 * b + 2 * c + i - 1)
                    for s in (0, 1):
                        tok = slice(T * s, T * (s + 1))
                        ins = t.matmul(EB2[T * s:T * (s + 1), i], KT[:, par, i, P * c + T * s:P * c + T * (s + 1)],
                                       QM[:, c // 2, i, c % 2, :, tok], start=True, stop=True)
                    ins.then_inc(pe_E, 1)
                    k = 2 * c + i
                    if k == NS:
                        return
                    if k == 0:
                        need(pe, a_kt, 2 * b + 2)
                        need(pe, a_v, 4 * b + 4)
                        if not isinstance(b, int) or b <= FIRST_LATE + 2:
                            need(pe, v_pos, b)
                    need(pe, v_S, NS * b + k)
                    tok = slice(T * i, T * (i + 1))
                    for half in (0, 1):
                        ins = t.matmul(SBK[:, T * half:T * half + T], Kt[tok, par, c, P * half:P * half + P],
                                       v_rows(par, c, half, tok), start=(k == 0 and half == 0), stop=True,
                                       skip_group_check=True)
                    ins.then_inc(pe_S, 1)

                def attend(b, par, c, s):
                    if s == 0:
                        need(pe, a_out, 4 * b + c)
                        need(pe, v_S, NS * b + 2 * c)
                        hold(pe, v_mask, 8 * b + 2 * c + 2, pe_woke)
                    else:
                        need(pe, v_S, NS * b + 2 * c + 1)
                        hold(pe, pe_av0, 4 * b + c + 1, pe_woke)
                    tok = slice(P * c + T * s, P * c + T * (s + 1))
                    keys = slice(T * s, T * (s + 1))
                    k = 2 * c + s
                    for half in (0, 1):
                        if k > 0:
                            t.matmul(OB[T * half:T * half + T, tok], SM[:, k - 1, T * half:T * half + T],
                                     QT[:, par, c // 2, half, P * (c % 2) + T * s:P * (c % 2) + T * (s + 1)], start=True, stop=False)
                    for i in range(4):
                        for j in range(4):
                            h = 4 * j + i
                            ins = t.matmul(OB[32 * j:32 * j + 32, tok], VP[keys, par, c, 32 * h:32 * h + 32],
                                           EM[keys, c % 2, h // 8, h % 8], start=(k == 0 and i == 0), stop=(i == 3))
                    ins.then_inc((pe_av0, pe_av)[s], 1)

                def shared_pair(f, q=None):
                    q = shared_turn(b) if q is None else q
                    if q is None:
                        return
                    n = 8 * q + f
                    ff = slice(P * f, P * (f + 1))
                    if f == 0:
                        need(pe, a_x1h, q + 1)
                        need(pe, v_x1l, q + 1)
                        if isinstance(b, int):
                            need(pe, s_w, 4)
                        if isinstance(b, int) and b == B:
                            need(pe, v_pos, B)
                    need(pe, a_sf, n)
                    three(GB[:], ws_hi[:, 0, ff], ws_lo[:, 0, ff], xhi[:, 1], xlo[:, 1]).then_inc(pe_gt, 1)
                    need(pe, v_h, n)
                    if f == 0:
                        need(pe, v_xs, q)
                    three(UB[:], ws_hi[:, 1, ff], ws_lo[:, 1, ff], xhi[:, 1], xlo[:, 1]).then_inc(pe_up, 1)

                def shared_down(cs, q=None):
                    q = shared_turn(b - 1) if q is None else q
                    if q is None:
                        return
                    need(pe, v_h, 8 * (q + 1))
                    for c in cs:
                        for f in range(8):
                            ins = t.matmul(UB[:, P * c:P * (c + 1)], hs[:, f, P * c:P * (c + 1)], sd_s[:, f],
                                           start=(f == 0), stop=(f == 7))
                    if NC - 1 in cs:
                        ins.then_inc(pe_dn, 1)

                def part(c, s):
                    if core:
                        energies(c, s)
                    if c > 0 and core:
                        attend(b, par, c - 1, s)
                    elif c == 0 and back:
                        attend(b - 1, 1 - par, 3, s)

                def turn_x1():
                    need(pe, v_x1, 4 * (b - 1))
                    need(pe, a_kt, 2 * last(b) + 2)
                    if isinstance(b, int):
                        need(pe, v_lg, b - 2)
                    for c in range(NC):
                        ins = t.transpose(PB[1][:, P * c:P * (c + 1)], x1[:, par, c, 0:D], ident[:])
                    ins.then_inc(pe_x1T, 1)

                part(0, 0)
                shared_down((0, 1))
                if front:
                    need(pe, ld_x, 16 * (f + 1))
                    need(pe, a_kt, 2 * f)
                    for c in range(NC):
                        ins = t.transpose(PB[0][:, P * c:P * (c + 1)], xin[:, fp, c], ident[:])
                    ins.then_inc(pe_xT, 1)
                x1_late = no_ffn(b) or isinstance(b, int) and b == B
                if route and not x1_late:
                    turn_x1()
                part(0, 1)
                shared_down((2, 3))
                if isinstance(b, int) and b == -1:
                    pe.wait_ge(c_dve, 9)
                if front:
                    project(f, 0)
                if x1_late:
                    turn_x1()
                part(1, 0)
                shared_pair(0)
                part(1, 1)
                shared_pair(1)
                if front:
                    project(f, 1)
                if back:
                    need(pe, a_out, 4 * b)
                    need(pe, a_silu, 4 * last(b + 1) + 1)
                    if isinstance(b, int):
                        need(pe, v_y, b - 1)
                    for c in range(NC):
                        ins = t.matmul(PB[0][:, P * c:P * (c + 1)], oT[:, 1 - par, P * c:P * (c + 1)], wo_s[:],
                                       start=True, stop=True)
                    ins.then_inc(pe_wo, 1)
                if route:
                    need(pe, a_x1T, b - 1)
                    need(pe, a_silu, 4 * last(b + 1) + 2)
                    for c in range(NC):
                        ins = t.matmul(PB[1][:, 8 * c:8 * c + 8], x1T[:, P * c:P * (c + 1)], rwt_s[:], start=True, stop=True)
                    ins.then_inc(pe_lg, 1)
                part(2, 0)
                shared_pair(2)
                part(2, 1)
                shared_pair(3)
                if front:
                    project(f, 2)
                    project(f, 3)
                shared_pair(4)
                if front:
                    for i in (0, 1):
                        need(pe, a_silu, 4 * f + 3 + i)
                        for c in (0, 1):
                            tok = slice(P * (2 * i + c), P * (2 * i + c + 1))
                            ins = three_r(PB[i][:, 256 * c:256 * c + 256], tok)
                        ins.then_inc(pe_vg, 1)
                part(3, 0)
                shared_pair(5)
                if front:
                    need(pe, v_qk, 4 * f + 4)
                    for i in (0, 1):
                        need(pe, a_v, 4 * f + 2 * i + 2)
                        need(pe, a_th, 2 * f + i + 1)
                        for c in (0, 1):
                            for half in (0, 1):
                                ins = t.transpose(PB[i][:, 256 * c + P * half:256 * c + P * half + P],
                                                  KT[:, fp, half, P * (2 * i + c):P * (2 * i + c + 1)], ident[:])
                        ins.then_inc(pe_kt, 1)
                part(3, 1)
                if route:
                    need(pe, v_M, 6 * (b - 2) + 3)
                    need(pe, v_S, NS * (last(b) + 1))
                    if isinstance(b, int) and b >= FIRST_LATE + 2:
                        need(pe, a_sf, 8 * FIRST_LATE)
                    o = position_bank(b)
                    t.matmul(o.rearrange("p (c e) -> p c e", c=NC), ones[:], seen[:].unsqueeze(1).broadcast_to([P, NC, 8]),
                             start=True, stop=False)
                    mf = mb[:].rearrange("p c e -> p (c e)")
                    for k in (1, 2, 3):
                        t.matmul(o[:, 8 * k:8 * NC], ones[:], mf[:, 0:8 * (NC - k)], start=False, stop=False,
                                 skip_group_check=True)
                    t.matmul(o, before[:], mf, start=False, stop=True).then_inc(pe_pos, 1)
                shared_pair(6)
                if isinstance(b, int) and b == B + 1:
                    for f in TILES_B1:
                        shared_pair(f, EARLY - 1)
                shared_pair(7)
                if isinstance(b, int) and b >= B:
                    for f in (TILES_B, TILES_END)[b - B]:
                        shared_pair(f, EARLY - 1)
                    if b == B + 1:
                        shared_down(range(NC), EARLY - 1)

            def three_r(dst, tok):
                t.matmul(dst, xhi[:, 0, tok], wvg_hi, start=True, stop=False)
                t.matmul(dst, xhi[:, 0, tok], wvg_lo, start=False, stop=False)
                return t.matmul(dst, xlo[:, 0, tok], wvg_hi, start=False, stop=True)

            def v_rows(par, c, half, tok):
                v = VP[tok, par, c]
                return bass.AP(tensor=v.tensor, offset=v.offset + 256 * half, ap=[list(v.ap[0]), [128, 2], [40, 4], [1, 8]])
            stage1(pe, step)

            def turn_late(n):
                need(pe, m_x1, 16 * n)
                for c in range(NC):
                    ins = t.transpose(PB[1][:, P * c:P * (c + 1)], x1t[:, c], ident[:])
                ins.then_inc(m_x1T, 1)

            def step(e, par):
                def turn_rows(k, kp, groups):
                    need(pe, e_ldx, 16 * (k + 1))
                    for i in groups:
                        t0, n = GROUPS[i]
                        bank = (3 * kp + i) % 2
                        need(pe, e_lo, 3 * k + i - 1)
                        for c in range(n):
                            ins = t.transpose(PB[bank][:, P * c:P * (c + 1)], xg[:, kp, t0 + c, 0:D], ident[:])
                        ins.then_inc(e_xT, 1)

                def gate_up(n):
                    cols = slice(P * GROUPS[n][0], P * (GROUPS[n][0] + GROUPS[n][1]))
                    w = P * GROUPS[n][1]
                    need(pe, e_lo, 3 * e + n + 1)
                    need(pe, e_hi, 3 * e + n + 1)
                    need(pe, e_w, 4 * e + 4)
                    for f in range(4):
                        need(pe, e_h, 12 * e + 4 * n + f - 1)
                        ff = slice(P * f, P * (f + 1))
                        for gu in (0, 1):
                            three(EB[2 * gu + f % 2][:, 0:w], we_hi[:, par, gu, ff], we_lo[:, par, gu, ff],
                                  xgT_hi[:, par, cols], xgT_lo[:, par, cols]).then_inc((e_gt, e_gu)[gu], 1)

                def down(n):
                    hp = (n + par) % 2
                    need(pe, e_h, 12 * e + 4 * n + 4)
                    need(pe, e_y, 3 * e + n - 1)
                    for c in range(GROUPS[n][1]):
                        for f in range(4):
                            ins = t.matmul((OB, SBK)[hp][:, P * c:P * (c + 1)], he[:, hp, f, P * c:P * (c + 1)],
                                           wd[:, par, f], start=(f == 0), stop=(f == 3))
                    ins.then_inc(e_dn, 1)
                if isinstance(e, int) and e == 0:
                    turn_rows(0, 0, (0, 1, 2))
                gate_up(0)
                if within(e, 0, E - 2):
                    turn_rows(e + 1, 1 - par, (0, 1))
                gate_up(1)
                if within(e, 0, E - 2):
                    turn_rows(e + 1, 1 - par, (2,))
                down(0)
                gate_up(2)
                if isinstance(e, int) and e == E - 1:
                    turn_late(1)
                down(1)
                down(2)
            stage2(pe, step)

            pe.wait_ge(e_h, 12 * E)

            def group(g):
                r = EARLY + g

                if not within(g, 0, 4):
                    return
                need(pe, a_x1h, r + 1)
                need(pe, v_x1l, r + 1)
                for f in range(8):
                    n = 8 * r + f
                    ff = slice(P * f, P * (f + 1))
                    need(pe, a_sf, n - 1)
                    three((GB[:], EB2[:, 0])[f % 2], ws_hi[:, 0, ff], ws_lo[:, 0, ff], xhi[:, 1], xlo[:, 1]).then_inc(pe_gt, 1)
                    need(pe, v_h, n - 1)
                    if f == 0:
                        need(pe, v_xs, r)
                    three((UB[:], EB2[:, 1])[f % 2], ws_hi[:, 1, ff], ws_lo[:, 1, ff], xhi[:, 1], xlo[:, 1]).then_inc(pe_up, 1)
                if within(g, 0, 3):
                    turn_late(g + 2)
                need(pe, v_h, 8 * r + 7)
                for c in range(NC):
                    for f in range(8):
                        if c == 0 and f == 7:
                            need(pe, v_h, 8 * (r + 1))
                        ins = t.matmul(UB[:, P * c:P * (c + 1)], hs[:, f, P * c:P * (c + 1)], sd_s[:, f],
                                       start=(f == 0), stop=(f == 7))
                ins.then_inc(pe_dn, 1)
            stage3(pe, group)


def kernel(**inputs):
    import numpy as _np
    import concourse.bacc as _bacc
    from concourse import mybir as _mybir
    from concourse.bass_utils import run_bass_kernel_spmd as _run

    d = {k.split("_", 2)[2]: _np.ascontiguousarray(_np.asarray(v)) for k, v in inputs.items() if k != "L0_attn_x"}
    x = _np.ascontiguousarray(_np.asarray(inputs["L0_attn_x"]))
    def doubled(w):
        w = w.reshape(D, 2, H // 2, 1, HD)
        return _np.broadcast_to(w, (D, 2, H // 2, 2, HD)).reshape(D, 2 * P)
    theta = _np.broadcast_to(d["theta"].reshape(2, H // 2, 1, HD), (2, H // 2, 2, HD)).reshape(2, P).T
    arrays = {
        "x": x, "wqk": _np.concatenate([doubled(d["Wq"]), doubled(d["Wk"])], axis=1), "wv": d["Wv"],
        "g1t": d["G1"].T, "g2": d["G2"], "wo": d["Wo"], "gamma": d["gamma"], "beta": d["beta"], "theta": theta,
        "rwt": d["router_w"].T, "rg": d["rg"], "ru": d["ru"], "rd": d["rd"], "sg": d["sg"], "su": d["su"], "sd": d["sd"],
    }
    arrays = {f"in_{k}": _np.ascontiguousarray(v) for k, v in arrays.items()}
    nc = _bacc.Bacc("TRN2", target_bir_lowering=False, num_devices=1)
    args = [nc.dram_tensor(k, v.shape, _mybir.dt.from_np(v.dtype), kind="ExternalInput").ap() for k, v in arrays.items()]
    args.append(nc.dram_tensor("out_x", (B, S, D), _mybir.dt.float32, kind="ExternalOutput").ap())
    build(nc, *args)
    r = _run(nc, [arrays], core_ids=[0])
    return r.results[0]["out_x"]
```
